# Optimizing a Trainium2 kernel written in Bass

```python
import numpy as np
import jax
import jax.numpy as jnp

def _softmax(x, axis=-1):
    return jax.nn.softmax(x, axis=axis)

def _gelu(x):
    return jax.nn.gelu(x, approximate=True)

def _silu(x):
    return jax.nn.silu(x)

def _sigmoid(x):
    return jax.nn.sigmoid(x)

def _layernorm(x, axis=-1, eps=1e-05):
    m = jnp.mean(x, axis=axis, keepdims=True)
    v = jnp.var(x, axis=axis, keepdims=True)
    return (x - m) / jnp.sqrt(v + eps)

def _scatter_add(tgt, idx, src, axis=0):
    return tgt.at[idx].add(src)

def _segment_sum(src, seg, n):
    return jax.ops.segment_sum(src, seg, n)
kernel_name = 'mk_adj_preln_d4_adj_r2_c76ee7'

def setup_inputs(seed: int=0):
    np.random.seed(seed)
    _w = jnp.asarray

    def _rec_inputs():
        import jax
        import jax.numpy as jnp
        _gk = jax.random.key(seed)
        x = -0.0002928 + 1 * jax.random.normal(jax.random.fold_in(_gk, 1), (2048, 512), jnp.float32)
        _w = (1.0 + jnp.arange(2048, dtype=jnp.float32)) ** (-0.5)
        _w = _w / _w.mean()
        _pij = jnp.clip(0.00195312 * _w[:, None] * _w[None, :], 0.0, 1.0)
        _a = jax.random.uniform(jax.random.fold_in(_gk, 2), (2048, 2048)) < _pij
        _af = _a.astype(jnp.float32)
        adj = _af
        return (x, adj)
    x, adj = _rec_inputs()

    def _L0_gnn_setup():
        import jax, jax.numpy as jnp
        import numpy as np
        N = 2048
        D_IN = 512
        H = 16
        DH = D_IN // H
        ALPHA = 0.2
        MASK_VAL = -65500.0
        key = jax.random.key(seed)
        ks = jax.random.split(key, 7)
        x = jax.random.normal(ks[0], (N, D_IN), dtype=jnp.float32)
        adj = jax.random.randint(ks[1], (N, N), 0, 2).astype(jnp.float32)
        s = 1.0 / np.sqrt(D_IN)
        W_seq = jax.random.normal(ks[2], (D_IN, D_IN), dtype=jnp.float32) * s
        a1 = jax.random.normal(ks[3], (DH,), dtype=jnp.float32) / np.sqrt(DH)
        a2 = jax.random.normal(ks[4], (DH,), dtype=jnp.float32) / np.sqrt(DH)
        W_out = jax.random.normal(ks[5], (D_IN, D_IN), dtype=jnp.float32) * s
        b_out = jax.random.normal(ks[6], (D_IN,), dtype=jnp.float32) * 0.01
        return {'x': x, 'adj': adj, 'W_seq': W_seq, 'a1': a1, 'a2': a2, 'W_out': W_out, 'b_out': b_out}
    _L0_gnn_all = _L0_gnn_setup()
    _L0_gnn_in = {k: v for k, v in _L0_gnn_all.items() if k in ('W_seq', 'a1', 'a2', 'W_out', 'b_out')}
    del _L0_gnn_all

    def _L1_gnn_setup():
        import jax, jax.numpy as jnp
        import numpy as np
        N = 4096
        D_IN = 512
        D_OUT = 512
        key = jax.random.key(seed)
        k1, k2, k3, k4 = jax.random.split(key, 4)
        features = jax.random.normal(k1, (N, D_IN), dtype=jnp.float32)
        adj = jax.random.uniform(k2, (N, N), dtype=jnp.float32)
        W = jax.random.normal(k3, (D_OUT, D_IN), dtype=jnp.float32) * (1.0 / np.sqrt(D_IN))
        b = jax.random.normal(k4, (D_OUT,), dtype=jnp.float32) * 0.01
        return {'features': features, 'adj': adj, 'W': W, 'b': b}
    _L1_gnn_all = _L1_gnn_setup()
    _L1_gnn_in = {k: v for k, v in _L1_gnn_all.items() if k in ('W', 'b')}
    del _L1_gnn_all

    def _L2_gnn_setup():
        import jax, jax.numpy as jnp
        import numpy as np
        N = 4096
        D = 512

        def adjacent_mat(adj):
            adj = adj + jnp.eye(adj.shape[0], dtype=adj.dtype)
            deg = jnp.sum(adj, axis=1)
            dinv = jnp.where(deg > 0, deg ** (-0.5), 0.0).astype(adj.dtype)
            return dinv[:, None] * adj * dinv[None, :]
        key = jax.random.key(seed)
        k1, k2 = jax.random.split(key)
        x = jax.random.normal(k1, (N, D), dtype=jnp.float32)
        Coefficient2 = 1e-08 * jnp.ones((N, N), dtype=jnp.float32)
        A = jax.random.uniform(k2, (N, N), dtype=jnp.float32)
        return {'x': x, 'Coefficient2': Coefficient2, 'A': A}
    _L2_gnn_all = _L2_gnn_setup()
    _L2_gnn_in = {k: v for k, v in _L2_gnn_all.items() if k in ()}
    del _L2_gnn_all

    def _L3_gnn_setup():
        import jax, jax.numpy as jnp
        import numpy as np
        ALPHA = 0.2
        NEG = -9000000000000000.0
        N, NFEAT, NHID, NHEADS = (2048, 512, 64, 8)
        EMB = NHID * NHEADS
        key = jax.random.key(seed)
        ks = jax.random.split(key, 16)
        x = jax.random.normal(ks[0], (N, NFEAT), dtype=jnp.float32)
        adj = (jax.random.uniform(ks[1], (N, N)) < 0.01).astype(jnp.float32)
        adj = jnp.maximum(adj, jnp.eye(N, dtype=jnp.float32))
        s = 0.05
        W = jax.random.normal(ks[2], (NHEADS, NFEAT, NHID), dtype=jnp.float32) * s
        a1 = jax.random.normal(ks[3], (NHEADS, NHID), dtype=jnp.float32) * s
        a2 = jax.random.normal(ks[4], (NHEADS, NHID), dtype=jnp.float32) * s
        W1 = jax.random.normal(ks[5], (EMB // 2, EMB), dtype=jnp.float32) * s
        b1 = jnp.zeros((EMB // 2,), dtype=jnp.float32)
        W2 = jax.random.normal(ks[6], (NFEAT // 4, EMB // 2), dtype=jnp.float32) * s
        b2 = jnp.zeros((NFEAT // 4,), dtype=jnp.float32)
        W3 = jax.random.normal(ks[7], (NFEAT // 2, NFEAT // 4), dtype=jnp.float32) * s
        b3 = jnp.zeros((NFEAT // 2,), dtype=jnp.float32)
        W4 = jax.random.normal(ks[8], (NFEAT, NFEAT // 2), dtype=jnp.float32) * s
        b4 = jnp.zeros((NFEAT,), dtype=jnp.float32)
        return {'x': x, 'adj': adj, 'W': W, 'a1': a1, 'a2': a2, 'W1': W1, 'b1': b1, 'W2': W2, 'b2': b2, 'W3': W3, 'b3': b3, 'W4': W4, 'b4': b4}
    _L3_gnn_all = _L3_gnn_setup()
    _L3_gnn_in = {k: v for k, v in _L3_gnn_all.items() if k in ('W', 'a1', 'a2', 'W1', 'b1', 'W2', 'b2', 'W3', 'b3', 'W4', 'b4')}
    del _L3_gnn_all
    return {'x': x, 'adj': adj, 'L0_gnn_W_seq': _L0_gnn_in['W_seq'], 'L0_gnn_a1': _L0_gnn_in['a1'], 'L0_gnn_a2': _L0_gnn_in['a2'], 'L0_gnn_W_out': _L0_gnn_in['W_out'], 'L0_gnn_b_out': _L0_gnn_in['b_out'], 'L1_gnn_W': _L1_gnn_in['W'], 'L1_gnn_b': _L1_gnn_in['b'], 'L3_gnn_W': _L3_gnn_in['W'], 'L3_gnn_a1': _L3_gnn_in['a1'], 'L3_gnn_a2': _L3_gnn_in['a2'], 'L3_gnn_W1': _L3_gnn_in['W1'], 'L3_gnn_b1': _L3_gnn_in['b1'], 'L3_gnn_W2': _L3_gnn_in['W2'], 'L3_gnn_b2': _L3_gnn_in['b2'], 'L3_gnn_W3': _L3_gnn_in['W3'], 'L3_gnn_b3': _L3_gnn_in['b3'], 'L3_gnn_W4': _L3_gnn_in['W4'], 'L3_gnn_b4': _L3_gnn_in['b4']}

def reference(x, adj, L0_gnn_W_seq, L0_gnn_a1, L0_gnn_a2, L0_gnn_W_out, L0_gnn_b_out, L1_gnn_W, L1_gnn_b, L3_gnn_W, L3_gnn_a1, L3_gnn_a2, L3_gnn_W1, L3_gnn_b1, L3_gnn_W2, L3_gnn_b2, L3_gnn_W3, L3_gnn_b3, L3_gnn_W4, L3_gnn_b4):
    import jax
    import jax.numpy as jnp

    def _L0_gnn_ref(x, adj, W_seq, a1, a2, W_out, b_out):
        import jax, jax.numpy as jnp
        import numpy as np
        N = 2048
        D_IN = 512
        H = 16
        DH = D_IN // H
        ALPHA = 0.2
        MASK_VAL = -65500.0
        seq = (x @ W_seq).reshape(N, H, DH)
        score1 = jnp.einsum('nhd,d->hn', seq, a1)
        score2 = jnp.einsum('nhd,d->hn', seq, a2)
        scores = score1[:, :, None] + score2[:, None, :]
        scores = jax.nn.leaky_relu(scores, negative_slope=ALPHA)
        scores = scores + (1.0 - adj)[None, :, :] * MASK_VAL
        attn = jax.nn.softmax(scores, axis=-1)
        hidden = jnp.einsum('hij,jhd->ihd', attn, seq).reshape(N, D_IN)
        hidden = hidden @ W_out + b_out
        return jax.nn.elu(hidden)

    def _L1_gnn_ref(features, adj, W, b):
        import jax, jax.numpy as jnp
        import numpy as np
        N = 4096
        D_IN = 512
        D_OUT = 512
        agg = adj @ features
        out = jnp.einsum('nd,od->no', agg, W) + b
        return jax.nn.relu(out)

    def _L2_gnn_ref(x, Coefficient2, A):
        import jax, jax.numpy as jnp
        import numpy as np
        N = 4096
        D = 512

        def adjacent_mat(adj):
            adj = adj + jnp.eye(adj.shape[0], dtype=adj.dtype)
            deg = jnp.sum(adj, axis=1)
            dinv = jnp.where(deg > 0, deg ** (-0.5), 0.0).astype(adj.dtype)
            return dinv[:, None] * adj * dinv[None, :]
        A_c = jax.lax.stop_gradient(A)
        adj = adjacent_mat((A_c + A_c.T) * 0.5)
        y = Coefficient2 @ adj
        y = y @ x
        return y

    def _L3_gnn_ref(x, adj, W, a1, a2, W1, b1, W2, b2, W3, b3, W4, b4):
        import jax, jax.numpy as jnp
        import numpy as np
        ALPHA = 0.2
        NEG = -9000000000000000.0
        N, NFEAT, NHID, NHEADS = (2048, 512, 64, 8)
        EMB = NHID * NHEADS
        Wh = jnp.einsum('nf,hfd->hnd', x, W)
        e_src = jnp.einsum('hnd,hd->hn', Wh, a1)
        e_dst = jnp.einsum('hnd,hd->hn', Wh, a2)
        e = jax.nn.leaky_relu(e_src[:, :, None] + e_dst[:, None, :], ALPHA)
        e = jnp.where(adj[None] > 0, e, NEG)
        att = jax.nn.softmax(e, axis=-1)
        h = jnp.einsum('hnm,hmd->hnd', att, Wh)
        h = jax.nn.elu(h)
        enc = jnp.transpose(h, (1, 0, 2)).reshape(x.shape[0], -1)
        out = jax.nn.relu(enc @ W1.T + b1)
        out = jax.nn.relu(out @ W2.T + b2)
        out = jax.nn.relu(out @ W3.T + b3)
        out = out @ W4.T + b4
        return out
    h = jnp.maximum(_layernorm(x, axis=-1), 0.0)
    x = x + _L0_gnn_ref(h, adj, L0_gnn_W_seq, L0_gnn_a1, L0_gnn_a2, L0_gnn_W_out, L0_gnn_b_out)
    h = jnp.maximum(_layernorm(x, axis=-1), 0.0)
    x = x + _L1_gnn_ref(h, adj, L1_gnn_W, L1_gnn_b)
    h = jnp.maximum(_layernorm(x, axis=-1), 0.0)
    x = x + _L2_gnn_ref(h, adj, adj)
    h = jnp.maximum(_layernorm(x, axis=-1), 0.0)
    x = x + _L3_gnn_ref(h, adj, L3_gnn_W, L3_gnn_a1, L3_gnn_a2, L3_gnn_W1, L3_gnn_b1, L3_gnn_W2, L3_gnn_b2, L3_gnn_W3, L3_gnn_b3, L3_gnn_W4, L3_gnn_b4)
    return x

_drawn_inputs = setup_inputs


def setup_inputs(seed=0):
    import zlib

    import numpy as np

    out = dict(_drawn_inputs(seed))
    spreads = {'L3_gnn_b1': (0.0, 0.8),
     'L3_gnn_b2': (0.0, 2.0),
     'L3_gnn_b3': (0.0, 2.0),
     'L3_gnn_b4': (0.0, 2.0)}
    factors = {'L0_gnn_a1': 6.387,
     'L0_gnn_b_out': 5.854,
     'L1_gnn_b': 8.0,
     'L3_gnn_W': 5.119,
     'L3_gnn_a1': 8.0,
     'L3_gnn_a2': 8.0,
     'L3_gnn_W1': 4.952,
     'L3_gnn_W2': 4.407,
     'L3_gnn_W3': 3.484}
    for name, (base, spread) in spreads.items():
        noise = np.random.default_rng([zlib.crc32(name.encode()), seed]).standard_normal(out[name].shape)
        drawn = base * np.exp(spread * noise) if base else spread * noise
        out[name] = jnp.asarray(drawn.astype(out[name].dtype))
    for name, factor in factors.items():
        out[name] = (out[name] * factor).astype(out[name].dtype)
    return out
```

```python
from contextlib import ExitStack

import concourse.bass as bass
from concourse import mybir

F32 = mybir.dt.float32
BF16 = mybir.dt.bfloat16
F16 = mybir.dt.float16
ALU = mybir.AluOpType
ACT = mybir.ActivationFunctionType
AX_X = mybir.AxisListType.X

P = 128
N = 2048
T = N // P
D = 512
KT = D // P
EPS = 1e-5
SLOPE = 0.2
LO_SCALE = float(2**11)
STEP_SCALE = float(2**60)
JB = 4
NB = T // JB
RING = 4


def later(t, than=1):
    return not isinstance(t, int) or t > than


def col(x, t):
    return x[:, bass.ds(t, 1)]


def staged_tiles(eng, *stages):
    lags = [lag for lag, _ in stages]
    head = (max(lags) + 3) // 2 * 2
    tail = T + min(lags) - min(lags) % 2

    def step(base, q, checked):
        for lag, emit in stages:
            par = (q - lag) % 2
            pair = base + (q - lag - par) // 2
            if not checked or 0 <= 2 * pair + par < T:
                emit(2 * pair + par, pair, par)

    for s in range(head):
        step(s // 2, s % 2, True)
    with eng.Fori(head // 2, tail // 2) as i:
        for q in range(2):
            step(i, q, False)
    for s in range(tail, T + max(lags)):
        step(s // 2, s % 2, True)


class Mem:

    def __init__(self, nc, stack, prefix):
        self.nc, self.stack, self.prefix = nc, stack, prefix

    def sb(self, name, shape, dt=F32):
        return self.stack.enter_context(self.nc.sbuf_tensor(f"{self.prefix}_{name}", shape, dt))

    def ps(self, name, shape, dt=F32):
        return self.stack.enter_context(self.nc.psum_tensor(f"{self.prefix}_{name}", shape, dt))

    def sem(self, name):
        return self.stack.enter_context(self.nc.semaphore(f"{self.prefix}_{name}"))


class LayerNorm:

    def __init__(self, nc, m, consts, row_factor=None):
        self.nc, self.consts, self.row_factor = nc, consts, row_factor
        self.stats = [m.sb(f"ln_stats{p}", [P, 6]) for p in range(2)]
        self.mean_var = [m.sb(f"ln_mean_var{p}", [P, 2]) for p in range(2)]
        self.var_eps = [m.sb(f"ln_var_eps{p}", [P, 1]) for p in range(2)]
        self.neg_mean = [m.sb(f"ln_neg_mean{p}", [P, 1]) for p in range(2)]
        self.rstd = [m.sb(f"ln_rstd{p}", [P, 1]) for p in range(2)]
        self.scale = [m.sb(f"ln_scale{p}", [P, 1]) for p in range(2)]
        self.shift = [m.sb(f"ln_shift{p}", [P, 1]) for p in range(2)]
        self.stats_done = m.sem("ln_stats_done")
        self.moments_done = m.sem("ln_moments_done")
        self.moments_ready = m.sem("ln_moments_ready")
        self.rstd_done = m.sem("ln_rstd_done")
        self.scale_done = m.sem("ln_scale_done")
        self.coefs_ready = m.sem("ln_coefs_ready")

    def vector(self, dve, x, t, par):
        nc = self.nc
        nc.vector.bn_stats(self.stats[par][:], x).then_inc(self.stats_done, 1)
        dve.wait_ge(self.stats_done, t + 1)
        self.consts["settle"](dve)
        nc.vector.bn_aggr(self.mean_var[par][:], self.stats[par][:]).then_inc(self.moments_done, 1)
        dve.wait_ge(self.moments_done, t + 1)
        nc.vector.tensor_scalar(self.var_eps[par][:], self.mean_var[par][:, 1:2], EPS, None, ALU.add)
        nc.vector.tensor_scalar(self.neg_mean[par][:], self.mean_var[par][:, 0:1], -1.0, None,
                                ALU.mult).then_inc(self.moments_ready, 1)

    def pool(self, pool, t, par):
        nc = self.nc
        pool.wait_ge(self.moments_ready, t + 1)
        nc.gpsimd.tensor_tensor(self.rstd[par][:], self.var_eps[par][:], self.consts["neg_half"][:, 0:1],
                                ALU.pow).then_inc(self.rstd_done, 1)
        pool.wait_ge(self.rstd_done, t + 1)
        last = self.rstd[par]
        if self.row_factor is not None:
            nc.gpsimd.tensor_tensor(self.scale[par][:], self.rstd[par][:], col(self.row_factor, t),
                                    ALU.mult).then_inc(self.scale_done, 1)
            pool.wait_ge(self.scale_done, t + 1)
            last = self.scale[par]
        nc.gpsimd.tensor_tensor(self.shift[par][:], self.neg_mean[par][:], last[:],
                                ALU.mult).then_inc(self.coefs_ready, 1)

    def scalar(self, act, out, x, t, par):
        act.wait_ge(self.coefs_ready, t + 1)
        scale = self.rstd if self.row_factor is None else self.scale
        return self.nc.scalar.activation(out, x, ACT.Relu, bias=self.shift[par][:], scale=scale[par][:])


def load_tiles(sp, src, dst, loaded, used, used_lead=2):
    def load(t, pair, par):
        sp.dma_start(dst[par][:], src[t]).then_inc(loaded[par], 16)

    for par in range(2):
        load(par, 0, par)
    with sp.Fori(1, T // 2) as pair:
        for par in range(2):
            sp.wait_ge(used, 2 * pair + par - 1)
            load(2 * pair + par, pair, par)


def rows(x):
    return x.rearrange("(t p) d -> t p d", p=P)


def build_constants(nc, consts):
    with ExitStack() as stack:
        m = Mem(nc, stack, "const")
        filled = m.sem("filled")
        with nc.Block() as block:

            @block.gpsimd
            def _(pool):
                nc.gpsimd.memset(consts["neg_half"][:], -0.5)
                nc.gpsimd.memset(consts["ones_bf16"][:], 1.0)
                nc.gpsimd.memset(consts["ident"][:], 0.0).then_inc(filled, 1)
                pool.wait_ge(filled, 1)
                nc.gpsimd.affine_select(out=consts["ident"][:], in_=consts["ident"][:],
                                        compare_op=ALU.not_equal, fill=1.0, base=0, pattern=[[-1, P]],
                                        channel_multiplier=1)


def build_projection(nc, name, consts, x_src, w_dram, a12_dram, heads, keep, s1_dram, spare):
    dh = D // heads
    with ExitStack() as stack:
        m = Mem(nc, stack, name)
        w = m.sb("w", [P, KT, D])
        a12 = m.sb("a12", [P, 2, D])
        wa_terms = spare[:, 0:KT * D].rearrange("p (k n) -> p k n", k=KT)
        wa = m.sb("wa", [P, KT, 2 * heads])
        x = [m.sb(f"x{p}", [P, D]) for p in range(2)]
        h = [m.sb(f"h{p}", [P, D]) for p in range(2)]
        ht = [m.sb(f"ht{p}", [P, KT, P]) for p in range(2)]
        s12 = m.sb("s12", [P, T, 2 * heads])
        clipped = m.sb("clipped", [P, T, 2, heads])
        s1_rows = spare[0:heads, KT * D:KT * D + N]
        ps_t = [m.ps(f"ps_t{p}", [P, KT, P]) for p in range(2)]
        ps_v = [m.ps(f"ps_v{p}", [P, D]) for p in range(2)]
        ps_s = [m.ps(f"ps_s{p}", [P, 512]) for p in range(2)]
        ps_r = [m.ps(f"ps_r{p}", [P, 512]) for p in range(2)]
        ln = LayerNorm(nc, m, consts)
        w_loaded = m.sem("w_loaded")
        x_loaded = [m.sem(f"x_loaded{p}") for p in range(2)]
        h_ready = m.sem("h_ready")
        h_transposed = m.sem("h_transposed")
        ht_ready = m.sem("ht_ready")
        wa_step = m.sem("wa_step")
        wa_ready = m.sem("wa_ready")
        ones_set = m.sem("ones_set")
        projected = m.sem("projected")
        values_out = m.sem("values_out")
        rows_out = m.sem("rows_out")
        clip_ready = m.sem("clip_ready")
        s1_stored = m.sem("s1_stored")
        values, exp_s2, step_bias, row_exps = keep["values"], keep["exp_s2"], keep["step_bias"], keep["row_exps"]
        with nc.Block() as block:

            @block.sync
            def _(sp):
                sp.dma_start(w[:], w_dram.rearrange("(k p) n -> p k n", p=P)).then_inc(w_loaded, 16)
                sp.dma_start(a12[:], a12_dram.unsqueeze(0).broadcast_to([P, 2, D])).then_inc(w_loaded, 16)
                load_tiles(sp, rows(x_src), x, x_loaded, h_ready)
                sp.wait_ge(rows_out, T)
                sp.dma_start(s1_dram, s1_rows).then_inc(s1_stored, 16)
                sp.wait_ge(s1_stored, 16)

            @block.gpsimd
            def _(pool):
                nc.gpsimd.memset(values[:, :, :, dh:dh + 1], 1.0).then_inc(ones_set, 1)
                staged_tiles(pool, (0, lambda t, pair, par: ln.pool(pool, t, par)))

            @block.scalar
            def _(act):
                def normed(t, pair, par):
                    if later(t):
                        act.wait_ge(h_transposed, t - 1)
                    ln.scalar(act, h[par][:], x[par][:], t, par).then_inc(h_ready, 1)

                def transposed_out(t, pair, par):
                    act.wait_ge(h_transposed, t + 1)
                    nc.scalar.copy(ht[par][:], ps_t[par][:]).then_inc(ht_ready, 1)

                def rows_copy(t, pair, par):
                    act.wait_ge(projected, t + 1)
                    nc.scalar.copy(s1_rows[:, bass.ts(t, P)], ps_r[par][0:heads, 0:P]).then_inc(rows_out, 1)

                staged_tiles(act, (0, normed), (1, transposed_out), (2, rows_copy))
                act.wait_ge(values_out, T + 2)
                nc.scalar.activation(exp_s2[:, :, :, 0], s12[:, :, heads:], ACT.Exp)
                nc.scalar.activation(exp_s2[:, :, :, 1], s12[:, :, heads:], ACT.Exp, scale=SLOPE)
                nc.scalar.mul(step_bias[:], s12[:, :, heads:], STEP_SCALE)
                act.wait_ge(clip_ready, 1)
                nc.scalar.activation(row_exps[:, :, 0, :], clipped[:, :, 0, :], ACT.Exp, scale=1.0 - SLOPE)
                nc.scalar.activation(row_exps[:, :, 1, :], clipped[:, :, 1, :], ACT.Exp, scale=SLOPE - 1.0)

            @block.vector
            def _(dve):
                def stats(t, pair, par):
                    dve.wait_ge(x_loaded[par], 16 * (pair + 1))
                    ln.vector(dve, x[par][:], t, par)

                def out(t, pair, par):
                    dve.wait_ge(projected, t + 1)
                    nc.vector.tensor_copy(values[:, t, :, 0:dh],
                                          ps_v[par][:].rearrange("p (h d) -> p h d", h=heads))
                    nc.vector.tensor_copy(s12[:, t, :], ps_s[par][:, 0:2 * heads]).then_inc(values_out, 1)

                dve.wait_ge(w_loaded, 32)
                for s in range(2):
                    if s:
                        dve.wait_ge(wa_ready, s)
                    nc.vector.tensor_tensor(wa_terms, w[:], a12[:, s:s + 1, :].broadcast_to([P, KT, D]),
                                            ALU.mult).then_inc(wa_step, 1)
                    dve.wait_ge(wa_step, s + 1)
                    nc.vector.tensor_reduce(wa[:, :, s * heads:(s + 1) * heads],
                                            wa_terms.rearrange("p k (h d) -> p k h d", h=heads),
                                            AX_X, ALU.add).then_inc(wa_ready, 1)
                dve.sem_inc(values_out, 2)
                staged_tiles(dve, (0, stats), (2, out))
                dve.wait_ge(values_out, T + 2)
                nc.vector.tensor_scalar(clipped[:, :, 0, :], s12[:, :, 0:heads], 0.0, None, ALU.min)
                nc.vector.tensor_scalar(clipped[:, :, 1, :], s12[:, :, 0:heads], 0.0, None,
                                        ALU.max).then_inc(clip_ready, 1)

            @block.tensor
            def _(pe):
                def turn(t, pair, par):
                    pe.wait_ge(h_ready, t + 1)
                    for k in range(KT):
                        mm = nc.tensor.transpose(ps_t[par][:, k, :], h[par][:, k * P:(k + 1) * P],
                                                 consts["ident"][:])
                    mm.then_inc(h_transposed, 1)

                def project(t, pair, par):
                    pe.wait_ge(ht_ready, t + 1)
                    pe.wait_ge(values_out, t + 1)
                    if later(t):
                        pe.wait_ge(rows_out, t - 1)
                    for k in range(KT):
                        nc.tensor.matmul(ps_v[par][:], ht[par][:, k, :], w[:, k, :],
                                         start=(k == 0), stop=(k == KT - 1))
                    for k in range(KT):
                        nc.tensor.matmul(ps_s[par][:, 0:2 * heads], ht[par][:, k, :], wa[:, k, :],
                                         start=(k == 0), stop=(k == KT - 1))
                    for k in range(KT):
                        mm = nc.tensor.matmul(ps_r[par][0:heads, 0:P], wa[:, k, 0:heads], ht[par][:, k, :],
                                              start=(k == 0), stop=(k == KT - 1))
                    mm.then_inc(projected, 1)

                pe.wait_ge(w_loaded, 32)
                pe.wait_ge(wa_ready, 2)
                staged_tiles(pe, (0, turn), (1, project))


def build_lonely_rows(nc, consts, adj_t, adj_loaded, lonely):
    CH = 512
    with ExitStack() as stack:
        m = Mem(nc, stack, "lonely")
        ps_deg = m.ps("ps_deg", [P, N // CH, CH])
        counted = m.sem("counted")
        flagged = m.sem("flagged")
        with nc.Block() as block:

            @block.tensor
            def _(pe):
                pe.wait_ge(adj_loaded, 16 * NB)
                for c in range(N // CH):
                    for j in range(T):
                        mm = nc.tensor.matmul(ps_deg[:, c, :], consts["ones_bf16"][:],
                                              adj_t[:, j, c * CH:(c + 1) * CH],
                                              start=(j == 0), stop=(j == T - 1))
                    mm.then_inc(counted, 1)

            @block.vector
            def _(dve):
                for c in range(N // CH):
                    cols = slice(c * CH, (c + 1) * CH)
                    dve.wait_ge(counted, c + 1)
                    nc.vector.tensor_scalar(lonely[:, cols], ps_deg[:, c, :], 0.0, None,
                                            ALU.is_equal).then_inc(flagged, 1)
                    dve.wait_ge(flagged, c + 1)
                    nc.vector.tensor_tensor(adj_t[:, :, cols], adj_t[:, :, cols],
                                            lonely[:, cols].unsqueeze(1).broadcast_to([P, T, CH]), ALU.add)


def build_attention(nc, name, settle, heads, keep, adj_t, s1_dram, ring, hidden, mean_rows=None):
    dh = D // heads
    c1 = dh + 1
    region = 256 if 6 * c1 <= 256 else 512
    IT = 2048 // region
    CW = IT * P
    NCH = N // CW
    NEVAC = 6 if mean_rows is None else 8
    with ExitStack() as stack:
        m = Mem(nc, stack, name)
        left = [ring[:, RING * JB * CW:].bitcast(F32) if RING * JB * CW < ring.shape[1] else None]

        def small(name, shape):
            size = 1
            for n in shape[1:]:
                size *= n
            if left[0] is None or size > left[0].shape[1]:
                return m.sb(name, shape)[:]
            at, left[0] = left[0][:, 0:size], left[0][:, size:]
            return at if len(shape) == 2 else at.rearrange(
                "p (i c) -> p i c" if len(shape) == 3 else "p (i s c) -> p i s c",
                **dict(zip("isc" if len(shape) == 4 else "ic", shape[1:])))

        s1_wide = [small(f"s1_wide{p}", [P, CW]) for p in range(2)]
        mask = [ring[:, r * JB * CW:(r + 1) * JB * CW].rearrange("p (q c) -> p q c", q=JB) for r in range(RING)]
        parts = [m.sb(f"parts{p}", [P, T, 9 * c1], BF16) for p in range(2)]
        JV = 4
        weighted = small("weighted", [P, JV, 2, c1])
        rest = small("rest", [P, JV, 2, c1])
        sum_a = small("sum_a", [P, IT, c1])
        sum_b = small("sum_b", [P, IT, c1])
        num_den = small("num_den", [P, IT, c1])
        recip = m.sb("recip", [P, IT, 1])
        ps = [m.ps(f"ps_sums{p}", [P, IT, region]) for p in range(2)]
        s1_loaded = [m.sem(f"s1_loaded{p}") for p in range(2)]
        steps_ready = m.sem("steps_ready")
        masks_ready = m.sem("masks_ready")
        masks_used = m.sem("masks_used")
        parts_step = m.sem("parts_step")
        parts_ready = m.sem("parts_ready")
        psum_free = m.sem("psum_free")
        evac_step = m.sem("evac_step")
        values, exp_s2, step_bias, row_exps = keep["values"], keep["exp_s2"], keep["step_bias"], keep["row_exps"]
        HC = 2 * NCH

        def head_pairs(eng, body):
            body(0, True)
            with eng.Fori(1, heads // 2) as pair:
                body(pair, False)

        with nc.Block() as block:

            @block.sync
            def _(sp):
                def body(pair, first):
                    for k in range(HC):
                        g = pair * HC + k
                        head, c = 2 * pair + k // NCH, k % NCH
                        if not first or k >= 2:
                            sp.wait_ge(steps_ready, NB * (g - 1))
                        sp.dma_start(s1_wide[k % 2][:],
                                     s1_dram[bass.ds(head, 1), c * CW:(c + 1) * CW].broadcast_to([P, CW])
                                     ).then_inc(s1_loaded[k % 2], 16)
                head_pairs(sp, body)

            @block.gpsimd
            def _(pool):
                NP = 5 * (T // JV)

                def body(pair, first):
                    for u in range(2):
                        head = 2 * pair + u
                        if not first:
                            pool.wait_ge(masks_used, NB * NCH * (head - 1))
                        for v in range(T // JV):
                            js = slice(v * JV, (v + 1) * JV)
                            base = NP * head + 5 * v

                            def part(n):
                                return parts[u][:, js, :].rearrange("p j (s n c) -> p j s n c", s=3, n=3)[:, :, 0::2, n, :]

                            if not first or u or v:
                                pool.wait_ge(parts_step, base)
                                settle(pool)
                            nc.gpsimd.tensor_tensor(
                                weighted[:],
                                values[:, js, head, :].unsqueeze(2).broadcast_to([P, JV, 2, c1]),
                                exp_s2[:, js, head, :].unsqueeze(3).broadcast_to([P, JV, 2, c1]),
                                ALU.mult).then_inc(parts_step, 1)
                            pool.wait_ge(parts_step, base + 1)
                            settle(pool)
                            nc.gpsimd.tensor_copy(part(0), weighted[:]).then_inc(parts_step, 1)
                            pool.wait_ge(parts_step, base + 2)
                            nc.gpsimd.tensor_tensor(rest[:], weighted[:], part(0), ALU.subtract).then_inc(parts_step, 1)
                            pool.wait_ge(parts_step, base + 3)
                            settle(pool)
                            nc.gpsimd.tensor_copy(part(1), rest[:]).then_inc(parts_step, 1)
                            pool.wait_ge(parts_step, base + 4)
                            nc.gpsimd.tensor_tensor(part(2), rest[:], part(1), ALU.subtract).then_inc(parts_step, 1)
                        pool.wait_ge(parts_step, NP * (head + 1))
                        settle(pool)
                        nc.gpsimd.tensor_scalar(parts[u][:, :, 3 * c1:6 * c1], parts[u][:, :, 6 * c1:9 * c1],
                                                -1.0, 1.0, ALU.mult, ALU.mult).then_inc(parts_ready, 1)
                head_pairs(pool, body)

            @block.scalar
            def _(act):
                def body(pair, first):
                    for k in range(HC):
                        head = 2 * pair + k // NCH
                        g = pair * HC + k
                        act.wait_ge(s1_loaded[k % 2], 16 * (pair * NCH + k // 2 + 1))
                        settle(act)
                        for b in range(NB):
                            if not first or k >= 1:
                                act.wait_ge(masks_used, NB * (g - 1) + b + 1)
                                settle(act)
                            for q in range(JB):
                                j = b * JB + q
                                op = nc.scalar.activation(mask[b][:, q, :], s1_wide[k % 2][:], ACT.Relu,
                                                          bias=step_bias[:, j, bass.ds(head, 1)],
                                                          scale=STEP_SCALE)
                            op.then_inc(steps_ready, 1)
                head_pairs(act, body)

            @block.vector
            def _(dve):
                def make_masks(pair, k, b):
                    c = k % NCH
                    g = pair * HC + k
                    dve.wait_ge(steps_ready, NB * g + b + 1)
                    nc.vector.tensor_tensor(mask[b], mask[b],
                                            adj_t[:, b * JB:(b + 1) * JB, c * CW:(c + 1) * CW],
                                            ALU.min).then_inc(masks_ready, 1)

                def evacuate(pair, k):
                    c = k % NCH
                    head = 2 * pair + k // NCH
                    g = pair * HC + k
                    its = slice(c * IT, (c + 1) * IT)
                    base = NEVAC * g
                    done = [0]

                    def link(op):
                        op.then_inc(evac_step, 1)
                        done[0] += 1
                        return base + done[0]

                    wide = [P, IT, c1]
                    if not isinstance(base, int) or base > 0:
                        dve.wait_ge(evac_step, base)
                    dve.wait_ge(masks_used, NB * (g + 1))
                    sums = ps[k % 2][:, :, 0:6 * c1].rearrange("p i (s n c) -> p i s c n", s=2, n=3)
                    link(nc.vector.tensor_reduce(sum_a[:], sums[:, :, 0], AX_X, ALU.add))
                    op = nc.vector.tensor_reduce(sum_b[:], sums[:, :, 1], AX_X, ALU.add)
                    op.then_inc(psum_free, 1)
                    dve.wait_ge(evac_step, base + 1)
                    link(nc.vector.tensor_tensor(sum_a[:], sum_a[:],
                                                 row_exps[:, its, 0, bass.ds(head, 1)].broadcast_to(wide), ALU.mult))
                    dve.wait_ge(psum_free, g + 3)
                    at = link(nc.vector.tensor_tensor(sum_b[:], sum_b[:],
                                                      row_exps[:, its, 1, bass.ds(head, 1)].broadcast_to(wide), ALU.mult))
                    dve.wait_ge(evac_step, at)
                    at = link(nc.vector.tensor_tensor(num_den[:], sum_a[:], sum_b[:], ALU.add))
                    if mean_rows is not None:
                        lonely_col, all_rows = mean_rows
                        dve.wait_ge(evac_step, at)
                        link(nc.vector.tensor_tensor(sum_a[:], lonely_col[:, its].unsqueeze(2).broadcast_to(wide),
                                                     all_rows[:, bass.ds(head, 1), :].broadcast_to(wide), ALU.mult))
                        dve.wait_ge(evac_step, at + 1)
                        at = link(nc.vector.tensor_tensor(num_den[:], num_den[:], sum_a[:], ALU.add))
                    dve.wait_ge(evac_step, at)
                    at = link(nc.vector.reciprocal(recip[:], num_den[:, :, dh:dh + 1]))
                    dve.wait_ge(evac_step, at)
                    at = link(nc.vector.tensor_tensor(hidden[:, its, bass.ds(head * dh, dh)], num_den[:, :, 0:dh],
                                                      recip[:].broadcast_to([P, IT, dh]), ALU.mult))
                    assert done[0] == NEVAC

                def body(pair, first):
                    for k in range(HC):
                        for b in range(NB):
                            make_masks(pair, k, b)
                            if b == 1 and k >= 1:
                                evacuate(pair, k - 1)
                            if b == 1 and k == 0 and not first:
                                evacuate(pair - 1, HC - 1)

                dve.sem_inc(psum_free, 2)
                head_pairs(dve, body)
                evacuate(heads // 2 - 1, HC - 1)

            @block.tensor
            def _(pe):
                def body(pair, first):
                    for k in range(HC):
                        g = pair * HC + k
                        c, u = k % NCH, k // NCH
                        if c == 0:
                            pe.wait_ge(parts_ready, 2 * pair + u + 1)
                        pe.wait_ge(psum_free, g + 1)
                        for b in range(NB):
                            pe.wait_ge(masks_ready, NB * g + b + 1)
                            for it in range(IT):
                                opens_bank = b == 0 and it * region % 512 == 0
                                for q in range(JB):
                                    j = b * JB + q
                                    out = ps[k % 2][:, it, :]
                                    nc.tensor.matmul(out[:, 0:6 * c1], mask[b][:, q, it * P:(it + 1) * P],
                                                     parts[u][:, j, 0:6 * c1],
                                                     start=(opens_bank and q == 0), stop=(j == T - 1),
                                                     skip_group_check=True)
                                    mm = nc.tensor.matmul(out[:, 3 * c1:6 * c1],
                                                          adj_t[:, j, c * CW + it * P:c * CW + (it + 1) * P],
                                                          parts[u][:, j, 6 * c1:9 * c1],
                                                          start=False, stop=(j == T - 1), skip_group_check=True)
                            mm.then_inc(masks_used, 1)
                with pe.Fori(0, heads // 2) as pair:
                    body(pair, False)


class Split:

    def __init__(self, nc, m, parts):
        self.nc, self.parts = nc, parts
        self.rest = [m.sb(f"split_rest{p}", [P, D]) for p in range(2)]
        self.hi_done = m.sem("split_hi_done")
        self.rest_ready = m.sem("split_rest_ready")
        self.done = m.sem("split_done")

    def vector(self, dve, h, t, par):
        nc = self.nc
        nc.vector.tensor_copy(self.parts[:, t, 0, :], h).then_inc(self.hi_done, 1)
        dve.wait_ge(self.hi_done, t + 1)
        return nc.vector.tensor_tensor(self.rest[par][:], h, self.parts[:, t, 0, :], ALU.subtract)\
            .then_inc(self.rest_ready, 1)

    def scalar(self, act, t, par):
        act.wait_ge(self.rest_ready, t + 1)
        self.nc.scalar.mul(self.parts[:, t, 1, :], self.rest[par][:], LO_SCALE).then_inc(self.done, 1)


def build_attention_out(nc, consts, x_src, x_dst, hidden, w_dram, b_dram, h_parts, adj_t, lonely):
    with ExitStack() as stack:
        m = Mem(nc, stack, "out0")
        w = m.sb("w", [P, KT, D])
        bias = m.sb("bias", [P, D])
        x = [m.sb(f"x{p}", [P, D]) for p in range(2)]
        g = [m.sb(f"g{p}", [P, D]) for p in range(2)]
        gt = [m.sb(f"gt{p}", [P, KT, P]) for p in range(2)]
        y = [m.sb(f"y{p}", [P, D]) for p in range(2)]
        low = [m.sb(f"low{p}", [P, D]) for p in range(2)]
        x1 = [m.sb(f"x1{p}", [P, D]) for p in range(2)]
        h = [m.sb(f"h{p}", [P, D]) for p in range(2)]
        ps_t = [m.ps(f"ps_t{p}", [P, KT, P]) for p in range(2)]
        ps_y = [m.ps(f"ps_y{p}", [P, D]) for p in range(2)]
        ln = LayerNorm(nc, m, consts)
        split = Split(nc, m, h_parts)
        w_loaded = m.sem("w_loaded")
        x_loaded = [m.sem(f"x_loaded{p}") for p in range(2)]
        x1_stored = [m.sem(f"x1_stored{p}") for p in range(2)]
        g_ready = m.sem("g_ready")
        turned = m.sem("turned")
        gt_ready = m.sem("gt_ready")
        projected = m.sem("projected")
        y_ready = m.sem("y_ready")
        low_ready = m.sem("low_ready")
        exp_ready = m.sem("exp_ready")
        x_added = m.sem("x_added")
        x1_ready = m.sem("x1_ready")
        h_ready = m.sem("h_ready")
        with nc.Block() as block:

            @block.sync
            def _(sp):
                sp.dma_start(w[:], w_dram.rearrange("(k p) n -> p k n", p=P)).then_inc(w_loaded, 16)
                sp.dma_start(bias[:], b_dram.unsqueeze(0).broadcast_to([P, D])).then_inc(w_loaded, 16)
                load_tiles(sp, rows(x_src), x, x_loaded, x_added)

            @block.gpsimd
            def _(pool):
                def pick(t, pair, par):
                    if later(t):
                        pool.wait_ge(turned, t - 1)
                    consts["settle"](pool)
                    nc.gpsimd.tensor_copy(g[par][:], hidden[:, t, :]).then_inc(g_ready, 1)

                def store(t, pair, par):
                    pool.wait_ge(x1_ready, t + 1)
                    pool.dma_start(rows(x_dst)[t], x1[par][:]).then_inc(x1_stored[par], 16)

                staged_tiles(pool, (0, pick), (3, lambda t, pair, par: ln.pool(pool, t, par)), (3, store))
                for par in range(2):
                    pool.wait_ge(x1_stored[par], 16 * (T // 2))

            @block.tensor
            def _(pe):
                def turn(t, pair, par):
                    pe.wait_ge(g_ready, t + 1)
                    for k in range(KT):
                        mm = nc.tensor.transpose(ps_t[par][:, k, :], g[par][:, k * P:(k + 1) * P],
                                                 consts["ident"][:])
                    mm.then_inc(turned, 1)

                def project(t, pair, par):
                    pe.wait_ge(gt_ready, t + 1)
                    if later(t):
                        pe.wait_ge(y_ready, t - 1)
                    for k in range(KT):
                        mm = nc.tensor.matmul(ps_y[par][:], gt[par][:, k, :], w[:, k, :],
                                              start=(k == 0), stop=(k == KT - 1))
                    mm.then_inc(projected, 1)

                pe.wait_ge(w_loaded, 32)
                staged_tiles(pe, (0, turn), (1, project))

            @block.scalar
            def _(act):
                def turned_out(t, pair, par):
                    act.wait_ge(turned, t + 1)
                    nc.scalar.copy(gt[par][:], ps_t[par][:]).then_inc(gt_ready, 1)

                def exp_low(t, pair, par):
                    act.wait_ge(low_ready, t + 1)
                    nc.scalar.activation(low[par][:], low[par][:], ACT.Exp).then_inc(exp_ready, 1)

                def normed(t, pair, par):
                    if later(t):
                        act.wait_ge(split.rest_ready, t - 1)
                    ln.scalar(act, h[par][:], x1[par][:], t, par).then_inc(h_ready, 1)

                staged_tiles(act, (0, turned_out), (1, exp_low), (2, normed),
                             (3, lambda t, pair, par: split.scalar(act, t, par)))

            @block.vector
            def _(dve):
                def biased(t, pair, par):
                    dve.wait_ge(projected, t + 1)
                    nc.vector.tensor_tensor(y[par][:], ps_y[par][:], bias[:], ALU.add).then_inc(y_ready, 1)
                    dve.wait_ge(y_ready, t + 1)
                    nc.vector.tensor_scalar(low[par][:], y[par][:], 0.0, None, ALU.min).then_inc(low_ready, 1)
                    dve.wait_ge(x_loaded[par], 16 * (pair + 1))
                    dve.wait_ge(low_ready, t + 1)
                    nc.vector.scalar_tensor_tensor(out=y[par][:], in0=y[par][:], scalar=0.0, in1=x[par][:],
                                                   op0=ALU.max, op1=ALU.add).then_inc(x_added, 1)

                def residual(t, pair, par):
                    dve.wait_ge(exp_ready, t + 1)
                    dve.wait_ge(x_added, t + 1)
                    if later(t):
                        dve.wait_ge(x1_stored[par], 16 * pair)
                        dve.wait_ge(h_ready, t - 1)
                    nc.vector.scalar_tensor_tensor(out=x1[par][:], in0=low[par][:], scalar=-1.0, in1=y[par][:],
                                                   op0=ALU.add, op1=ALU.add).then_inc(x1_ready, 1)
                    dve.wait_ge(x1_ready, t + 1)
                    ln.vector(dve, x1[par][:], t, par)

                def halves(t, pair, par):
                    dve.wait_ge(h_ready, t + 1)
                    if later(t):
                        dve.wait_ge(split.done, t - 1)
                    split.vector(dve, h[par][:], t, par)

                def restore(t, pair, par):
                    nc.vector.tensor_tensor(adj_t[:, t, :], adj_t[:, t, :], lonely[:], ALU.subtract)

                dve.wait_ge(w_loaded, 32)
                staged_tiles(dve, (0, biased), (1, residual), (2, halves), (2, restore))


class AdjacencyProduct:

    def __init__(self, nc, m, matrix, parts):
        self.nc, self.matrix, self.parts = nc, matrix, parts
        self.hi = [m.ps(f"prod_hi{p}", [P, D]) for p in range(2)]
        self.lo = [m.ps(f"prod_lo{p}", [P, D]) for p in range(2)]
        self.lo_scaled = [m.sb(f"prod_lo_scaled{p}", [P, D]) for p in range(2)]
        self.summed = m.sem("prod_summed")
        self.lo_ready = m.sem("prod_lo_ready")
        self.joined = m.sem("prod_joined")

    def tensor(self, pe, t, par, js):
        if js[0] == 0 and later(t):
            pe.wait_ge(self.joined, t - 1)
            pe.wait_ge(self.lo_ready, t - 1)
        for j in js:
            for n, out in ((0, self.hi), (1, self.lo)):
                mm = self.nc.tensor.matmul(out[par][:], self.matrix[:, j, bass.ts(t, P)], self.parts[:, j, n, :],
                                           start=(j == 0), stop=(j == T - 1))
        if js[-1] == T - 1:
            mm.then_inc(self.summed, 1)

    def scalar(self, act, t, par, scale=1.0 / LO_SCALE):
        act.wait_ge(self.summed, t + 1)
        if later(t):
            act.wait_ge(self.joined, t - 1)
        if isinstance(scale, float):
            op = self.nc.scalar.mul(self.lo_scaled[par][:], self.lo[par][:], scale)
        else:
            op = self.nc.scalar.activation(self.lo_scaled[par][:], self.lo[par][:], ACT.Copy, scale=scale)
        op.then_inc(self.lo_ready, 1)

    def vector(self, dve, out, t, par, scale=1.0):
        dve.wait_ge(self.lo_ready, t + 1)
        return self.nc.vector.scalar_tensor_tensor(out=out, in0=self.hi[par][:], scalar=scale,
                                                   in1=self.lo_scaled[par][:], op0=ALU.mult,
                                                   op1=ALU.add).then_inc(self.joined, 1)


def build_linear_layer(nc, consts, x_src, x_dst, wt_dram, b_dram, adj_dram, adj_t, h_parts, sym, stats, adj_copy):
    with ExitStack() as stack:
        m = Mem(nc, stack, "lin")
        w = m.sb("w", [P, KT, D])
        bias = m.sb("bias", [P, D])
        x = [m.sb(f"x{p}", [P, D]) for p in range(2)]
        agg = [m.sb(f"agg{p}", [P, D]) for p in range(2)]
        aggt = [m.sb(f"aggt{p}", [P, KT, P]) for p in range(2)]
        y = [m.sb("y", [P, D])] * 2
        x2 = [m.sb(f"x2{p}", [P, D]) for p in range(2)]
        adj_rows = m.sb("adj_rows", [P, N])
        ps_t = [m.ps(f"ps_t{p}", [P, KT, P]) for p in range(2)]
        ps_y = [m.ps(f"ps_y{p}", [P, D]) for p in range(2)]
        prod = AdjacencyProduct(nc, m, adj_t, h_parts)
        w_loaded = m.sem("w_loaded")
        x_loaded = [m.sem(f"x_loaded{p}") for p in range(2)]
        x2_stored = [m.sem(f"x2_stored{p}") for p in range(2)]
        adj_loaded = m.sem("adj_loaded")
        adj_counted = m.sem("adj_counted")
        sym_ready = m.sem("sym_ready")
        turned = m.sem("turned")
        aggt_ready = m.sem("aggt_ready")
        projected = m.sem("projected")
        y_ready = m.sem("y_ready")
        x2_ready = m.sem("x2_ready")
        deg_step = m.sem("deg_step")
        with nc.Block() as block:

            @block.sync
            def _(sp):
                sp.dma_start(w[:], wt_dram.rearrange("(k p) n -> p k n", p=P)).then_inc(w_loaded, 16)
                sp.dma_start(bias[:], b_dram.unsqueeze(0).broadcast_to([P, D])).then_inc(w_loaded, 16)
                load_tiles(sp, rows(x_src), x, x_loaded, x2_ready)

            @block.gpsimd
            def _(pool):
                def fetch(t, pair, par):
                    if later(t, 0):
                        pool.wait_ge(adj_counted, t)
                        pool.wait_ge(sym_ready, t)
                    pool.dma_start(adj_rows[:], rows(adj_dram)[t]).then_inc(adj_loaded, 16)

                def store(t, pair, par):
                    pool.wait_ge(x2_ready, t + 1)
                    pool.dma_start(rows(x_dst)[t], x2[par][:]).then_inc(x2_stored[par], 16)

                staged_tiles(pool, (0, fetch), (2, store))
                for par in range(2):
                    pool.wait_ge(x2_stored[par], 16 * (T // 2))
                pool.wait_ge(deg_step, 1)
                nc.gpsimd.tensor_tensor(stats["dinv"][:], stats["deg"][:],
                                        consts["neg_half"][:, 0:1].broadcast_to([P, T]), ALU.pow)\
                    .then_inc(deg_step, 1)

            @block.tensor
            def _(pe):
                def turn(t, pair, par):
                    pe.wait_ge(prod.joined, t + 1)
                    for k in range(KT):
                        mm = nc.tensor.transpose(ps_t[par][:, k, :], agg[par][:, k * P:(k + 1) * P],
                                                 consts["ident"][:])
                    mm.then_inc(turned, 1)

                def project(t, pair, par):
                    pe.wait_ge(aggt_ready, t + 1)
                    if later(t):
                        pe.wait_ge(y_ready, t - 1)
                    for k in range(KT):
                        mm = nc.tensor.matmul(ps_y[par][:], aggt[par][:, k, :], w[:, k, :],
                                              start=(k == 0), stop=(k == KT - 1))
                    mm.then_inc(projected, 1)

                pe.wait_ge(w_loaded, 32)
                staged_tiles(pe, (0, lambda t, pair, par: prod.tensor(pe, t, par, range(0, T // 2))), (1, turn),
                             (0, lambda t, pair, par: prod.tensor(pe, t, par, range(T // 2, T))), (1, project))

            @block.scalar
            def _(act):
                def turned_out(t, pair, par):
                    act.wait_ge(turned, t + 1)
                    nc.scalar.copy(aggt[par][:], ps_t[par][:]).then_inc(aggt_ready, 1)

                def count(t, pair, par):
                    act.wait_ge(adj_loaded, 16 * (t + 1))
                    nc.scalar.activation(adj_copy[:], adj_rows[:], ACT.Copy,
                                         accum_out=col(stats["neighbours"], t)).then_inc(adj_counted, 1)

                staged_tiles(act, (1, turned_out), (0, lambda t, pair, par: prod.scalar(act, t, par)), (0, count))

            @block.vector
            def _(dve):
                def join(t, pair, par):
                    if later(t):
                        dve.wait_ge(turned, t - 1)
                    prod.vector(dve, agg[par][:], t, par)

                def out(t, pair, par):
                    dve.wait_ge(projected, t + 1)
                    if later(t, 0):
                        dve.wait_ge(x2_ready, t)
                    nc.vector.tensor_tensor(y[par][:], ps_y[par][:], bias[:], ALU.add).then_inc(y_ready, 1)
                    dve.wait_ge(y_ready, t + 1)
                    dve.wait_ge(x_loaded[par], 16 * (pair + 1))
                    if later(t):
                        dve.wait_ge(x2_stored[par], 16 * pair)
                    nc.vector.scalar_tensor_tensor(out=x2[par][:], in0=y[par][:], scalar=0.0, in1=x[par][:],
                                                   op0=ALU.max, op1=ALU.add).then_inc(x2_ready, 1)

                def symmetric(t, pair, par):
                    dve.wait_ge(adj_loaded, 16 * (t + 1))
                    nc.vector.scalar_tensor_tensor(out=sym[:, t, :], in0=adj_rows[:], scalar=1.0,
                                                   in1=adj_t[:, t, :], op0=ALU.mult, op1=ALU.add,
                                                   accum_out=col(stats["deg2"], t)).then_inc(sym_ready, 1)
                    dve.wait_ge(sym_ready, t + 1)
                    diag = sym[:, t, bass.ts(t, P)]
                    nc.vector.scalar_tensor_tensor(out=diag, in0=consts["ident"][:], scalar=2.0, in1=diag,
                                                   op0=ALU.mult, op1=ALU.add)

                dve.wait_ge(w_loaded, 32)
                staged_tiles(dve, (0, symmetric), (0, join), (1, out))
                dve.wait_ge(sym_ready, T)
                nc.vector.tensor_scalar(stats["deg"][:], stats["deg2"][:], 0.5, 1.0, ALU.mult,
                                        ALU.add).then_inc(deg_step, 1)
                dve.wait_ge(adj_counted, T)
                nc.vector.tensor_scalar(stats["lonely"][:], stats["neighbours"][:], 0.0, None, ALU.is_equal)
                dve.wait_ge(deg_step, 2)
                nc.vector.tensor_scalar(stats["half_dinv"][:], stats["dinv"][:], 0.5, None, ALU.mult)
                nc.vector.tensor_scalar(stats["lo_half_dinv"][:], stats["dinv"][:], 0.5 / LO_SCALE, None, ALU.mult)


def build_scaled_rows(nc, consts, x_src, g_parts, stats):
    with ExitStack() as stack:
        m = Mem(nc, stack, "scaled")
        x = [m.sb(f"x{p}", [P, D]) for p in range(2)]
        h = [m.sb(f"h{p}", [P, D]) for p in range(2)]
        ln = LayerNorm(nc, m, consts, stats["dinv"])
        split = Split(nc, m, g_parts)
        x_loaded = [m.sem(f"x_loaded{p}") for p in range(2)]
        h_ready = m.sem("h_ready")
        with nc.Block() as block:

            @block.sync
            def _(sp):
                load_tiles(sp, rows(x_src), x, x_loaded, h_ready)

            @block.gpsimd
            def _(pool):
                staged_tiles(pool, (0, lambda t, pair, par: ln.pool(pool, t, par)))

            @block.scalar
            def _(act):
                def normed(t, pair, par):
                    if later(t):
                        act.wait_ge(split.rest_ready, t - 1)
                    ln.scalar(act, h[par][:], x[par][:], t, par).then_inc(h_ready, 1)

                staged_tiles(act, (0, normed), (1, lambda t, pair, par: split.scalar(act, t, par)))

            @block.vector
            def _(dve):
                def stats_of(t, pair, par):
                    dve.wait_ge(x_loaded[par], 16 * (pair + 1))
                    ln.vector(dve, x[par][:], t, par)

                def halves(t, pair, par):
                    dve.wait_ge(h_ready, t + 1)
                    if later(t):
                        dve.wait_ge(split.done, t - 1)
                    split.vector(dve, h[par][:], t, par)

                staged_tiles(dve, (0, stats_of), (1, halves))


def build_normalised_product(nc, consts, sym, g_parts, z_parts, stats):
    with ExitStack() as stack:
        m = Mem(nc, stack, "norm")
        z = m.sb("z", [P, D])
        prod = AdjacencyProduct(nc, m, sym, g_parts)
        split_rest = m.sb("rest", [P, D])
        hi_done = m.sem("hi_done")
        rest_ready = m.sem("rest_ready")
        lo_done = m.sem("lo_done")
        with nc.Block() as block:

            @block.tensor
            def _(pe):
                staged_tiles(pe, (0, lambda t, pair, par: prod.tensor(pe, t, par, range(T))))

            @block.scalar
            def _(act):
                def low(t, pair, par):
                    prod.scalar(act, t, par, col(stats["lo_half_dinv"], t))

                def lo_part(t, pair, par):
                    act.wait_ge(rest_ready, t + 1)
                    nc.scalar.mul(z_parts[:, t, 1, :], split_rest[:], LO_SCALE).then_inc(lo_done, 1)

                staged_tiles(act, (0, low), (0, lo_part))

            @block.vector
            def _(dve):
                def join(t, pair, par):
                    if later(t, 0):
                        dve.wait_ge(rest_ready, t)
                    prod.vector(dve, z[:], t, par, col(stats["half_dinv"], t))
                    dve.wait_ge(prod.joined, t + 1)
                    nc.vector.tensor_copy(z_parts[:, t, 0, :], z[:]).then_inc(hi_done, 1)
                    dve.wait_ge(hi_done, t + 1)
                    if later(t, 0):
                        dve.wait_ge(lo_done, t)
                    nc.vector.tensor_tensor(split_rest[:], z[:], z_parts[:, t, 0, :],
                                            ALU.subtract).then_inc(rest_ready, 1)

                staged_tiles(dve, (0, join))


def build_second_product(nc, x_src, x_dst, adj_t, z_parts, spare):
    with ExitStack() as stack:
        m = Mem(nc, stack, "second")
        x = [spare[:, p * D:(p + 1) * D] for p in range(2)]
        y = [m.sb("y", [P, D])] * 2
        x3 = [spare[:, (2 + p) * D:(3 + p) * D] for p in range(2)]
        prod = AdjacencyProduct(nc, m, adj_t, z_parts)
        x_loaded = [m.sem(f"x_loaded{p}") for p in range(2)]
        x3_stored = [m.sem(f"x3_stored{p}") for p in range(2)]
        x3_ready = m.sem("x3_ready")
        with nc.Block() as block:

            @block.sync
            def _(sp):
                load_tiles(sp, rows(x_src), x, x_loaded, x3_ready)

            @block.gpsimd
            def _(pool):
                def store(t, pair, par):
                    pool.wait_ge(x3_ready, t + 1)
                    pool.dma_start(rows(x_dst)[t], x3[par][:]).then_inc(x3_stored[par], 16)

                staged_tiles(pool, (0, store))
                for par in range(2):
                    pool.wait_ge(x3_stored[par], 16 * (T // 2))

            @block.tensor
            def _(pe):
                staged_tiles(pe, (0, lambda t, pair, par: prod.tensor(pe, t, par, range(T))))

            @block.scalar
            def _(act):
                staged_tiles(act, (0, lambda t, pair, par: prod.scalar(act, t, par)))

            @block.vector
            def _(dve):
                def residual(t, pair, par):
                    if later(t, 0):
                        dve.wait_ge(x3_ready, t)
                    prod.vector(dve, y[par][:], t, par)
                    dve.wait_ge(prod.joined, t + 1)
                    dve.wait_ge(x_loaded[par], 16 * (pair + 1))
                    if later(t):
                        dve.wait_ge(x3_stored[par], 16 * pair)
                    nc.vector.tensor_tensor(x3[par][:], y[par][:], x[par][:], ALU.add).then_inc(x3_ready, 1)

                staged_tiles(dve, (0, residual))


def build_value_sums(nc, heads, values, all_rows):
    c1 = D // heads + 1
    half = heads // 2
    with ExitStack() as stack:
        m = Mem(nc, stack, "sums")
        ones = m.sb("ones", [P, P])
        ps = [m.ps(f"ps{p}", [P, 512]) for p in range(2)]
        ones_set = m.sem("ones_set")
        summed = m.sem("summed")
        with nc.Block() as block:

            @block.tensor
            def _(pe):
                pe.wait_ge(ones_set, 1)
                for s in range(2):
                    for t in range(T):
                        mm = nc.tensor.matmul(ps[s][:, 0:half * c1], ones[:],
                                              values[:, t, s * half:(s + 1) * half, :].rearrange("p h c -> p (h c)"),
                                              start=(t == 0), stop=(t == T - 1))
                mm.then_inc(summed, 1)

            @block.vector
            def _(dve):
                nc.vector.memset(ones[:], 1.0).then_inc(ones_set, 1)
                dve.wait_ge(summed, 1)
                for s in range(2):
                    nc.vector.tensor_copy(all_rows[:, s * half:(s + 1) * half, :].rearrange("p h c -> p (h c)"),
                                          ps[s][:, 0:half * c1])


def build_perceptron(nc, consts, x_src, out, hidden, layers):
    (w1_dram, b1_dram), (w2_dram, b2_dram), (w3_dram, b3_dram), (w4_dram, b4_dram) = layers
    with ExitStack() as stack:
        m = Mem(nc, stack, "mlp")
        M1, M2, M3 = (w1_dram.shape[1] // P, w2_dram.shape[1] // P, w3_dram.shape[1] // P)
        w1 = m.sb("w1", [P, KT, M1 * P])
        w2 = m.sb("w2", [P, M1, M2 * P])
        w3 = m.sb("w3", [P, M2, M3 * P])
        w4 = m.sb("w4", [P, M3, D])
        b1 = m.sb("b1", [P, M1])
        b2 = m.sb("b2", [P, M2])
        b3 = m.sb("b3", [P, M3])
        b4 = m.sb("b4", [P, D])
        x = [m.sb(f"x{p}", [P, D]) for p in range(2)]
        low = [m.sb(f"low{p}", [P, D]) for p in range(2)]
        high = [m.sb(f"high{p}", [P, D]) for p in range(2)]
        enc = [m.sb(f"enc{p}", [P, D]) for p in range(2)]
        enct = [m.sb(f"enct{p}", [P, KT, P]) for p in range(2)]
        o1 = [m.sb(f"o1{p}", [P, M1, P]) for p in range(2)]
        o2 = [m.sb(f"o2{p}", [P, M2, P]) for p in range(2)]
        o3 = [m.sb(f"o3{p}", [P, M3, P]) for p in range(2)]
        xb = [m.sb(f"xb{p}", [P, D]) for p in range(2)]
        y = [m.sb(f"y{p}", [P, D]) for p in range(2)]
        ps_t = [m.ps(f"ps_t{p}", [P, KT, P]) for p in range(2)]
        ps_1 = [m.ps(f"ps_1{p}", [P, 512]) for p in range(2)]
        ps_2 = m.ps("ps_2", [P, 512])
        ps_3 = m.ps("ps_3", [P, 512])
        ps_4 = [m.ps(f"ps_4{p}", [P, D]) for p in range(2)]
        w_loaded = m.sem("w_loaded")
        x_loaded = [m.sem(f"x_loaded{p}") for p in range(2)]
        stored = [m.sem(f"stored{p}") for p in range(2)]
        low_ready = m.sem("low_ready")
        high_ready = m.sem("high_ready")
        exp_ready = m.sem("exp_ready")
        enc_ready = m.sem("enc_ready")
        turned = m.sem("turned")
        enct_ready = m.sem("enct_ready")
        summed = [m.sem(f"summed{n}") for n in range(1, 5)]
        relu_ready = [m.sem(f"relu_ready{n}") for n in range(1, 4)]
        xb_ready = m.sem("xb_ready")
        y_ready = m.sem("y_ready")

        with nc.Block() as block:

            @block.sync
            def _(sp):
                for w, dram in ((w1, w1_dram), (w2, w2_dram), (w3, w3_dram), (w4, w4_dram)):
                    sp.dma_start(w[:], dram.rearrange("(k p) n -> p k n", p=P)).then_inc(w_loaded, 16)
                for b, dram in ((b1, b1_dram), (b2, b2_dram), (b3, b3_dram)):
                    sp.dma_start(b[:], dram).then_inc(w_loaded, 16)
                sp.dma_start(b4[:], b4_dram.unsqueeze(0).broadcast_to([P, D])).then_inc(w_loaded, 16)
                load_tiles(sp, rows(x_src), x, x_loaded, xb_ready)

            @block.gpsimd
            def _(pool):
                def biased(t, pair, par):
                    pool.wait_ge(x_loaded[par], 16 * (pair + 1))
                    if later(t):
                        pool.wait_ge(y_ready, t - 1)
                    nc.gpsimd.tensor_tensor(xb[par][:], x[par][:], b4[:], ALU.add).then_inc(xb_ready, 1)

                def store(t, pair, par):
                    pool.wait_ge(y_ready, t + 1)
                    pool.dma_start(rows(out)[t], y[par][:]).then_inc(stored[par], 16)

                pool.wait_ge(w_loaded, 16 * 8)
                staged_tiles(pool, (0, biased), (2, store))
                for par in range(2):
                    pool.wait_ge(stored[par], 16 * (T // 2))

            @block.tensor
            def _(pe):
                def turn(t, pair, par):
                    pe.wait_ge(enc_ready, t + 1)
                    for k in range(KT):
                        mm = nc.tensor.transpose(ps_t[par][:, k, :], enc[par][:, k * P:(k + 1) * P],
                                                 consts["ident"][:])
                    mm.then_inc(turned, 1)

                def layer(n, ps, w, src, src_ready, kts, mts, free, lag_free):
                    def emit(t, pair, par):
                        pe.wait_ge(src_ready, t + 1)
                        if later(t, lag_free - 1):
                            pe.wait_ge(free, t + 1 - lag_free)
                        o = ps[par] if isinstance(ps, list) else ps
                        for mt in range(mts):
                            for k in range(kts):
                                mm = nc.tensor.matmul(o[:, mt * P:(mt + 1) * P], w[:, k, mt * P:(mt + 1) * P],
                                                      src[par][:, k, :], start=(k == 0), stop=(k == kts - 1))
                        mm.then_inc(summed[n - 1], 1)
                    return emit

                def last(t, pair, par):
                    pe.wait_ge(relu_ready[2], t + 1)
                    if later(t):
                        pe.wait_ge(y_ready, t - 1)
                    for k in range(M3):
                        mm = nc.tensor.matmul(ps_4[par][:], o3[par][:, k, :], w4[:, k, :],
                                              start=(k == 0), stop=(k == M3 - 1))
                    mm.then_inc(summed[3], 1)

                pe.wait_ge(w_loaded, 16 * 8)
                staged_tiles(pe, (0, turn), (4, last),
                             (3, layer(3, ps_3, w3, o2, relu_ready[1], M2, M3, relu_ready[2], 1)),
                             (2, layer(2, ps_2, w2, o1, relu_ready[0], M1, M2, relu_ready[1], 1)),
                             (1, layer(1, ps_1, w1, enct, enct_ready, KT, M1, relu_ready[0], 2)))

            @block.scalar
            def _(act):
                def exps(t, pair, par):
                    act.wait_ge(low_ready, t + 1)
                    nc.scalar.activation(low[par][:], low[par][:], ACT.Exp).then_inc(exp_ready, 1)

                def turned_out(t, pair, par):
                    act.wait_ge(turned, t + 1)
                    nc.scalar.copy(enct[par][:], ps_t[par][:]).then_inc(enct_ready, 1)

                def relu(n, ps, dst, b, mts):
                    def emit(t, pair, par):
                        act.wait_ge(summed[n - 1], t + 1)
                        o = ps[par] if isinstance(ps, list) else ps
                        for mt in range(mts):
                            op = nc.scalar.activation(dst[par][:, mt, :], o[:, mt * P:(mt + 1) * P], ACT.Relu,
                                                      bias=b[:, mt:mt + 1])
                        op.then_inc(relu_ready[n - 1], 1)
                    return emit

                act.wait_ge(w_loaded, 16 * 8)
                staged_tiles(act, (1, turned_out), (4, relu(3, ps_3, o3, b3, M3)), (3, relu(2, ps_2, o2, b2, M2)),
                             (2, relu(1, ps_1, o1, b1, M1)), (0, exps))

            @block.vector
            def _(dve):
                def parts_of(t, pair, par):
                    if later(t):
                        dve.wait_ge(enc_ready, t - 1)
                    nc.vector.tensor_scalar(low[par][:], hidden[:, t, :], 0.0, None, ALU.min).then_inc(low_ready, 1)
                    nc.vector.tensor_scalar(high[par][:], hidden[:, t, :], 0.0, None, ALU.max).then_inc(high_ready, 1)

                def encode(t, pair, par):
                    dve.wait_ge(exp_ready, t + 1)
                    dve.wait_ge(high_ready, t + 1)
                    if later(t):
                        dve.wait_ge(turned, t - 1)
                    nc.vector.scalar_tensor_tensor(out=enc[par][:], in0=low[par][:], scalar=-1.0, in1=high[par][:],
                                                   op0=ALU.add, op1=ALU.add).then_inc(enc_ready, 1)

                def final(t, pair, par):
                    dve.wait_ge(summed[3], t + 1)
                    dve.wait_ge(xb_ready, t + 1)
                    if later(t):
                        dve.wait_ge(stored[par], 16 * pair)
                    nc.vector.tensor_tensor(y[par][:], ps_4[par][:], xb[par][:], ALU.add).then_inc(y_ready, 1)

                staged_tiles(dve, (0, parts_of), (1, encode), (5, final))


def build(nc, a, out):
    x1 = nc.dram_tensor("after_l0", (N, D), F32, kind="Internal").ap()
    x2 = nc.dram_tensor("after_l1", (N, D), F32, kind="Internal").ap()
    x3 = nc.dram_tensor("after_l2", (N, D), F32, kind="Internal").ap()

    def attention_memory(stack, prefix, heads):
        m = Mem(nc, stack, prefix)
        return {"values": m.sb("values", [P, T, heads, D // heads + 1]),
                "exp_s2": m.sb("exp_s2", [P, T, heads, 2]),
                "step_bias": m.sb("step_bias", [P, T, heads]),
                "row_exps": m.sb("row_exps", [P, T, 2, heads])}

    with ExitStack() as stack:
        m = Mem(nc, stack, "all")
        consts = {"neg_half": m.sb("neg_half", [P, 1]), "ident": m.sb("ident", [P, P]),
                  "ones_bf16": m.sb("ones_bf16", [P, P], BF16)}
        passed = m.sem("wait_passed")
        consts["settle"] = lambda eng: eng.sem_inc(passed, 1)
        stats = {n: m.sb(n, [P, T]) for n in ("deg2", "deg", "dinv", "half_dinv", "lo_half_dinv", "neighbours",
                                              "lonely")}
        adj_t = m.sb("adj_t", [P, T, N], BF16)
        sym = m.sb("sym_or_hidden", [P, T, N], BF16)
        flat = sym[:].rearrange("p t n -> p (t n)")
        hidden = flat[:, 0:T * N // 2].bitcast(F32).rearrange("p (t d) -> p t d", t=T)
        ring = flat[:, T * N // 2:T * N]
        spare = ring.bitcast(F32)
        adj_loaded = m.sem("adj_t_loaded")
        with nc.Block() as block:

            @block.gpsimd
            def _(pool):
                for b in range(NB):
                    pool.dma_start(adj_t[:, b * JB:(b + 1) * JB, :],
                                   a["adj_t"][b * JB * P:(b + 1) * JB * P, :].rearrange("(j p) n -> p j n", p=P))\
                        .then_inc(adj_loaded, 16)

        build_constants(nc, consts)
        wide = m.sb("lonely_wide", [P, N], BF16)
        with ExitStack() as att:
            keep = attention_memory(att, "keep0", 16)
            s1 = nc.dram_tensor("s1_rows0", (16, N), F32, kind="Internal").ap()
            build_projection(nc, "proj0", consts, a["x"], a["w0"], a["a0"], 16, keep, s1, spare)
            build_lonely_rows(nc, consts, adj_t, adj_loaded, wide)
            build_attention(nc, "att0", consts["settle"], 16, keep, adj_t, s1, ring, hidden)
        with ExitStack() as layers:
            h_parts = Mem(nc, layers, "gcn").sb("h_parts", [P, T, 2, D], F16)
            build_attention_out(nc, consts, a["x"], x1, hidden, a["w0_out"], a["b0_out"], h_parts, adj_t, wide)
            build_linear_layer(nc, consts, x1, x2, a["w1_t"], a["b1"], a["adj"], adj_t, h_parts, sym, stats, wide)
            build_scaled_rows(nc, consts, x2, h_parts, stats)
            z_parts = Mem(nc, layers, "gcn2").sb("z_parts", [P, T, 2, D], F16)
            build_normalised_product(nc, consts, sym, h_parts, z_parts, stats)
            build_second_product(nc, x2, x3, adj_t, z_parts, spare)
        with ExitStack() as att:
            keep = attention_memory(att, "keep3", 8)
            all_rows = Mem(nc, att, "gat3").sb("all_rows", [P, 8, D // 8 + 1])
            s1 = nc.dram_tensor("s1_rows3", (8, N), F32, kind="Internal").ap()
            build_projection(nc, "proj3", consts, x3, a["w3"], a["a3"], 8, keep, s1, spare)
            build_value_sums(nc, 8, keep["values"], all_rows)
            build_attention(nc, "att3", consts["settle"], 8, keep, adj_t, s1, ring, hidden, (stats["lonely"], all_rows))
        build_perceptron(nc, consts, x3, out, hidden,
                         [(a[f"mlp_w{n}_t"], a[f"mlp_b{n}"]) for n in range(1, 5)])


def kernel(**inputs):
    import numpy as np
    import concourse.bacc as bacc
    from concourse.bass_utils import run_bass_kernel_spmd

    i = {k: np.asarray(v) for k, v in inputs.items()}
    laid = {
        "x": i["x"], "adj": i["adj"], "adj_t": i["adj"].T,
        "w0": i["L0_gnn_W_seq"],
        "a0": np.stack([np.tile(i["L0_gnn_a1"], 16), np.tile(i["L0_gnn_a2"], 16)]),
        "w0_out": i["L0_gnn_W_out"], "b0_out": i["L0_gnn_b_out"],
        "w1_t": i["L1_gnn_W"].T, "b1": i["L1_gnn_b"],
        "w3": i["L3_gnn_W"].transpose(1, 0, 2).reshape(D, D),
        "a3": np.stack([i["L3_gnn_a1"].reshape(D), i["L3_gnn_a2"].reshape(D)]),
    }
    for n in range(1, 5):
        laid[f"mlp_w{n}_t"] = i[f"L3_gnn_W{n}"].T
        b = i[f"L3_gnn_b{n}"]
        laid[f"mlp_b{n}"] = b if n == 4 else b.reshape(-1, P).T
    nc = bacc.Bacc("TRN2", target_bir_lowering=False, num_devices=1)
    arrays = {f"in_{k}": np.ascontiguousarray(v) for k, v in laid.items()}
    aps = {k: nc.dram_tensor(f"in_{k}", arrays[f"in_{k}"].shape, F32, kind="ExternalInput").ap() for k in laid}
    out = nc.dram_tensor("out_0_dram", (N, D), F32, kind="ExternalOutput").ap()
    build(nc, aps, out)
    return run_bass_kernel_spmd(nc, [arrays], core_ids=[0]).results[0]["out_0_dram"]
```

```python
from contextlib import ExitStack

import concourse.bass as bass
from concourse import mybir

F32 = mybir.dt.float32
BF16 = mybir.dt.bfloat16
F16 = mybir.dt.float16
ALU = mybir.AluOpType
ACT = mybir.ActivationFunctionType
AX_X = mybir.AxisListType.X

P = 128
N = 2048
T = N // P
D = 512
KT = D // P
EPS = 1e-5
SLOPE = 0.2
LO_SCALE = float(2**11)
STEP_SCALE = float(2**60)
JB = 4
NB = T // JB
RING = 4


def later(t, than=1):
    return not isinstance(t, int) or t > than


def col(x, t):
    return x[:, bass.ds(t, 1)]


def staged_tiles(eng, *stages):
    lags = [lag for lag, _ in stages]
    head = (max(lags) + 3) // 2 * 2
    tail = T + min(lags) - min(lags) % 2

    def step(base, q, checked):
        for lag, emit in stages:
            par = (q - lag) % 2
            pair = base + (q - lag - par) // 2
            if not checked or 0 <= 2 * pair + par < T:
                emit(2 * pair + par, pair, par)

    for s in range(head):
        step(s // 2, s % 2, True)
    with eng.Fori(head // 2, tail // 2) as i:
        for q in range(2):
            step(i, q, False)
    for s in range(tail, T + max(lags)):
        step(s // 2, s % 2, True)


class Mem:

    def __init__(self, nc, stack, prefix):
        self.nc, self.stack, self.prefix, self.sems = nc, stack, prefix, []

    def sb(self, name, shape, dt=F32):
        return self.stack.enter_context(self.nc.sbuf_tensor(f"{self.prefix}_{name}", shape, dt))

    def ps(self, name, shape, dt=F32):
        return self.stack.enter_context(self.nc.psum_tensor(f"{self.prefix}_{name}", shape, dt))

    def sem(self, name):
        self.sems.append(self.stack.enter_context(self.nc.semaphore(f"{self.prefix}_{name}")))
        return self.sems[-1]


class LayerNorm:

    def __init__(self, nc, m, consts, row_factor=None):
        self.nc, self.consts, self.row_factor = nc, consts, row_factor
        self.stats = [m.sb(f"ln_stats{p}", [P, 6]) for p in range(2)]
        self.mean_var = [m.sb(f"ln_mean_var{p}", [P, 2]) for p in range(2)]
        self.var_eps = [m.sb(f"ln_var_eps{p}", [P, 1]) for p in range(2)]
        self.neg_mean = [m.sb(f"ln_neg_mean{p}", [P, 1]) for p in range(2)]
        self.rstd = [m.sb(f"ln_rstd{p}", [P, 1]) for p in range(2)]
        self.scale = [m.sb(f"ln_scale{p}", [P, 1]) for p in range(2)]
        self.shift = [m.sb(f"ln_shift{p}", [P, 1]) for p in range(2)]
        self.stats_done = m.sem("ln_stats_done")
        self.moments_done = m.sem("ln_moments_done")
        self.moments_ready = m.sem("ln_moments_ready")
        self.rstd_done = m.sem("ln_rstd_done")
        self.scale_done = m.sem("ln_scale_done")
        self.coefs_ready = m.sem("ln_coefs_ready")

    def vector(self, dve, x, t, par):
        self.vector_stats(dve, x, t, par)
        self.vector_moments(dve, t, par)

    def vector_stats(self, dve, x, t, par):
        self.nc.vector.bn_stats(self.stats[par][:], x).then_inc(self.stats_done, 1)

    def vector_moments(self, dve, t, par):
        nc = self.nc
        dve.wait_ge(self.stats_done, t + 1)
        self.consts["settle"](dve)
        nc.vector.bn_aggr(self.mean_var[par][:], self.stats[par][:]).then_inc(self.moments_done, 1)
        dve.wait_ge(self.moments_done, t + 1)
        nc.vector.tensor_scalar(self.var_eps[par][:], self.mean_var[par][:, 1:2], EPS, None, ALU.add)
        nc.vector.tensor_scalar(self.neg_mean[par][:], self.mean_var[par][:, 0:1], -1.0, None,
                                ALU.mult).then_inc(self.moments_ready, 1)

    def pool(self, pool, t, par):
        nc = self.nc
        pool.wait_ge(self.moments_ready, t + 1)
        nc.gpsimd.tensor_tensor(self.rstd[par][:], self.var_eps[par][:], self.consts["neg_half"][:, 0:1],
                                ALU.pow).then_inc(self.rstd_done, 1)
        pool.wait_ge(self.rstd_done, t + 1)
        last = self.rstd[par]
        if self.row_factor is not None:
            nc.gpsimd.tensor_tensor(self.scale[par][:], self.rstd[par][:], col(self.row_factor, t),
                                    ALU.mult).then_inc(self.scale_done, 1)
            pool.wait_ge(self.scale_done, t + 1)
            last = self.scale[par]
        nc.gpsimd.tensor_tensor(self.shift[par][:], self.neg_mean[par][:], last[:],
                                ALU.mult).then_inc(self.coefs_ready, 1)

    def scalar(self, act, out, x, t, par):
        act.wait_ge(self.coefs_ready, t + 1)
        scale = self.rstd if self.row_factor is None else self.scale
        return self.nc.scalar.activation(out, x, ACT.Relu, bias=self.shift[par][:], scale=scale[par][:])


def load_tiles(sp, src, dst, loaded, used, used_lead=2):
    def load(t, pair, par):
        sp.dma_start(dst[par][:], src[t]).then_inc(loaded[par], 16)

    for par in range(2):
        load(par, 0, par)
    with sp.Fori(1, T // 2) as pair:
        for par in range(2):
            sp.wait_ge(used, 2 * pair + par - 1)
            load(2 * pair + par, pair, par)


def rows(x):
    return x.rearrange("(t p) d -> t p d", p=P)


def build_constants(nc, consts):
    with ExitStack() as stack:
        m = Mem(nc, stack, "const")
        filled = m.sem("filled")
        with nc.Block() as block:

            @block.gpsimd
            def _(pool):
                nc.gpsimd.memset(consts["neg_half"][:], -0.5)
                nc.gpsimd.memset(consts["ones_bf16"][:], 1.0)
                nc.gpsimd.memset(consts["ident"][:], 0.0).then_inc(filled, 1)
                pool.wait_ge(filled, 1)
                nc.gpsimd.affine_select(out=consts["ident"][:], in_=consts["ident"][:],
                                        compare_op=ALU.not_equal, fill=1.0, base=0, pattern=[[-1, P]],
                                        channel_multiplier=1)
    return m.sems


def build_projection(nc, name, consts, x_src, w_dram, a12_dram, heads, keep, s1_dram, spare,
                     adj_loads=None, has_neighbour=None, value_sum=None):
    dh = D // heads
    with ExitStack() as stack:
        m = Mem(nc, stack, name)
        w = m.sb("w", [P, KT, D])
        a12 = m.sb("a12", [P, 2, D])
        wa_terms = spare[:, 0:KT * D].rearrange("p (k n) -> p k n", k=KT)
        wa = m.sb("wa", [P, KT, 2 * heads])
        x = [m.sb(f"x{p}", [P, D]) for p in range(2)]
        h = [m.sb(f"h{p}", [P, D]) for p in range(2)]
        ht = [m.sb(f"ht{p}", [P, KT, P]) for p in range(2)]
        s12 = m.sb("s12", [P, T, 2 * heads])
        s12_tile = [m.sb(f"s12_tile{p}", [P, 2 * heads]) for p in range(2)]
        clipped = m.sb("clipped", [P, T, 2, heads])
        s1_rows = spare[0:heads, KT * D:KT * D + N]
        ps_t = [m.ps(f"ps_t{p}", [P, KT, P]) for p in range(2)]
        ps_v = [m.ps(f"ps_v{p}", [P, D]) for p in range(2)]
        ps_s = [m.ps(f"ps_s{p}", [P, 512]) for p in range(2)]
        ps_r = [m.ps(f"ps_r{p}", [P, 512]) for p in range(2)]
        ln = LayerNorm(nc, m, consts)
        w_loaded = m.sem("w_loaded")
        x_loaded = [m.sem(f"x_loaded{p}") for p in range(2)]
        h_ready = m.sem("h_ready")
        h_transposed = m.sem("h_transposed")
        ht_ready = m.sem("ht_ready")
        wa_step = m.sem("wa_step")
        wa_ready = m.sem("wa_ready")
        ones_set = m.sem("ones_set")
        projected = m.sem("projected")
        values_out = m.sem("values_out")
        rows_out = m.sem("rows_out")
        clip_ready = m.sem("clip_ready")
        s1_stored = m.sem("s1_stored")
        sum_step = m.sem("sum_step")
        rows_turned = m.sem("rows_turned")
        tile_scores = m.sem("tile_scores")
        exps_ready = m.sem("exps_ready")
        values, exp_s2, step_bias, row_exps = keep["values"], keep["exp_s2"], keep["step_bias"], keep["row_exps"]
        with nc.Block() as block:

            @block.sync
            def _(sp):
                sp.dma_start(w[:], w_dram.rearrange("(k p) n -> p k n", p=P)).then_inc(w_loaded, 16)
                sp.dma_start(a12[:], a12_dram.unsqueeze(0).broadcast_to([P, 2, D])).then_inc(w_loaded, 16)
                load_tiles(sp, rows(x_src), x, x_loaded, h_ready)
                sp.wait_ge(rows_out, T)
                sp.dma_start(s1_dram, s1_rows).then_inc(s1_stored, 16)
                sp.wait_ge(s1_stored, 16)

            @block.gpsimd
            def _(pool):
                if adj_loads is not None:
                    adj_loads(pool)
                nc.gpsimd.memset(values[:, :, :, dh:dh + 1], 1.0).then_inc(ones_set, 1)
                if value_sum is None:
                    staged_tiles(pool, (0, lambda t, pair, par: ln.pool(pool, t, par)))
                else:
                    def add_values(t, pair, par):
                        pool.wait_ge(sum_step, t + 1)
                        pool.wait_ge(values_out, t + 3)
                        consts["settle"](pool)
                        nc.gpsimd.tensor_tensor(value_sum[:], value_sum[:], values[:, t, :, :],
                                                ALU.add).then_inc(sum_step, 1)

                    nc.gpsimd.memset(value_sum[:], 0.0).then_inc(sum_step, 1)
                    pool.wait_ge(ones_set, 1)
                    staged_tiles(pool, (0, lambda t, pair, par: ln.pool(pool, t, par)), (3, add_values))

            @block.scalar
            def _(act):
                def normed(t, pair, par):
                    if later(t):
                        act.wait_ge(h_transposed, t - 1)
                    ln.scalar(act, h[par][:], x[par][:], t, par).then_inc(h_ready, 1)

                def transposed_out(t, pair, par):
                    act.wait_ge(h_transposed, t + 1)
                    nc.scalar.copy(ht[par][:], ps_t[par][:]).then_inc(ht_ready, 1)

                def rows_copy(t, pair, par):
                    act.wait_ge(rows_turned, t + 1)
                    nc.scalar.copy(s1_rows[:, bass.ts(t, P)], ps_r[par][0:heads, 0:P]).then_inc(rows_out, 1)

                staged_tiles(act, (0, normed), (1, transposed_out), (3, rows_copy))
                act.wait_ge(values_out, T + 2)
                nc.scalar.activation(exp_s2[:, :, :, 0], s12[:, :, heads:], ACT.Exp)
                nc.scalar.activation(exp_s2[:, :, :, 1], s12[:, :, heads:], ACT.Exp, scale=SLOPE)
                nc.scalar.mul(step_bias[:], s12[:, :, heads:], STEP_SCALE)
                act.wait_ge(clip_ready, 1)
                nc.scalar.activation(row_exps[:, :, 0, :], clipped[:, :, 0, :], ACT.Exp, scale=1.0 - SLOPE)
                nc.scalar.activation(row_exps[:, :, 1, :], clipped[:, :, 1, :], ACT.Exp, scale=SLOPE - 1.0).then_inc(exps_ready, 1)

            @block.vector
            def _(dve):
                def stats(t, pair, par):
                    dve.wait_ge(x_loaded[par], 16 * (pair + 1))
                    ln.vector(dve, x[par][:], t, par)

                def out(t, pair, par):
                    dve.wait_ge(projected, t + 1)
                    nc.vector.tensor_copy(values[:, t, :, 0:dh],
                                          ps_v[par][:].rearrange("p (h d) -> p h d", h=heads))
                    if later(t):
                        dve.wait_ge(rows_turned, t - 1)
                    nc.vector.tensor_copy(s12_tile[par][:], ps_s[par][:, 0:2 * heads]).then_inc(tile_scores, 1)
                    nc.vector.tensor_copy(s12[:, t, :], ps_s[par][:, 0:2 * heads]).then_inc(values_out, 1)

                dve.wait_ge(w_loaded, 32)
                for s in range(2):
                    if s:
                        dve.wait_ge(wa_ready, s)
                    nc.vector.tensor_tensor(wa_terms, w[:], a12[:, s:s + 1, :].broadcast_to([P, KT, D]),
                                            ALU.mult).then_inc(wa_step, 1)
                    dve.wait_ge(wa_step, s + 1)
                    nc.vector.tensor_reduce(wa[:, :, s * heads:(s + 1) * heads],
                                            wa_terms.rearrange("p k (h d) -> p k h d", h=heads),
                                            AX_X, ALU.add).then_inc(wa_ready, 1)
                dve.sem_inc(values_out, 2)
                staged_tiles(dve, (0, stats), (2, out))
                dve.wait_ge(values_out, T + 2)
                nc.vector.tensor_scalar(clipped[:, :, 0, :], s12[:, :, 0:heads], 0.0, None, ALU.min)
                nc.vector.tensor_scalar(clipped[:, :, 1, :], s12[:, :, 0:heads], 0.0, None,
                                        ALU.max).then_inc(clip_ready, 1)
                dve.wait_ge(exps_ready, 1)
                nc.vector.tensor_scalar(row_exps[:, :, 1, :], row_exps[:, :, 1, :], -1.0, None,
                                        ALU.mult).then_inc(exps_ready, 1)
                if has_neighbour is not None:
                    dve.wait_ge(exps_ready, 2)
                    nc.vector.tensor_tensor(row_exps[:], row_exps[:], has_neighbour[:].unsqueeze(2).unsqueeze(3)
                                            .broadcast_to([P, T, 2, heads]), ALU.mult)

            @block.tensor
            def _(pe):
                def turn(t, pair, par):
                    pe.wait_ge(h_ready, t + 1)
                    for k in range(KT):
                        mm = nc.tensor.transpose(ps_t[par][:, k, :], h[par][:, k * P:(k + 1) * P],
                                                 consts["ident"][:])
                    mm.then_inc(h_transposed, 1)

                def project(t, pair, par):
                    pe.wait_ge(ht_ready, t + 1)
                    pe.wait_ge(values_out, t + 1)
                    for k in range(KT):
                        nc.tensor.matmul(ps_v[par][:], ht[par][:, k, :], w[:, k, :],
                                         start=(k == 0), stop=(k == KT - 1))
                    for k in range(KT):
                        mm = nc.tensor.matmul(ps_s[par][:, 0:2 * heads], ht[par][:, k, :], wa[:, k, :],
                                              start=(k == 0), stop=(k == KT - 1))
                    mm.then_inc(projected, 1)

                def score_rows(t, pair, par):
                    pe.wait_ge(tile_scores, t + 1)
                    if later(t):
                        pe.wait_ge(rows_out, t - 1)
                    nc.tensor.transpose(ps_r[par][0:2 * heads, 0:P], s12_tile[par][:],
                                        consts["ident"][:]).then_inc(rows_turned, 1)

                pe.wait_ge(w_loaded, 32)
                pe.wait_ge(wa_ready, 2)
                staged_tiles(pe, (0, turn), (1, project), (2, score_rows))
    return m.sems



def build_lonely_rows(nc, consts, adj_t, adj_loaded, lonely, stats, spare, done_with):
    CH = 512
    with ExitStack() as stack:
        m = Mem(nc, stack, "lonely")
        ps_deg = m.ps("ps_deg", [P, N // CH, CH])
        counted = m.sem("counted")
        flagged = m.sem("flagged")
        column_step = m.sem("column_step")
        picked = spare[:, 0:N].rearrange("p (t c) -> p t c", t=T)
        with nc.Block() as block:

            @block.gpsimd
            def _(pool):
                for sem in done_with:
                    pool.sem_clear(sem)

            @block.tensor
            def _(pe):
                pe.wait_ge(adj_loaded, 16 * NB)
                for c in range(N // CH):
                    for j in range(T):
                        mm = nc.tensor.matmul(ps_deg[:, c, :], consts["ones_bf16"][:],
                                              adj_t[:, j, c * CH:(c + 1) * CH],
                                              start=(j == 0), stop=(j == T - 1))
                    mm.then_inc(counted, 1)

            @block.vector
            def _(dve):
                for c in range(N // CH):
                    cols = slice(c * CH, (c + 1) * CH)
                    dve.wait_ge(counted, c + 1)
                    nc.vector.tensor_scalar(lonely[:, cols], ps_deg[:, c, :], 0.0, None,
                                            ALU.is_equal).then_inc(flagged, 1)
                    dve.wait_ge(flagged, c + 1)
                    nc.vector.tensor_tensor(adj_t[:, :, cols], adj_t[:, :, cols],
                                            lonely[:, cols].unsqueeze(1).broadcast_to([P, T, CH]), ALU.add)
                nc.vector.tensor_tensor(picked, lonely[:].rearrange("p (t c) -> p t c", t=T),
                                        consts["ident"][:].unsqueeze(1).broadcast_to([P, T, P]),
                                        ALU.mult).then_inc(column_step, 1)
                dve.wait_ge(column_step, 1)
                nc.vector.tensor_reduce(stats["lonely"][:], picked, AX_X, ALU.add).then_inc(column_step, 1)
                dve.wait_ge(column_step, 2)
                nc.vector.tensor_scalar(stats["has_neighbour"][:], stats["lonely"][:], -1.0, 1.0, ALU.mult,
                                        ALU.add)
                nc.vector.tensor_scalar(stats["lo_has_neighbour"][:], stats["lonely"][:], -1.0 / LO_SCALE,
                                        1.0 / LO_SCALE, ALU.mult, ALU.add)


def build_attention(nc, name, settle, heads, keep, adj_t, s1_dram, ring, wide, hidden, complements, mean_rows=None):
    dh = D // heads
    c1 = dh + 1
    region = 256 if 6 * c1 <= 256 else 512
    IT = 2048 // region
    CW = IT * P
    NCH = N // CW
    EVAC_AT=2
    NEVAC = 6 if mean_rows is None else 8
    with ExitStack() as stack:
        m = Mem(nc, stack, name)
        taken = RING * JB * CW
        left = [wide[:].bitcast(F32)] if wide is not None else []
        other = {}
        for b in complements:
            other[b] = ring[:, taken:taken + JB * CW].rearrange("p (q c) -> p q c", q=JB)
            taken += JB * CW
        if taken < ring.shape[1]:
            left.append(ring[:, taken:].bitcast(F32))

        def small(name, shape):
            size = 1
            for n in shape[1:]:
                size *= n
            left.sort(key=lambda place: place.shape[1])
            fits = [n for n, place in enumerate(left) if place.shape[1] >= size]
            if not fits:
                return m.sb(name, shape)[:]
            place = left.pop(fits[0])
            at = place[:, 0:size]
            if place.shape[1] > size:
                left.append(place[:, size:])
            return at if len(shape) == 2 else at.rearrange(
                "p (i c) -> p i c" if len(shape) == 3 else "p (i s c) -> p i s c",
                **dict(zip("isc" if len(shape) == 4 else "ic", shape[1:])))

        s1_wide = [small(f"s1_wide{p}", [P, CW]) for p in range(2)]
        mask = [ring[:, r * JB * CW:(r + 1) * JB * CW].rearrange("p (q c) -> p q c", q=JB) for r in range(RING)]
        plain = [b for b in range(NB) if b not in complements]
        parts = [m.sb(f"parts{p}", [P, T, 6 * c1], BF16) for p in range(2)]
        minus = [m.sb(f"minus{p}", [P, len(plain) * JB, 3 * c1], BF16) for p in range(2)]

        def minus_b(u, j, n=1):
            if j // JB in complements:
                return parts[u][:, j:j + n, 3 * c1:6 * c1]
            at = plain.index(j // JB) * JB + j % JB
            return minus[u][:, at:at + n, :]

        JV = 4
        weighted = small("weighted", [P, JV, 2, c1])
        rest = small("rest", [P, JV, 2, c1])
        sum_a = small("sum_a", [P, IT, c1])
        sum_b = small("sum_b", [P, IT, c1])
        num_den = small("num_den", [P, IT, c1])
        recip = m.sb("recip", [P, IT, 1])
        ps = [m.ps(f"ps_sums{p}", [P, IT, region]) for p in range(2)]
        s1_loaded = [m.sem(f"s1_loaded{p}") for p in range(2)]
        steps_ready = m.sem("steps_ready")
        mask_made = m.sem("mask_made")
        other_made = m.sem("other_made")
        masks_used = m.sem("masks_used")
        parts_step = m.sem("parts_step")
        parts_ready = m.sem("parts_ready")
        psum_free = m.sem("psum_free")
        evac_step = m.sem("evac_step")
        values, exp_s2, step_bias, row_exps = keep["values"], keep["exp_s2"], keep["step_bias"], keep["row_exps"]
        HC = 2 * NCH

        def head_pairs(eng, body):
            body(0, True)
            with eng.Fori(1, heads // 2) as pair:
                body(pair, False)

        with nc.Block() as block:

            @block.sync
            def _(sp):
                def body(pair, first):
                    for k in range(HC):
                        g = pair * HC + k
                        head, c = 2 * pair + k // NCH, k % NCH
                        if not first or k >= 2:
                            sp.wait_ge(steps_ready, NB * (g - 1))
                        sp.dma_start(s1_wide[k % 2][:],
                                     s1_dram[bass.ds(head, 1), c * CW:(c + 1) * CW].broadcast_to([P, CW])
                                     ).then_inc(s1_loaded[k % 2], 16)
                head_pairs(sp, body)

            @block.gpsimd
            def _(pool):
                NP = 5 * (T // JV)

                def body(pair, first):
                    for u in range(2):
                        head = 2 * pair + u
                        if not first:
                            pool.wait_ge(masks_used, NB * NCH * (head - 1))
                        for v in range(T // JV):
                            js = slice(v * JV, (v + 1) * JV)
                            base = NP * head + 5 * v

                            def part(n):
                                return parts[u][:, js, :].rearrange("p j (s n c) -> p j s n c", s=2, n=3)[:, :, :, n, :]

                            if not first or u or v:
                                pool.wait_ge(parts_step, base)
                                settle(pool)
                            nc.gpsimd.tensor_tensor(
                                weighted[:],
                                values[:, js, head, :].unsqueeze(2).broadcast_to([P, JV, 2, c1]),
                                exp_s2[:, js, head, :].unsqueeze(3).broadcast_to([P, JV, 2, c1]),
                                ALU.mult).then_inc(parts_step, 1)
                            pool.wait_ge(parts_step, base + 1)
                            settle(pool)
                            nc.gpsimd.tensor_copy(part(0), weighted[:]).then_inc(parts_step, 1)
                            pool.wait_ge(parts_step, base + 2)
                            nc.gpsimd.tensor_tensor(rest[:], weighted[:], part(0), ALU.subtract).then_inc(parts_step, 1)
                            pool.wait_ge(parts_step, base + 3)
                            settle(pool)
                            nc.gpsimd.tensor_copy(part(1), rest[:]).then_inc(parts_step, 1)
                            pool.wait_ge(parts_step, base + 4)
                            nc.gpsimd.tensor_tensor(part(2), rest[:], part(1), ALU.subtract).then_inc(parts_step, 1)
                            pool.wait_ge(parts_step, base + 5)
                            settle(pool)
                            nc.gpsimd.tensor_scalar(minus_b(u, v * JV, JV), parts[u][:, js, 3 * c1:6 * c1],
                                                    -1.0, 1.0, ALU.mult, ALU.mult).then_inc(parts_ready, 1)
                head_pairs(pool, body)

            @block.scalar
            def _(act):
                def body(pair, first):
                    for k in range(HC):
                        head = 2 * pair + k // NCH
                        g = pair * HC + k
                        act.wait_ge(s1_loaded[k % 2], 16 * (pair * NCH + k // 2 + 1))
                        settle(act)
                        for b in range(NB):
                            if not first or k >= 1:
                                act.wait_ge(masks_used, NB * (g - 1) + b + 1)
                                settle(act)
                            for q in range(JB):
                                j = b * JB + q
                                op = nc.scalar.activation(mask[b][:, q, :], s1_wide[k % 2][:], ACT.Relu,
                                                          bias=step_bias[:, j, bass.ds(head, 1)],
                                                          scale=STEP_SCALE)
                            op.then_inc(steps_ready, 1)
                head_pairs(act, body)

            @block.vector
            def _(dve):
                def make_masks(pair, k, b):
                    c = k % NCH
                    g = pair * HC + k
                    dve.wait_ge(steps_ready, NB * g + b + 1)
                    adj_part = adj_t[:, b * JB:(b + 1) * JB, c * CW:(c + 1) * CW]
                    nc.vector.tensor_tensor(mask[b], mask[b],
                                            adj_part, ALU.min).then_inc(mask_made, 1)

                def make_other(pair, k, b):
                    c = k % NCH
                    g = pair * HC + k
                    dve.wait_ge(mask_made, NB * g + b + 1)
                    nc.vector.tensor_tensor(other[b], adj_t[:, b * JB:(b + 1) * JB, c * CW:(c + 1) * CW],
                                            mask[b], ALU.subtract).then_inc(other_made, 1)

                def evacuate(pair, k):
                    c = k % NCH
                    head = 2 * pair + k // NCH
                    g = pair * HC + k
                    its = slice(c * IT, (c + 1) * IT)
                    base = NEVAC * g
                    done = [0]

                    def link(op):
                        op.then_inc(evac_step, 1)
                        done[0] += 1
                        return base + done[0]

                    wide = [P, IT, c1]
                    if not isinstance(base, int) or base > 0:
                        dve.wait_ge(evac_step, base)
                    dve.wait_ge(masks_used, NB * (g + 1))
                    sums = ps[k % 2][:, :, 0:6 * c1].rearrange("p i (s n c) -> p i s c n", s=2, n=3)
                    link(nc.vector.tensor_reduce(sum_a[:], sums[:, :, 0], AX_X, ALU.add))
                    op = nc.vector.tensor_reduce(sum_b[:], sums[:, :, 1], AX_X, ALU.add)
                    op.then_inc(psum_free, 1)
                    dve.wait_ge(evac_step, base + 1)
                    link(nc.vector.tensor_tensor(sum_a[:], sum_a[:],
                                                 row_exps[:, its, 0, bass.ds(head, 1)].broadcast_to(wide), ALU.mult))
                    dve.wait_ge(psum_free, g + 3)
                    at = link(nc.vector.tensor_tensor(sum_b[:], sum_b[:],
                                                      row_exps[:, its, 1, bass.ds(head, 1)].broadcast_to(wide), ALU.mult))
                    dve.wait_ge(evac_step, at)
                    at = link(nc.vector.tensor_tensor(num_den[:], sum_a[:], sum_b[:], ALU.add))
                    if mean_rows is not None:
                        lonely_col, all_rows = mean_rows
                        dve.wait_ge(evac_step, at)
                        link(nc.vector.tensor_tensor(sum_a[:], lonely_col[:, its].unsqueeze(2).broadcast_to(wide),
                                                     all_rows[:, bass.ds(head, 1), :].broadcast_to(wide), ALU.mult))
                        dve.wait_ge(evac_step, at + 1)
                        at = link(nc.vector.tensor_tensor(num_den[:], num_den[:], sum_a[:], ALU.add))
                    dve.wait_ge(evac_step, at)
                    at = link(nc.vector.reciprocal(recip[:], num_den[:, :, dh:dh + 1]))
                    dve.wait_ge(evac_step, at)
                    at = link(nc.vector.tensor_tensor(hidden[:, its, bass.ds(head * dh, dh)], num_den[:, :, 0:dh],
                                                      recip[:].broadcast_to([P, IT, dh]), ALU.mult))
                    assert done[0] == NEVAC

                def body(pair, first):
                    for k in range(HC):
                        for b in range(NB):
                            make_masks(pair, k, b)
                            if b in other:
                                make_other(pair, k, b)
                            if b == EVAC_AT and k >= 1:
                                evacuate(pair, k - 1)
                            if b == EVAC_AT and k == 0 and not first:
                                evacuate(pair - 1, HC - 1)

                dve.sem_inc(psum_free, 2)
                head_pairs(dve, body)
                evacuate(heads // 2 - 1, HC - 1)

            @block.tensor
            def _(pe):
                def body(pair, first):
                    for k in range(HC):
                        g = pair * HC + k
                        c, u = k % NCH, k // NCH
                        pe.wait_ge(psum_free, g + 1)
                        for b in range(NB):
                            if c == 0:
                                pe.wait_ge(parts_ready, NB * (2 * pair + u) + b + 1)
                            pe.wait_ge(mask_made, NB * g + b + 1)
                            if b in other:
                                pe.wait_ge(other_made, len(other) * g + complements.index(b) + 1)
                            for it in range(IT):
                                opens_bank = b == 0 and it * region % 512 == 0
                                for q in range(JB):
                                    j = b * JB + q
                                    out = ps[k % 2][:, it, :]
                                    width = 3 * c1 if b in other else 6 * c1
                                    nc.tensor.matmul(out[:, 0:width], mask[b][:, q, it * P:(it + 1) * P],
                                                     parts[u][:, j, 0:width],
                                                     start=(opens_bank and q == 0), stop=(j == T - 1),
                                                     skip_group_check=True)
                                    rest_of = other[b][:, q, it * P:(it + 1) * P] if b in other else \
                                        adj_t[:, j, c * CW + it * P:c * CW + (it + 1) * P]
                                    mm = nc.tensor.matmul(out[:, 3 * c1:6 * c1], rest_of,
                                                          minus_b(u, j)[:, 0, :],
                                                          start=False, stop=(j == T - 1), skip_group_check=True)
                            mm.then_inc(masks_used, 1)
                with pe.Fori(0, heads // 2) as pair:
                    body(pair, False)


class Split:

    def __init__(self, nc, m, parts, settle):
        self.nc, self.parts, self.settle = nc, parts, settle
        self.rest = [m.sb(f"split_rest{p}", [P, D]) for p in range(2)]
        self.hi_done = m.sem("split_hi_done")
        self.rest_ready = m.sem("split_rest_ready")
        self.done = m.sem("split_done")

    def pool(self, pool, h, t, par):
        pool.wait_ge(self.hi_done, t + 1)
        if later(t):
            pool.wait_ge(self.done, t - 1)
        self.settle(pool)
        self.nc.gpsimd.tensor_tensor(self.rest[par][:], h, self.parts[:, t, 0, :], ALU.subtract)\
            .then_inc(self.rest_ready, 1)

    def scalar(self, act, t, par):
        act.wait_ge(self.rest_ready, t + 1)
        self.nc.scalar.mul(self.parts[:, t, 1, :], self.rest[par][:], LO_SCALE).then_inc(self.done, 1)


def build_attention_out(nc, consts, x_src, x_dst, hidden, w_dram, b_dram, h_parts):
    with ExitStack() as stack:
        m = Mem(nc, stack, "out0")
        w = m.sb("w", [P, KT, D])
        bias = m.sb("bias", [P, D])
        x = [m.sb(f"x{p}", [P, D]) for p in range(2)]
        g = [m.sb(f"g{p}", [P, D]) for p in range(2)]
        gt = [m.sb(f"gt{p}", [P, KT, P]) for p in range(2)]
        y = [m.sb(f"y{p}", [P, D]) for p in range(2)]
        low = [m.sb(f"low{p}", [P, D]) for p in range(2)]
        x1 = [m.sb(f"x1{p}", [P, D]) for p in range(2)]
        h = [m.sb(f"h{p}", [P, D]) for p in range(2)]
        ps_t = [m.ps(f"ps_t{p}", [P, KT, P]) for p in range(2)]
        ps_y = [m.ps(f"ps_y{p}", [P, D]) for p in range(2)]
        ln = LayerNorm(nc, m, consts)
        split = Split(nc, m, h_parts, consts["settle"])
        w_loaded = m.sem("w_loaded")
        x_loaded = [m.sem(f"x_loaded{p}") for p in range(2)]
        x1_stored = [m.sem(f"x1_stored{p}") for p in range(2)]
        g_ready = m.sem("g_ready")
        turned = m.sem("turned")
        gt_ready = m.sem("gt_ready")
        projected = m.sem("projected")
        y_ready = m.sem("y_ready")
        low_ready = m.sem("low_ready")
        exp_ready = m.sem("exp_ready")
        x_added = m.sem("x_added")
        x1_ready = m.sem("x1_ready")
        with nc.Block() as block:

            @block.sync
            def _(sp):
                sp.dma_start(w[:], w_dram.rearrange("(k p) n -> p k n", p=P)).then_inc(w_loaded, 16)
                sp.dma_start(bias[:], b_dram.unsqueeze(0).broadcast_to([P, D])).then_inc(w_loaded, 16)
                load_tiles(sp, rows(x_src), x, x_loaded, x_added)

            @block.gpsimd
            def _(pool):
                def pick(t, pair, par):
                    if later(t):
                        pool.wait_ge(turned, t - 1)
                    consts["settle"](pool)
                    nc.gpsimd.tensor_copy(g[par][:], hidden[:, t, :]).then_inc(g_ready, 1)

                def store(t, pair, par):
                    pool.wait_ge(x1_ready, t + 1)
                    pool.dma_start(rows(x_dst)[t], x1[par][:]).then_inc(x1_stored[par], 16)

                staged_tiles(pool, (0, pick), (3, lambda t, pair, par: ln.pool(pool, t, par)), (3, store),
                             (4, lambda t, pair, par: split.pool(pool, h[par][:], t, par)))
                for par in range(2):
                    pool.wait_ge(x1_stored[par], 16 * (T // 2))

            @block.tensor
            def _(pe):
                def turn(t, pair, par):
                    pe.wait_ge(g_ready, t + 1)
                    for k in range(KT):
                        mm = nc.tensor.transpose(ps_t[par][:, k, :], g[par][:, k * P:(k + 1) * P],
                                                 consts["ident"][:])
                    mm.then_inc(turned, 1)

                def project(t, pair, par):
                    pe.wait_ge(gt_ready, t + 1)
                    if later(t):
                        pe.wait_ge(y_ready, t - 1)
                    for k in range(KT):
                        mm = nc.tensor.matmul(ps_y[par][:], gt[par][:, k, :], w[:, k, :],
                                              start=(k == 0), stop=(k == KT - 1))
                    mm.then_inc(projected, 1)

                pe.wait_ge(w_loaded, 32)
                staged_tiles(pe, (0, turn), (1, project))

            @block.scalar
            def _(act):
                def turned_out(t, pair, par):
                    act.wait_ge(turned, t + 1)
                    nc.scalar.copy(gt[par][:], ps_t[par][:]).then_inc(gt_ready, 1)

                def exp_low(t, pair, par):
                    act.wait_ge(low_ready, t + 1)
                    nc.scalar.activation(low[par][:], low[par][:], ACT.Exp).then_inc(exp_ready, 1)

                def normed(t, pair, par):
                    if later(t):
                        act.wait_ge(split.rest_ready, t - 1)
                    ln.scalar(act, h[par][:], x1[par][:], t, par)
                    consts["settle"](act)
                    ln.scalar(act, h_parts[:, t, 0, :], x1[par][:], t, par).then_inc(split.hi_done, 1)

                staged_tiles(act, (3, normed), (4, lambda t, pair, par: split.scalar(act, t, par)),
                             (0, turned_out), (1, exp_low))

            @block.vector
            def _(dve):
                def biased(t, pair, par):
                    dve.wait_ge(projected, t + 1)
                    nc.vector.tensor_tensor(y[par][:], ps_y[par][:], bias[:], ALU.add).then_inc(y_ready, 1)

                def lower(t, pair, par):
                    dve.wait_ge(y_ready, t + 1)
                    nc.vector.tensor_scalar(low[par][:], y[par][:], 0.0, None, ALU.min).then_inc(low_ready, 1)

                def add_x(t, pair, par):
                    dve.wait_ge(x_loaded[par], 16 * (pair + 1))
                    dve.wait_ge(low_ready, t + 1)
                    nc.vector.scalar_tensor_tensor(out=y[par][:], in0=y[par][:], scalar=0.0, in1=x[par][:],
                                                   op0=ALU.max, op1=ALU.add).then_inc(x_added, 1)

                def residual(t, pair, par):
                    dve.wait_ge(exp_ready, t + 1)
                    dve.wait_ge(x_added, t + 1)
                    if later(t):
                        dve.wait_ge(x1_stored[par], 16 * pair)
                        dve.wait_ge(split.hi_done, t - 1)
                    nc.vector.scalar_tensor_tensor(out=x1[par][:], in0=low[par][:], scalar=-1.0, in1=y[par][:],
                                                   op0=ALU.add, op1=ALU.add).then_inc(x1_ready, 1)

                def stats_of(t, pair, par):
                    dve.wait_ge(x1_ready, t + 1)
                    ln.vector_stats(dve, x1[par][:], t, par)

                def moments(t, pair, par):
                    ln.vector_moments(dve, t, par)

                dve.wait_ge(w_loaded, 32)
                staged_tiles(dve, (0, biased), (1, residual), (0, lower), (1, stats_of), (0, add_x), (1, moments))


class AdjacencyProduct:

    def __init__(self, nc, m, matrix, parts):
        self.nc, self.matrix, self.parts = nc, matrix, parts
        self.hi = [m.ps(f"prod_hi{p}", [P, D]) for p in range(2)]
        self.lo = [m.ps(f"prod_lo{p}", [P, D]) for p in range(2)]
        self.lo_scaled = [m.sb(f"prod_lo_scaled{p}", [P, D]) for p in range(2)]
        self.summed = m.sem("prod_summed")
        self.lo_ready = m.sem("prod_lo_ready")
        self.joined = m.sem("prod_joined")

    def tensor(self, pe, t, par, js):
        if js[0] == 0 and later(t):
            pe.wait_ge(self.joined, t - 1)
            pe.wait_ge(self.lo_ready, t - 1)
        for j in js:
            for n, out in ((0, self.hi), (1, self.lo)):
                mm = self.nc.tensor.matmul(out[par][:], self.matrix[:, j, bass.ts(t, P)], self.parts[:, j, n, :],
                                           start=(j == 0), stop=(j == T - 1))
        if js[-1] == T - 1:
            mm.then_inc(self.summed, 1)

    def scalar(self, act, t, par, scale=1.0 / LO_SCALE):
        act.wait_ge(self.summed, t + 1)
        if later(t):
            act.wait_ge(self.joined, t - 1)
        if isinstance(scale, float):
            op = self.nc.scalar.mul(self.lo_scaled[par][:], self.lo[par][:], scale)
        else:
            op = self.nc.scalar.activation(self.lo_scaled[par][:], self.lo[par][:], ACT.Copy, scale=scale)
        op.then_inc(self.lo_ready, 1)

    def vector(self, dve, out, t, par, scale=1.0):
        dve.wait_ge(self.lo_ready, t + 1)
        return self.nc.vector.scalar_tensor_tensor(out=out, in0=self.hi[par][:], scalar=scale,
                                                   in1=self.lo_scaled[par][:], op0=ALU.mult,
                                                   op1=ALU.add).then_inc(self.joined, 1)


def build_linear_layer(nc, consts, x_src, x_dst, wt_dram, b_dram, adj_dram, adj_t, h_parts, sym, stats, lonely_wide):
    with ExitStack() as stack:
        m = Mem(nc, stack, "lin")
        w = m.sb("w", [P, KT, D])
        bias = m.sb("bias", [P, D])
        x = [m.sb(f"x{p}", [P, D]) for p in range(2)]
        agg = [m.sb(f"agg{p}", [P, D]) for p in range(2)]
        aggt = [m.sb(f"aggt{p}", [P, KT, P]) for p in range(2)]
        y = [m.sb("y", [P, D])] * 2
        x2 = [m.sb(f"x2{p}", [P, D]) for p in range(2)]
        adj_rows = m.sb("adj_rows", [P, N])
        ps_t = [m.ps(f"ps_t{p}", [P, KT, P]) for p in range(2)]
        ps_y = [m.ps(f"ps_y{p}", [P, D]) for p in range(2)]
        prod = AdjacencyProduct(nc, m, adj_t, h_parts)
        w_loaded = m.sem("w_loaded")
        x_loaded = [m.sem(f"x_loaded{p}") for p in range(2)]
        x2_stored = [m.sem(f"x2_stored{p}") for p in range(2)]
        adj_loaded = m.sem("adj_loaded")
        true_columns = m.sem("true_columns")
        sym_ready = m.sem("sym_ready")
        turned = m.sem("turned")
        aggt_ready = m.sem("aggt_ready")
        projected = m.sem("projected")
        y_ready = m.sem("y_ready")
        x2_ready = m.sem("x2_ready")
        deg_step = m.sem("deg_step")
        with nc.Block() as block:

            @block.sync
            def _(sp):
                sp.dma_start(w[:], wt_dram.rearrange("(k p) n -> p k n", p=P)).then_inc(w_loaded, 16)
                sp.dma_start(bias[:], b_dram.unsqueeze(0).broadcast_to([P, D])).then_inc(w_loaded, 16)
                load_tiles(sp, rows(x_src), x, x_loaded, x2_ready)

            @block.gpsimd
            def _(pool):
                def fetch(t, pair, par):
                    if later(t, 0):
                        pool.wait_ge(sym_ready, t)
                    pool.dma_start(adj_rows[:], rows(adj_dram)[t]).then_inc(adj_loaded, 16)

                def store(t, pair, par):
                    pool.wait_ge(x2_ready, t + 1)
                    pool.dma_start(rows(x_dst)[t], x2[par][:]).then_inc(x2_stored[par], 16)

                staged_tiles(pool, (0, fetch), (2, store))
                for par in range(2):
                    pool.wait_ge(x2_stored[par], 16 * (T // 2))
                pool.wait_ge(deg_step, 1)
                nc.gpsimd.tensor_tensor(stats["dinv"][:], stats["deg"][:],
                                        consts["neg_half"][:, 0:1].broadcast_to([P, T]), ALU.pow)\
                    .then_inc(deg_step, 1)

            @block.tensor
            def _(pe):
                def turn(t, pair, par):
                    pe.wait_ge(prod.joined, t + 1)
                    for k in range(KT):
                        mm = nc.tensor.transpose(ps_t[par][:, k, :], agg[par][:, k * P:(k + 1) * P],
                                                 consts["ident"][:])
                    mm.then_inc(turned, 1)

                def project(t, pair, par):
                    pe.wait_ge(aggt_ready, t + 1)
                    if later(t):
                        pe.wait_ge(y_ready, t - 1)
                    for k in range(KT):
                        mm = nc.tensor.matmul(ps_y[par][:], aggt[par][:, k, :], w[:, k, :],
                                              start=(k == 0), stop=(k == KT - 1))
                    mm.then_inc(projected, 1)

                pe.wait_ge(w_loaded, 32)
                staged_tiles(pe, (0, lambda t, pair, par: prod.tensor(pe, t, par, range(0, T // 2))), (1, turn),
                             (0, lambda t, pair, par: prod.tensor(pe, t, par, range(T // 2, T))), (1, project))

            @block.scalar
            def _(act):
                def turned_out(t, pair, par):
                    act.wait_ge(turned, t + 1)
                    nc.scalar.copy(aggt[par][:], ps_t[par][:]).then_inc(aggt_ready, 1)

                def low(t, pair, par):
                    prod.scalar(act, t, par, col(stats["lo_has_neighbour"], t))

                staged_tiles(act, (1, turned_out), (0, low))

            @block.vector
            def _(dve):
                def join(t, pair, par):
                    if later(t):
                        dve.wait_ge(turned, t - 1)
                    prod.vector(dve, agg[par][:], t, par, col(stats["has_neighbour"], t))

                def out(t, pair, par):
                    dve.wait_ge(projected, t + 1)
                    if later(t, 0):
                        dve.wait_ge(x2_ready, t)
                    nc.vector.tensor_tensor(y[par][:], ps_y[par][:], bias[:], ALU.add).then_inc(y_ready, 1)
                    dve.wait_ge(y_ready, t + 1)
                    dve.wait_ge(x_loaded[par], 16 * (pair + 1))
                    if later(t):
                        dve.wait_ge(x2_stored[par], 16 * pair)
                    nc.vector.scalar_tensor_tensor(out=x2[par][:], in0=y[par][:], scalar=0.0, in1=x[par][:],
                                                   op0=ALU.max, op1=ALU.add).then_inc(x2_ready, 1)

                def symmetric(t, pair, par):
                    nc.vector.tensor_tensor(sym[:, t, :], adj_t[:, t, :], lonely_wide[:],
                                            ALU.subtract).then_inc(true_columns, 1)
                    dve.wait_ge(true_columns, t + 1)
                    dve.wait_ge(adj_loaded, 16 * (t + 1))
                    nc.vector.scalar_tensor_tensor(out=sym[:, t, :], in0=adj_rows[:], scalar=1.0,
                                                   in1=sym[:, t, :], op0=ALU.mult, op1=ALU.add,
                                                   accum_out=col(stats["deg2"], t)).then_inc(sym_ready, 1)
                    dve.wait_ge(sym_ready, t + 1)
                    diag = sym[:, t, bass.ts(t, P)]
                    nc.vector.scalar_tensor_tensor(out=diag, in0=consts["ident"][:], scalar=2.0, in1=diag,
                                                   op0=ALU.mult, op1=ALU.add)

                dve.wait_ge(w_loaded, 32)
                staged_tiles(dve, (0, symmetric), (0, join), (1, out))
                dve.wait_ge(sym_ready, T)
                nc.vector.tensor_scalar(stats["deg"][:], stats["deg2"][:], 0.5, 1.0, ALU.mult,
                                        ALU.add).then_inc(deg_step, 1)
                dve.wait_ge(deg_step, 2)
                nc.vector.tensor_scalar(stats["half_dinv"][:], stats["dinv"][:], 0.5, None, ALU.mult)
                nc.vector.tensor_scalar(stats["lo_half_dinv"][:], stats["dinv"][:], 0.5 / LO_SCALE, None, ALU.mult)


def build_scaled_rows(nc, consts, x_src, g_parts, stats):
    XB = 4
    with ExitStack() as stack:
        m = Mem(nc, stack, "scaled")
        x = m.sb("x", [P, T, D])
        h = [m.sb(f"h{p}", [P, D]) for p in range(2)]
        ln = LayerNorm(nc, m, consts, stats["dinv"])
        split = Split(nc, m, g_parts, consts["settle"])
        x_loaded = m.sem("x_loaded")
        with nc.Block() as block:

            @block.sync
            def _(sp):
                for b in range(T // XB):
                    tiles = slice(b * XB, (b + 1) * XB)
                    sp.dma_start(x[:, tiles, :], rows(x_src)[tiles].rearrange("t p d -> p t d"))\
                        .then_inc(x_loaded, 16)
                    sp.wait_ge(x_loaded, 16 * (b + 1))

            @block.gpsimd
            def _(pool):
                staged_tiles(pool, (0, lambda t, pair, par: ln.pool(pool, t, par)),
                             (2, lambda t, pair, par: split.pool(pool, h[par][:], t, par)))

            @block.scalar
            def _(act):
                def normed(t, pair, par):
                    if later(t):
                        act.wait_ge(split.rest_ready, t - 1)
                    act.wait_ge(ln.coefs_ready, t + 1)
                    consts["settle"](act)
                    ln.scalar(act, h[par][:], x[:, t, :], t, par)
                    ln.scalar(act, g_parts[:, t, 0, :], x[:, t, :], t, par).then_inc(split.hi_done, 1)

                staged_tiles(act, (0, normed), (2, lambda t, pair, par: split.scalar(act, t, par)))

            @block.vector
            def _(dve):
                def stats_of(t, pair, par):
                    if later(t):
                        dve.wait_ge(split.hi_done, t - 1)
                    dve.wait_ge(x_loaded, 16 * T // XB)
                    ln.vector(dve, x[:, t, :], t, par)

                staged_tiles(dve, (0, stats_of))


def build_normalised_product(nc, consts, sym, g_parts, z_parts, stats):
    with ExitStack() as stack:
        m = Mem(nc, stack, "norm")
        z = m.sb("z", [P, D])
        prod = AdjacencyProduct(nc, m, sym, g_parts)
        split_rest = m.sb("rest", [P, D])
        hi_done = m.sem("hi_done")
        rest_ready = m.sem("rest_ready")
        lo_done = m.sem("lo_done")
        with nc.Block() as block:

            @block.tensor
            def _(pe):
                staged_tiles(pe, (0, lambda t, pair, par: prod.tensor(pe, t, par, range(T))))

            @block.scalar
            def _(act):
                def low(t, pair, par):
                    prod.scalar(act, t, par, col(stats["lo_half_dinv"], t))

                def lo_part(t, pair, par):
                    act.wait_ge(rest_ready, t + 1)
                    nc.scalar.mul(z_parts[:, t, 1, :], split_rest[:], LO_SCALE).then_inc(lo_done, 1)

                staged_tiles(act, (0, low), (0, lo_part))

            @block.vector
            def _(dve):
                def join(t, pair, par):
                    if later(t, 0):
                        dve.wait_ge(rest_ready, t)
                    prod.vector(dve, z[:], t, par, col(stats["half_dinv"], t))
                    dve.wait_ge(prod.joined, t + 1)
                    nc.vector.tensor_copy(z_parts[:, t, 0, :], z[:]).then_inc(hi_done, 1)
                    dve.wait_ge(hi_done, t + 1)
                    if later(t, 0):
                        dve.wait_ge(lo_done, t)
                    nc.vector.tensor_tensor(split_rest[:], z[:], z_parts[:, t, 0, :],
                                            ALU.subtract).then_inc(rest_ready, 1)

                staged_tiles(dve, (0, join))


def build_second_product(nc, x_src, x_dst, adj_t, z_parts, spare, stats):
    with ExitStack() as stack:
        m = Mem(nc, stack, "second")
        x = [spare[:, p * D:(p + 1) * D] for p in range(2)]
        y = [m.sb("y", [P, D])] * 2
        x3 = [spare[:, (2 + p) * D:(3 + p) * D] for p in range(2)]
        prod = AdjacencyProduct(nc, m, adj_t, z_parts)
        x_loaded = [m.sem(f"x_loaded{p}") for p in range(2)]
        x3_stored = [m.sem(f"x3_stored{p}") for p in range(2)]
        x3_ready = m.sem("x3_ready")
        with nc.Block() as block:

            @block.sync
            def _(sp):
                load_tiles(sp, rows(x_src), x, x_loaded, x3_ready)

            @block.gpsimd
            def _(pool):
                def store(t, pair, par):
                    pool.wait_ge(x3_ready, t + 1)
                    pool.dma_start(rows(x_dst)[t], x3[par][:]).then_inc(x3_stored[par], 16)

                staged_tiles(pool, (0, store))
                for par in range(2):
                    pool.wait_ge(x3_stored[par], 16 * (T // 2))

            @block.tensor
            def _(pe):
                staged_tiles(pe, (0, lambda t, pair, par: prod.tensor(pe, t, par, range(T))))

            @block.scalar
            def _(act):
                staged_tiles(act, (0, lambda t, pair, par: prod.scalar(act, t, par, col(stats["lo_has_neighbour"], t))))

            @block.vector
            def _(dve):
                def residual(t, pair, par):
                    if later(t, 0):
                        dve.wait_ge(x3_ready, t)
                    prod.vector(dve, y[par][:], t, par, col(stats["has_neighbour"], t))
                    dve.wait_ge(prod.joined, t + 1)
                    dve.wait_ge(x_loaded[par], 16 * (pair + 1))
                    if later(t):
                        dve.wait_ge(x3_stored[par], 16 * pair)
                    nc.vector.tensor_tensor(x3[par][:], y[par][:], x[par][:], ALU.add).then_inc(x3_ready, 1)

                staged_tiles(dve, (0, residual))


def build_value_sums(nc, heads, value_sum, all_rows):
    half = heads // 2
    with ExitStack() as stack:
        m = Mem(nc, stack, "sums")
        width = half * value_sum.shape[2]
        ones = m.sb("ones", [P, P])
        ps = [m.ps(f"ps{p}", [P, 512]) for p in range(2)]
        ones_set = m.sem("ones_set")
        summed = m.sem("summed")
        with nc.Block() as block:

            @block.tensor
            def _(pe):
                pe.wait_ge(ones_set, 1)
                for s in range(2):
                    nc.tensor.matmul(ps[s][:, 0:width], ones[:],
                                     value_sum[:, s * half:(s + 1) * half, :].rearrange("p h c -> p (h c)"),
                                     start=True, stop=True).then_inc(summed, 1)

            @block.vector
            def _(dve):
                nc.vector.memset(ones[:], 1.0).then_inc(ones_set, 1)
                dve.wait_ge(summed, 2)
                for s in range(2):
                    nc.vector.tensor_copy(all_rows[:, s * half:(s + 1) * half, :].rearrange("p h c -> p (h c)"),
                                          ps[s][:, 0:width])


def build_perceptron(nc, consts, x_src, out, hidden, layers):
    (w1_dram, b1_dram), (w2_dram, b2_dram), (w3_dram, b3_dram), (w4_dram, b4_dram) = layers
    with ExitStack() as stack:
        m = Mem(nc, stack, "mlp")
        M1, M2, M3 = (w1_dram.shape[1] // P, w2_dram.shape[1] // P, w3_dram.shape[1] // P)
        w1 = m.sb("w1", [P, KT, M1 * P])
        w2 = m.sb("w2", [P, M1, M2 * P])
        w3 = m.sb("w3", [P, M2, M3 * P])
        w4 = m.sb("w4", [P, M3, D])
        b1 = m.sb("b1", [P, M1])
        b2 = m.sb("b2", [P, M2])
        b3 = m.sb("b3", [P, M3])
        b4 = m.sb("b4", [P, D])
        x = [m.sb(f"x{p}", [P, D]) for p in range(2)]
        low = [m.sb(f"low{p}", [P, D]) for p in range(2)]
        high = [m.sb(f"high{p}", [P, D]) for p in range(2)]
        enc = [m.sb(f"enc{p}", [P, D]) for p in range(2)]
        enct = [m.sb(f"enct{p}", [P, KT, P]) for p in range(2)]
        o1 = [m.sb(f"o1{p}", [P, M1, P]) for p in range(2)]
        o2 = [m.sb(f"o2{p}", [P, M2, P]) for p in range(2)]
        o3 = [m.sb(f"o3{p}", [P, M3, P]) for p in range(2)]
        xb = [m.sb(f"xb{p}", [P, D]) for p in range(2)]
        y = [m.sb(f"y{p}", [P, D]) for p in range(2)]
        ps_t = [m.ps(f"ps_t{p}", [P, KT, P]) for p in range(2)]
        ps_1 = [m.ps(f"ps_1{p}", [P, 512]) for p in range(2)]
        ps_2 = m.ps("ps_2", [P, 512])
        ps_3 = m.ps("ps_3", [P, 512])
        ps_4 = [m.ps(f"ps_4{p}", [P, D]) for p in range(2)]
        w_loaded = m.sem("w_loaded")
        x_loaded = [m.sem(f"x_loaded{p}") for p in range(2)]
        stored = [m.sem(f"stored{p}") for p in range(2)]
        low_ready = m.sem("low_ready")
        high_ready = m.sem("high_ready")
        exp_ready = m.sem("exp_ready")
        enc_ready = m.sem("enc_ready")
        turned = m.sem("turned")
        enct_ready = m.sem("enct_ready")
        summed = [m.sem(f"summed{n}") for n in range(1, 5)]
        relu_ready = [m.sem(f"relu_ready{n}") for n in range(1, 4)]
        xb_ready = m.sem("xb_ready")
        y_ready = m.sem("y_ready")

        with nc.Block() as block:

            @block.sync
            def _(sp):
                for w, dram in ((w1, w1_dram), (w2, w2_dram), (w3, w3_dram), (w4, w4_dram)):
                    sp.dma_start(w[:], dram.rearrange("(k p) n -> p k n", p=P)).then_inc(w_loaded, 16)
                for b, dram in ((b1, b1_dram), (b2, b2_dram), (b3, b3_dram)):
                    sp.dma_start(b[:], dram).then_inc(w_loaded, 16)
                sp.dma_start(b4[:], b4_dram.unsqueeze(0).broadcast_to([P, D])).then_inc(w_loaded, 16)
                load_tiles(sp, rows(x_src), x, x_loaded, xb_ready)

            @block.gpsimd
            def _(pool):
                def biased(t, pair, par):
                    pool.wait_ge(x_loaded[par], 16 * (pair + 1))
                    if later(t):
                        pool.wait_ge(y_ready, t - 1)
                    nc.gpsimd.tensor_tensor(xb[par][:], x[par][:], b4[:], ALU.add).then_inc(xb_ready, 1)

                def store(t, pair, par):
                    pool.wait_ge(y_ready, t + 1)
                    pool.dma_start(rows(out)[t], y[par][:]).then_inc(stored[par], 16)

                pool.wait_ge(w_loaded, 16 * 8)
                staged_tiles(pool, (0, biased), (2, store))
                for par in range(2):
                    pool.wait_ge(stored[par], 16 * (T // 2))

            @block.tensor
            def _(pe):
                def turn(t, pair, par):
                    pe.wait_ge(enc_ready, t + 1)
                    for k in range(KT):
                        mm = nc.tensor.transpose(ps_t[par][:, k, :], enc[par][:, k * P:(k + 1) * P],
                                                 consts["ident"][:])
                    mm.then_inc(turned, 1)

                def layer(n, ps, w, src, src_ready, kts, mts, free, lag_free):
                    def emit(t, pair, par):
                        pe.wait_ge(src_ready, t + 1)
                        if later(t, lag_free - 1):
                            pe.wait_ge(free, t + 1 - lag_free)
                        o = ps[par] if isinstance(ps, list) else ps
                        for mt in range(mts):
                            for k in range(kts):
                                mm = nc.tensor.matmul(o[:, mt * P:(mt + 1) * P], w[:, k, mt * P:(mt + 1) * P],
                                                      src[par][:, k, :], start=(k == 0), stop=(k == kts - 1))
                        mm.then_inc(summed[n - 1], 1)
                    return emit

                def last(t, pair, par):
                    pe.wait_ge(relu_ready[2], t + 1)
                    if later(t):
                        pe.wait_ge(y_ready, t - 1)
                    for k in range(M3):
                        mm = nc.tensor.matmul(ps_4[par][:], o3[par][:, k, :], w4[:, k, :],
                                              start=(k == 0), stop=(k == M3 - 1))
                    mm.then_inc(summed[3], 1)

                pe.wait_ge(w_loaded, 16 * 8)
                staged_tiles(pe, (0, turn), (4, last),
                             (3, layer(3, ps_3, w3, o2, relu_ready[1], M2, M3, relu_ready[2], 1)),
                             (2, layer(2, ps_2, w2, o1, relu_ready[0], M1, M2, relu_ready[1], 1)),
                             (1, layer(1, ps_1, w1, enct, enct_ready, KT, M1, relu_ready[0], 2)))

            @block.scalar
            def _(act):
                def exps(t, pair, par):
                    act.wait_ge(low_ready, t + 1)
                    nc.scalar.activation(low[par][:], low[par][:], ACT.Exp).then_inc(exp_ready, 1)

                def turned_out(t, pair, par):
                    act.wait_ge(turned, t + 1)
                    nc.scalar.copy(enct[par][:], ps_t[par][:]).then_inc(enct_ready, 1)

                def relu(n, ps, dst, b, mts):
                    def emit(t, pair, par):
                        act.wait_ge(summed[n - 1], t + 1)
                        o = ps[par] if isinstance(ps, list) else ps
                        for mt in range(mts):
                            op = nc.scalar.activation(dst[par][:, mt, :], o[:, mt * P:(mt + 1) * P], ACT.Relu,
                                                      bias=b[:, mt:mt + 1])
                        op.then_inc(relu_ready[n - 1], 1)
                    return emit

                act.wait_ge(w_loaded, 16 * 8)
                staged_tiles(act, (0, exps), (2, turned_out), (5, relu(3, ps_3, o3, b3, M3)),
                             (4, relu(2, ps_2, o2, b2, M2)), (3, relu(1, ps_1, o1, b1, M1)))

            @block.vector
            def _(dve):
                def parts_of(t, pair, par):
                    if later(t):
                        dve.wait_ge(enc_ready, t - 1)
                    nc.vector.tensor_scalar(low[par][:], hidden[:, t, :], 0.0, None, ALU.min).then_inc(low_ready, 1)
                    nc.vector.tensor_scalar(high[par][:], hidden[:, t, :], 0.0, None, ALU.max).then_inc(high_ready, 1)

                def encode(t, pair, par):
                    dve.wait_ge(exp_ready, t + 1)
                    dve.wait_ge(high_ready, t + 1)
                    if later(t):
                        dve.wait_ge(turned, t - 1)
                    nc.vector.scalar_tensor_tensor(out=enc[par][:], in0=low[par][:], scalar=-1.0, in1=high[par][:],
                                                   op0=ALU.add, op1=ALU.add).then_inc(enc_ready, 1)

                def final(t, pair, par):
                    dve.wait_ge(summed[3], t + 1)
                    dve.wait_ge(xb_ready, t + 1)
                    if later(t):
                        dve.wait_ge(stored[par], 16 * pair)
                    nc.vector.tensor_tensor(y[par][:], ps_4[par][:], xb[par][:], ALU.add).then_inc(y_ready, 1)

                staged_tiles(dve, (0, parts_of), (1, encode), (6, final))


def build(nc, a, out):
    x1 = nc.dram_tensor("after_l0", (N, D), F32, kind="Internal").ap()
    x2 = nc.dram_tensor("after_l1", (N, D), F32, kind="Internal").ap()
    x3 = nc.dram_tensor("after_l2", (N, D), F32, kind="Internal").ap()

    def attention_memory(stack, prefix, heads):
        m = Mem(nc, stack, prefix)
        return {"values": m.sb("values", [P, T, heads, D // heads + 1]),
                "exp_s2": m.sb("exp_s2", [P, T, heads, 2]),
                "step_bias": m.sb("step_bias", [P, T, heads]),
                "row_exps": m.sb("row_exps", [P, T, 2, heads])}

    with ExitStack() as stack:
        m = Mem(nc, stack, "all")
        consts = {"neg_half": m.sb("neg_half", [P, 1]), "ident": m.sb("ident", [P, P]),
                  "ones_bf16": m.sb("ones_bf16", [P, P], BF16)}
        passed = m.sem("wait_passed")
        consts["settle"] = lambda eng: eng.sem_inc(passed, 1)
        stats = {n: m.sb(n, [P, T]) for n in ("deg2", "deg", "dinv", "half_dinv", "lo_half_dinv", "lonely",
                                              "has_neighbour", "lo_has_neighbour")}
        adj_t = m.sb("adj_t", [P, T, N], BF16)
        sym = m.sb("sym_or_hidden", [P, T, N], BF16)
        flat = sym[:].rearrange("p t n -> p (t n)")
        hidden = flat[:, 0:T * N // 2].bitcast(F32).rearrange("p (t d) -> p t d", t=T)
        ring = flat[:, T * N // 2:T * N]
        spare = ring.bitcast(F32)
        adj_loaded = m.sem("adj_t_loaded")

        def load_adj_t(pool):
            for b in range(NB):
                pool.dma_start(adj_t[:, b * JB:(b + 1) * JB, :],
                               a["adj_t"][b * JB * P:(b + 1) * JB * P, :].rearrange("(j p) n -> p j n", p=P))\
                    .then_inc(adj_loaded, 16)

        const_sems = build_constants(nc, consts)
        wide = m.sb("lonely_wide", [P, N], BF16)
        with ExitStack() as att:
            keep = attention_memory(att, "keep0", 16)
            s1 = nc.dram_tensor("s1_rows0", (16, N), F32, kind="Internal").ap()
            done_with = build_projection(nc, "proj0", consts, a["x"], a["w0"], a["a0"], 16, keep, s1, spare, load_adj_t)
            build_lonely_rows(nc, consts, adj_t, adj_loaded, wide, stats, spare, const_sems + done_with)
            build_attention(nc, "att0", consts["settle"], 16, keep, adj_t, s1, ring, None, hidden, [])
        with ExitStack() as layers:
            h_parts = Mem(nc, layers, "gcn").sb("h_parts", [P, T, 2, D], F16)
            build_attention_out(nc, consts, a["x"], x1, hidden, a["w0_out"], a["b0_out"], h_parts)
            build_linear_layer(nc, consts, x1, x2, a["w1_t"], a["b1"], a["adj"], adj_t, h_parts, sym, stats, wide)
            build_scaled_rows(nc, consts, x2, h_parts, stats)
            z_parts = Mem(nc, layers, "gcn2").sb("z_parts", [P, T, 2, D], F16)
            build_normalised_product(nc, consts, sym, h_parts, z_parts, stats)
            build_second_product(nc, x2, x3, adj_t, z_parts, spare, stats)
        with ExitStack() as att:
            keep = attention_memory(att, "keep3", 8)
            all_rows = Mem(nc, att, "gat3").sb("all_rows", [P, 8, D // 8 + 1])
            s1 = nc.dram_tensor("s1_rows3", (8, N), F32, kind="Internal").ap()
            with ExitStack() as sums:
                value_sum = Mem(nc, sums, "gat3_sum").sb("value_sum", [P, 8, D // 8 + 1])
                build_projection(nc, "proj3", consts, x3, a["w3"], a["a3"], 8, keep, s1, spare,
                                 has_neighbour=stats["has_neighbour"], value_sum=value_sum)
                build_value_sums(nc, 8, value_sum, all_rows)
            build_attention(nc, "att3", consts["settle"], 8, keep, adj_t, s1, ring, wide, hidden, [0, 1, 3], (stats["lonely"], all_rows))
        build_perceptron(nc, consts, x3, out, hidden,
                         [(a[f"mlp_w{n}_t"], a[f"mlp_b{n}"]) for n in range(1, 5)])


def kernel(**inputs):
    import numpy as np
    import concourse.bacc as bacc
    from concourse.bass_utils import run_bass_kernel_spmd

    i = {k: np.asarray(v) for k, v in inputs.items()}
    laid = {
        "x": i["x"], "adj": i["adj"], "adj_t": i["adj"].T,
        "w0": i["L0_gnn_W_seq"],
        "a0": np.stack([np.tile(i["L0_gnn_a1"], 16), np.tile(i["L0_gnn_a2"], 16)]),
        "w0_out": i["L0_gnn_W_out"], "b0_out": i["L0_gnn_b_out"],
        "w1_t": i["L1_gnn_W"].T, "b1": i["L1_gnn_b"],
        "w3": i["L3_gnn_W"].transpose(1, 0, 2).reshape(D, D),
        "a3": np.stack([i["L3_gnn_a1"].reshape(D), i["L3_gnn_a2"].reshape(D)]),
    }
    for n in range(1, 5):
        laid[f"mlp_w{n}_t"] = i[f"L3_gnn_W{n}"].T
        b = i[f"L3_gnn_b{n}"]
        laid[f"mlp_b{n}"] = b if n == 4 else b.reshape(-1, P).T
    nc = bacc.Bacc("TRN2", target_bir_lowering=False, num_devices=1)
    arrays = {f"in_{k}": np.ascontiguousarray(v) for k, v in laid.items()}
    aps = {k: nc.dram_tensor(f"in_{k}", arrays[f"in_{k}"].shape, F32, kind="ExternalInput").ap() for k in laid}
    out = nc.dram_tensor("out_0_dram", (N, D), F32, kind="ExternalOutput").ap()
    build(nc, aps, out)
    return run_bass_kernel_spmd(nc, [arrays], core_ids=[0]).results[0]["out_0_dram"]
```

```python
from contextlib import ExitStack

import concourse.bass as bass
from concourse import mybir

F32 = mybir.dt.float32
BF16 = mybir.dt.bfloat16
F16 = mybir.dt.float16
ALU = mybir.AluOpType
ACT = mybir.ActivationFunctionType
AX_X = mybir.AxisListType.X

P = 128
N = 2048
T = N // P
D = 512
KT = D // P
EPS = 1e-5
SLOPE = 0.2
LO_SCALE = float(2**11)
STEP_SCALE = float(2**60)
JB = 4
NB = T // JB
RING = 4
EVAC_AT = 1
LIMITS = {2: (72.0, 6.0, 100.0), 3: (72.0, 72.0, 5000.0)}



def later(t, than=1):
    return not isinstance(t, int) or t > than


def col(x, t):
    return x[:, bass.ds(t, 1)]


def staged_tiles(eng, *stages):
    lags = [lag for lag, _ in stages]
    head = (max(lags) + 3) // 2 * 2
    tail = T + min(lags) - min(lags) % 2

    def step(base, q, checked):
        for lag, emit in stages:
            par = (q - lag) % 2
            pair = base + (q - lag - par) // 2
            if not checked or 0 <= 2 * pair + par < T:
                emit(2 * pair + par, pair, par)

    for s in range(head):
        step(s // 2, s % 2, True)
    with eng.Fori(head // 2, tail // 2) as i:
        for q in range(2):
            step(i, q, False)
    for s in range(tail, T + max(lags)):
        step(s // 2, s % 2, True)


class Mem:

    def __init__(self, nc, stack, prefix):
        self.nc, self.stack, self.prefix, self.sems = nc, stack, prefix, []

    def sb(self, name, shape, dt=F32):
        return self.stack.enter_context(self.nc.sbuf_tensor(f"{self.prefix}_{name}", shape, dt))

    def ps(self, name, shape, dt=F32):
        return self.stack.enter_context(self.nc.psum_tensor(f"{self.prefix}_{name}", shape, dt))

    def sem(self, name):
        self.sems.append(self.stack.enter_context(self.nc.semaphore(f"{self.prefix}_{name}")))
        return self.sems[-1]


class LayerNorm:

    def __init__(self, nc, m, consts, row_factor=None, keep=None):
        self.nc, self.consts, self.row_factor, self.keep = nc, consts, row_factor, keep
        self.stats = [m.sb(f"ln_stats{p}", [P, 6]) for p in range(2)]
        self.mean_var = [m.sb(f"ln_mean_var{p}", [P, 2]) for p in range(2)]
        self.var_eps = [m.sb(f"ln_var_eps{p}", [P, 1]) for p in range(2)]
        self.neg_mean = [m.sb(f"ln_neg_mean{p}", [P, 1]) for p in range(2)]
        self.rstd = [m.sb(f"ln_rstd{p}", [P, 1]) for p in range(2)]
        self.scale = [m.sb(f"ln_scale{p}", [P, 1]) for p in range(2)]
        self.shift = [m.sb(f"ln_shift{p}", [P, 1]) for p in range(2)]
        self.stats_done = m.sem("ln_stats_done")
        self.moments_done = m.sem("ln_moments_done")
        self.moments_ready = m.sem("ln_moments_ready")
        self.rstd_done = m.sem("ln_rstd_done")
        self.scale_done = m.sem("ln_scale_done")
        self.coefs_ready = m.sem("ln_coefs_ready")

    def vector(self, dve, x, t, par):
        self.vector_stats(dve, x, t, par)
        self.vector_moments(dve, t, par)

    def vector_stats(self, dve, x, t, par):
        self.nc.vector.bn_stats(self.stats[par][:], x).then_inc(self.stats_done, 1)

    def vector_moments(self, dve, t, par):
        nc = self.nc
        dve.wait_ge(self.stats_done, t + 1)
        self.consts["settle"](dve)
        nc.vector.bn_aggr(self.mean_var[par][:], self.stats[par][:]).then_inc(self.moments_done, 1)
        dve.wait_ge(self.moments_done, t + 1)
        nc.vector.tensor_scalar(self.var_eps[par][:], self.mean_var[par][:, 1:2], EPS, None, ALU.add)
        nc.vector.tensor_scalar(self.neg_mean[par][:], self.mean_var[par][:, 0:1], -1.0, None,
                                ALU.mult).then_inc(self.moments_ready, 1)

    def pool(self, pool, t, par):
        nc = self.nc
        pool.wait_ge(self.moments_ready, t + 1)
        nc.gpsimd.tensor_tensor(self.rstd[par][:], self.var_eps[par][:], self.consts["neg_half"][:, 0:1],
                                ALU.pow).then_inc(self.rstd_done, 1)
        pool.wait_ge(self.rstd_done, t + 1)
        last = self.rstd[par][:]
        if self.row_factor is not None:
            last = col(self.keep[0], t) if self.keep else self.scale[par][:]
            self.consts["settle"](pool)
            nc.gpsimd.tensor_tensor(last, self.rstd[par][:], col(self.row_factor, t),
                                    ALU.mult).then_inc(self.scale_done, 1)
            pool.wait_ge(self.scale_done, t + 1)
            self.consts["settle"](pool)
        nc.gpsimd.tensor_tensor(col(self.keep[1], t) if self.keep else self.shift[par][:], self.neg_mean[par][:],
                                last, ALU.mult).then_inc(self.coefs_ready, 1)

    def scalar(self, act, out, x, t, par):
        act.wait_ge(self.coefs_ready, t + 1)
        scale = self.rstd if self.row_factor is None else self.scale
        return self.nc.scalar.activation(out, x, ACT.Relu, bias=self.shift[par][:], scale=scale[par][:])


def load_tiles(sp, src, dst, loaded, used, then=None, store=None, store_lag=2):
    def load(t, pair, par):
        if later(t):
            if used is None:
                sp.wait_ge(loaded[par], 16 * pair)
            else:
                sp.wait_ge(used, t - 1)
        sp.dma_start(dst[:, t, :] if used is None else dst[par][:], src[t]).then_inc(loaded[par], 16)
        if then is not None and isinstance(t, int) and t == 1:
            then()

    staged_tiles(sp, (0, load), *([(store_lag, store)] if store else []))


def rows(x):
    return x.rearrange("(t p) d -> t p d", p=P)


def build_constants(nc, consts):
    with ExitStack() as stack:
        m = Mem(nc, stack, "const")
        filled = m.sem("filled")
        with nc.Block() as block:

            @block.gpsimd
            def _(pool):
                nc.gpsimd.memset(consts["neg_half"][:], -0.5)
                nc.gpsimd.memset(consts["neg_one"][:], -1.0)
                nc.gpsimd.memset(consts["ones_bf16"][:], 1.0)
                nc.gpsimd.memset(consts["ident"][:], 0.0).then_inc(filled, 1)
                pool.wait_ge(filled, 1)
                nc.gpsimd.affine_select(out=consts["ident"][:], in_=consts["ident"][:],
                                        compare_op=ALU.not_equal, fill=1.0, base=0, pattern=[[-1, P]],
                                        channel_multiplier=1)
    return m.sems


def head_weights(nc, dve, w, a12, wa, terms, heads, wa_step, wa_ready):
    for s in range(2):
        if s:
            dve.wait_ge(wa_ready, s)
        nc.vector.tensor_tensor(terms, w, a12[:, s:s + 1, :].broadcast_to([P, KT, D]), ALU.mult).then_inc(wa_step, 1)
        dve.wait_ge(wa_step, s + 1)
        nc.vector.tensor_reduce(wa[:, :, s * heads:(s + 1) * heads],
                                terms.rearrange("p k (h d) -> p k h d", h=heads), AX_X, ALU.add).then_inc(wa_ready, 1)


def load_head_weights(sp, w, w_dram, a12, a12_dram, w_loaded):
    sp.dma_start(w, w_dram.rearrange("(k p) n -> p k n", p=P)).then_inc(w_loaded, 16)
    sp.dma_start(a12, a12_dram.unsqueeze(0).broadcast_to([P, 2, D])).then_inc(w_loaded, 16)


def build_projection(nc, name, consts, x, x_src, weights, heads, terms, keep, s12_dram, spare,
                     adj_loads=None, value_sum=None):
    dh = D // heads
    w, a12, wa = weights
    with ExitStack() as stack:
        m = Mem(nc, stack, name)
        wa_terms = spare[:, 0:KT * D].rearrange("p (k n) -> p k n", k=KT)
        h = [m.sb(f"h{p}", [P, D]) for p in range(2)]
        ht = [m.sb(f"ht{p}", [P, KT, P]) for p in range(2)]
        s12 = m.sb("s12", [P, T, 2 * heads])
        s12_tile = [m.sb(f"s12_tile{p}", [P, 2 * heads]) for p in range(2)]
        clipped = m.sb("clipped", [P, T, 2, heads])
        at = KT * D + N
        squares = spare[:, at:at + T * 2 * heads].rearrange("p (t s) -> p t s", t=T)
        at += T * 2 * heads
        value_squares, square_sum = spare[:, at:at + D], spare[:, at + D:at + 2 * D]
        limits = LIMITS[terms]
        square_step = m.sem("square_step")
        s12_rows = spare[0:2 * heads, KT * D:KT * D + N]
        largest = [m.sb(f"largest{n}", [P, 1]) for n in range(3)]
        largest_all = m.sb("largest_all", [1, 1])
        ps_t = [m.ps(f"ps_t{p}", [P, KT, P]) for p in range(2)]
        ps_v = [m.ps(f"ps_v{p}", [P, D]) for p in range(2)]
        ps_s = [m.ps(f"ps_s{p}", [P, 512]) for p in range(2)]
        ps_r = [m.ps(f"ps_r{p}", [P, 512]) for p in range(2)]
        ln = LayerNorm(nc, m, consts)
        w_loaded = m.sem("w_loaded")
        x_loaded = [m.sem(f"x_loaded{p}") for p in range(2)]
        h_ready = m.sem("h_ready")
        h_transposed = m.sem("h_transposed")
        ht_ready = m.sem("ht_ready")
        wa_step = m.sem("wa_step")
        wa_ready = m.sem("wa_ready")
        ones_set = m.sem("ones_set")
        projected = m.sem("projected")
        values_out = m.sem("values_out")
        rows_out = m.sem("rows_out")
        bounded = m.sem("bounded")
        clip_ready = m.sem("clip_ready")
        scores_stored = m.sem("scores_stored")
        range_step = m.sem("range_step")
        range_turned = m.sem("range_turned")
        sum_step = m.sem("sum_step")
        rows_turned = m.sem("rows_turned")
        tile_scores = m.sem("tile_scores")
        exps_ready = m.sem("exps_ready")
        values, exp_s2, step_bias, row_exps = keep["values"], keep["exp_s2"], keep["step_bias"], keep["row_exps"]
        with nc.Block() as block:

            @block.sync
            def _(sp):
                if x_src is not None:
                    load_tiles(sp, rows(x_src[0]), x, x_loaded, None,
                               lambda: load_head_weights(sp, w, x_src[1], a12, x_src[2], w_loaded))
                sp.wait_ge(rows_out, T)
                sp.dma_start(s12_dram, s12_rows).then_inc(scores_stored, 16)
                sp.wait_ge(scores_stored, 16)

            @block.gpsimd
            def _(pool):
                def start_adj_loads(t, pair, par):
                    if isinstance(t, int) and t == 1:
                        pool.wait_ge(w_loaded, 32)
                        adj_loads(pool)

                nc.gpsimd.memset(values[:, :, :, dh:dh + 1], 1.0).then_inc(ones_set, 1)
                def square(t, pair, par):
                    pool.wait_ge(values_out, t + 3)
                    pool.wait_ge(square_step, 2 * t + 1)
                    consts["settle"](pool)
                    v = values[:, t, :, 0:dh]
                    nc.gpsimd.tensor_tensor(value_squares.rearrange("p (h d) -> p h d", h=heads), v, v,
                                            ALU.mult).then_inc(square_step, 1)
                    pool.wait_ge(square_step, 2 * t + 2)
                    nc.gpsimd.tensor_tensor(square_sum, square_sum, value_squares, ALU.add).then_inc(square_step, 1)

                def add_values(t, pair, par):
                    pool.wait_ge(sum_step, t + 1)
                    pool.wait_ge(values_out, t + 3)
                    consts["settle"](pool)
                    nc.gpsimd.tensor_tensor(value_sum[:], value_sum[:], values[:, t, :, :],
                                            ALU.add).then_inc(sum_step, 1)

                nc.gpsimd.memset(square_sum, 0.0).then_inc(square_step, 1)
                stages = [(0, lambda t, pair, par: ln.pool(pool, t, par)), (3, square)]
                if adj_loads is not None:
                    stages.insert(1, (0, start_adj_loads))
                if value_sum is not None:
                    nc.gpsimd.memset(value_sum[:], 0.0).then_inc(sum_step, 1)
                    pool.wait_ge(ones_set, 1)
                    stages.append((3, add_values))
                staged_tiles(pool, *stages)

            @block.scalar
            def _(act):
                def normed(t, pair, par):
                    if later(t):
                        act.wait_ge(h_transposed, t - 1)
                    ln.scalar(act, h[par][:], x[:, t, :], t, par).then_inc(h_ready, 1)

                def transposed_out(t, pair, par):
                    act.wait_ge(h_transposed, t + 1)
                    nc.scalar.copy(ht[par][:], ps_t[par][:]).then_inc(ht_ready, 1)

                def rows_copy(t, pair, par):
                    act.wait_ge(rows_turned, t + 1)
                    nc.scalar.copy(s12_rows[:, bass.ts(t, P)], ps_r[par][0:2 * heads, 0:P]).then_inc(rows_out, 1)

                staged_tiles(act, (0, normed), (1, transposed_out), (4, rows_copy))
                act.wait_ge(bounded, 1)
                nc.scalar.activation(exp_s2[:, :, :, 0], s12[:, :, heads:], ACT.Exp)
                nc.scalar.activation(exp_s2[:, :, :, 1], s12[:, :, heads:], ACT.Exp, scale=SLOPE)
                nc.scalar.mul(step_bias[:], s12[:, :, heads:], STEP_SCALE)
                act.wait_ge(clip_ready, 1)
                nc.scalar.activation(row_exps[:, :, 0, :], clipped[:, :, 0, :], ACT.Exp, scale=1.0 - SLOPE)
                nc.scalar.activation(row_exps[:, :, 1, :], clipped[:, :, 1, :], ACT.Exp,
                                     scale=SLOPE - 1.0).then_inc(exps_ready, 1)

            @block.vector
            def _(dve):
                def stats(t, pair, par):
                    if x_src is not None:
                        dve.wait_ge(x_loaded[par], 16 * (pair + 1))
                    if later(t):
                        dve.wait_ge(h_ready, t - 1)
                    ln.vector(dve, x[:, t, :], t, par)

                def out(t, pair, par):
                    dve.wait_ge(projected, t + 1)
                    nc.vector.tensor_copy(values[:, t, :, 0:dh],
                                          ps_v[par][:].rearrange("p (h d) -> p h d", h=heads))
                    if later(t):
                        dve.wait_ge(rows_turned, t - 1)
                    nc.vector.tensor_copy(s12_tile[par][:], ps_s[par][:, 0:2 * heads]).then_inc(tile_scores, 1)
                    nc.vector.tensor_copy(s12[:, t, :], ps_s[par][:, 0:2 * heads]).then_inc(values_out, 1)

                def weights_by_head(t, pair, par):
                    if x_src is not None and isinstance(t, int) and t == 0:
                        dve.wait_ge(w_loaded, 32)
                        head_weights(nc, dve, w, a12, wa, wa_terms, heads, wa_step, wa_ready)

                dve.sem_inc(values_out, 2)
                staged_tiles(dve, (0, stats), (1, weights_by_head), (2, out))
                dve.wait_ge(values_out, T + 2)
                nc.vector.tensor_scalar(s12[:], s12[:], limits[0], -limits[0], ALU.min, ALU.max).then_inc(bounded, 1)
                dve.wait_ge(bounded, 1)
                nc.vector.tensor_scalar(clipped[:, :, 0, :], s12[:, :, 0:heads], 0.0, None, ALU.min)
                nc.vector.tensor_scalar(clipped[:, :, 1, :], s12[:, :, 0:heads], 0.0, None,
                                        ALU.max).then_inc(clip_ready, 1)
                for n in range(2):
                    side = s12[:, :, n * heads:(n + 1) * heads]
                    nc.vector.scalar_tensor_tensor(out=squares[:, :, n * heads:(n + 1) * heads], in0=side,
                                                   scalar=limits[n]**-2, in1=side, op0=ALU.mult,
                                                   op1=ALU.mult).then_inc(range_step, 1)
                dve.wait_ge(range_step, 2)
                nc.vector.tensor_reduce(largest[0][:], squares.rearrange("p t s -> p (t s)"), AX_X,
                                        ALU.max).then_inc(range_step, 1)
                dve.wait_ge(square_step, 2 * T + 1)
                nc.vector.tensor_reduce(largest[1][:], square_sum, AX_X, ALU.max).then_inc(range_step, 1)
                dve.wait_ge(range_step, 4)
                nc.vector.scalar_tensor_tensor(out=largest[2][:], in0=largest[1][:], scalar=limits[2]**-2,
                                               in1=largest[0][:], op0=ALU.mult, op1=ALU.max).then_inc(range_step, 1)
                if "neg_s2" in keep:
                    nc.vector.tensor_scalar(keep["neg_s2"][:], s12[:, :, heads:], -1.0, None, ALU.mult)
                    dve.wait_ge(exps_ready, 1)
                    nc.vector.tensor_scalar(row_exps[:, :, 1, :], row_exps[:, :, 1, :], -1.0, None, ALU.mult)
                dve.wait_ge(range_turned, 1)
                nc.vector.tensor_reduce(largest_all[:], ps_r[0][0:1, 0:P], AX_X, ALU.max).then_inc(range_step, 1)
                dve.wait_ge(range_step, 6)
                nc.vector.tensor_scalar(keep["far"][:], largest_all[:], 1.0, None, ALU.is_ge)

            @block.tensor
            def _(pe):
                def turn(t, pair, par):
                    pe.wait_ge(h_ready, t + 1)
                    for k in range(KT):
                        mm = nc.tensor.transpose(ps_t[par][:, k, :], h[par][:, k * P:(k + 1) * P],
                                                 consts["ident"][:])
                    mm.then_inc(h_transposed, 1)

                def project(t, pair, par):
                    if x_src is not None and isinstance(t, int) and t == 0:
                        pe.wait_ge(w_loaded, 32)
                    pe.wait_ge(ht_ready, t + 1)
                    pe.wait_ge(values_out, t + 1)
                    for k in range(KT):
                        nc.tensor.matmul(ps_v[par][:], ht[par][:, k, :], w[:, k, :],
                                         start=(k == 0), stop=(k == KT - 1))
                    if x_src is not None and isinstance(t, int) and t == 0:
                        pe.wait_ge(wa_ready, 2)
                    for k in range(KT):
                        mm = nc.tensor.matmul(ps_s[par][:, 0:2 * heads], ht[par][:, k, :], wa[:, k, :],
                                              start=(k == 0), stop=(k == KT - 1))
                    mm.then_inc(projected, 1)

                def score_rows(t, pair, par):
                    pe.wait_ge(tile_scores, t + 1)
                    if later(t):
                        pe.wait_ge(rows_out, t - 1)
                    nc.tensor.transpose(ps_r[par][0:2 * heads, 0:P], s12_tile[par][:],
                                        consts["ident"][:]).then_inc(rows_turned, 1)

                staged_tiles(pe, (0, turn), (3, score_rows), (1, project))
                pe.wait_ge(range_step, 5)
                pe.wait_ge(rows_out, T)
                nc.tensor.transpose(ps_r[0][0:1, 0:P], largest[2][:], consts["ident"][:]).then_inc(range_turned, 1)
    return m.sems



def build_lonely_rows(nc, consts, adj_t, adj_loaded, lonely, stats, done_with):
    CH = 512
    with ExitStack() as stack:
        m = Mem(nc, stack, "lonely")
        ps_deg = m.ps("ps_deg", [P, N // CH, CH])
        counted = m.sem("counted")
        flagged = m.sem("flagged")
        column_step = m.sem("column_step")
        ps_col = m.ps("ps_col", [P, 512])
        turned = m.sem("turned")
        JD = 12
        with nc.Block() as block:

            @block.gpsimd
            def _(pool):
                for sem in done_with:
                    pool.sem_clear(sem)
                for c in range(N // CH):
                    cols = slice(c * CH, (c + 1) * CH)
                    pool.wait_ge(flagged, c + 1)
                    nc.gpsimd.tensor_tensor(adj_t[:, JD:T, cols], adj_t[:, JD:T, cols],
                                            lonely[:, cols].unsqueeze(1).broadcast_to([P, T - JD, CH]), ALU.add)

            @block.tensor
            def _(pe):
                pe.wait_ge(adj_loaded, 16 * NB)
                for c in range(N // CH):
                    for j in range(T):
                        mm = nc.tensor.matmul(ps_deg[:, c, :], consts["ones_bf16"][:],
                                              adj_t[:, j, c * CH:(c + 1) * CH],
                                              start=(j == 0), stop=(j == T - 1))
                    mm.then_inc(counted, 1)
                pe.wait_ge(flagged, N // CH)
                for t in range(T):
                    mm = nc.tensor.matmul(ps_col[:, t:t + 1], lonely[0:1, t * P:(t + 1) * P],
                                          consts["ones_bf16"][0:1, 0:1], start=(t == 0), stop=(t == T - 1),
                                          skip_group_check=True)
                mm.then_inc(turned, 1)

            @block.vector
            def _(dve):
                for c in range(N // CH):
                    cols = slice(c * CH, (c + 1) * CH)
                    dve.wait_ge(counted, c + 1)
                    nc.vector.tensor_scalar(lonely[:, cols], ps_deg[:, c, :], 0.0, None,
                                            ALU.is_equal).then_inc(flagged, 1)
                    dve.wait_ge(flagged, c + 1)
                    nc.vector.tensor_tensor(adj_t[:, 0:JD, cols], adj_t[:, 0:JD, cols],
                                            lonely[:, cols].unsqueeze(1).broadcast_to([P, JD, CH]), ALU.add)
                dve.wait_ge(turned, 1)
                nc.vector.tensor_copy(stats["lonely"][:], ps_col[:, 0:T]).then_inc(column_step, 1)
                dve.wait_ge(column_step, 1)
                nc.vector.tensor_scalar(stats["has_neighbour"][:], stats["lonely"][:], -1.0, 1.0, ALU.mult,
                                        ALU.add)
                nc.vector.tensor_scalar(stats["lo_has_neighbour"][:], stats["lonely"][:], -1.0 / LO_SCALE,
                                        1.0 / LO_SCALE, ALU.mult, ALU.add)
    return m.sems


def build_attention(nc, name, settle, neg_one, heads, keep, adj_t, s1_dram, ring, wide, hidden, terms, complements, direct):
    dh = D // heads
    c1 = dh + 1
    side = terms * c1
    region = 256 if 2 * side <= 256 else 512
    IT = 2048 // region
    CW = IT * P
    NCH = N // CW
    HC = 2 * NCH
    TERM = BF16 if terms == 3 else F16
    all_other = len(complements) == NB
    with ExitStack() as stack:
        m = Mem(nc, stack, name)
        taken = RING * JB * CW
        left = [wide[:].bitcast(F32)] if wide is not None else []
        other = {}
        for b in complements:
            other[b] = ring[:, taken:taken + JB * CW].rearrange("p (q c) -> p q c", q=JB)
            taken += JB * CW
        if taken < ring.shape[1]:
            left.append(ring[:, taken:].bitcast(F32))

        def small(name, shape):
            size = 1
            for n in shape[1:]:
                size *= n
            left.sort(key=lambda place: place.shape[1])
            fits = [n for n, place in enumerate(left) if place.shape[1] >= size]
            if not fits:
                return m.sb(name, shape)[:]
            place = left.pop(fits[0])
            at = place[:, 0:size]
            if place.shape[1] > size:
                left.append(place[:, size:])
            return at if len(shape) == 2 else at.rearrange("p (i s c) -> p i s c", **dict(zip("isc", shape[1:])))

        JV = JB
        s1_wide = [small(f"s1_wide{p}", [P, CW]) for p in range(2)]
        mask = [ring[:, r * JB * CW:(r + 1) * JB * CW].rearrange("p (q c) -> p q c", q=JB) for r in range(RING)]
        parts = [m.sb(f"parts{p}", [P, T, 2 * side], TERM) for p in range(2)]
        minus = None if all_other else [m.sb(f"minus{p}", [P, T, side], TERM) for p in range(2)]
        weighted = small("weighted", [P, JV, 2, c1])
        rest = small("rest", [P, JV, 2, c1])
        sums = [small(f"sums{p}", [P, IT, 2, c1]) for p in range(2)]
        ps = [m.ps(f"ps_sums{p}", [P, IT, region]) for p in range(2)]
        s1_loaded = [m.sem(f"s1_loaded{p}") for p in range(2)]
        steps_ready = m.sem("steps_ready")
        mask_made = m.sem("mask_made")
        other_made = m.sem("other_made")
        masks_used = m.sem("masks_used")
        parts_step = m.sem("parts_step")
        parts_ready = m.sem("parts_ready")
        sums_out = m.sem("sums_out")
        lo_out = m.sem("lo_out")
        row_step = m.sem("row_step")
        chunk_done = m.sem("chunk_done")
        values, exp_s2, step_bias, row_exps = keep["values"], keep["exp_s2"], keep["step_bias"], keep["row_exps"]

        def head_pairs(eng, body):
            body(0, True)
            with eng.Fori(1, heads // 2) as pair:
                body(pair, False)

        with nc.Block() as block:

            @block.sync
            def _(sp):
                def body(pair, first):
                    for k in range(HC):
                        g = pair * HC + k
                        head, c = 2 * pair + k // NCH, k % NCH
                        if not first or k >= 2:
                            sp.wait_ge(mask_made, NB * (g - 1))
                        sp.dma_start(s1_wide[k % 2][:],
                                     s1_dram[bass.ds(head, 1), c * CW:(c + 1) * CW].broadcast_to([P, CW])
                                     ).then_inc(s1_loaded[k % 2], 16)
                head_pairs(sp, body)

            @block.gpsimd
            def _(pool):
                NP = 3 - (1 if all_other else 0)

                def make_parts(head, u, v, first):
                    js = slice(v * JV, (v + 1) * JV)
                    base = NP * (NB * head + v)
                    done = [0]

                    def part(n):
                        return parts[u][:, js, :].rearrange("p j (s n c) -> p j s n c", s=2, n=terms)[:, :, :, n, :]

                    def link(op):
                        op.then_inc(parts_step, 1)
                        done[0] += 1
                        pool.wait_ge(parts_step, base + done[0])
                        settle(pool)

                    if not first and v == 0:
                        pool.wait_ge(masks_used, NB * NCH * (head - 1))
                    if not isinstance(head, int) or head > 0 or v > 0:
                        pool.wait_ge(parts_ready, NB * head + v)
                        settle(pool)
                    v_rows = values[:, js, bass.ds(head, 1), :].broadcast_to([P, JV, 2, c1])
                    exps = exp_s2[:, js, bass.ds(head, 1), :].rearrange("p j h s -> p j (h s)").unsqueeze(3)\
                        .broadcast_to([P, JV, 2, c1])
                    nc.gpsimd.tensor_tensor(weighted[:], v_rows, exps, ALU.mult)
                    link(nc.gpsimd.tensor_tensor(part(0), v_rows, exps, ALU.mult))
                    if terms == 3:
                        nc.gpsimd.tensor_tensor(rest[:], weighted[:], part(0), ALU.subtract)
                        link(nc.gpsimd.tensor_tensor(part(1), weighted[:], part(0), ALU.subtract))
                        last = nc.gpsimd.tensor_tensor(part(2), rest[:], part(1), ALU.subtract)
                    else:
                        link(nc.gpsimd.tensor_tensor(rest[:], weighted[:], part(0), ALU.subtract))
                        last = nc.gpsimd.tensor_scalar(part(1), rest[:], LO_SCALE, 1.0, ALU.mult, ALU.mult)
                    if not all_other:
                        link(last)
                        last = nc.gpsimd.tensor_scalar(minus[u][:, js, :], parts[u][:, js, side:2 * side],
                                                       -1.0, 1.0, ALU.mult, ALU.mult)
                    last.then_inc(parts_ready, 1)
                    assert done[0] == NP

                def rows_out(pair, k):
                    c = k % NCH
                    head = 2 * pair + k // NCH
                    g = pair * HC + k
                    its = slice(c * IT, (c + 1) * IT)
                    x = sums[k % 2]
                    pool.wait_ge(sums_out, g + 3)
                    settle(pool)
                    nc.gpsimd.tensor_tensor(x, x, row_exps[:, its, :, bass.ds(head, 1)]
                                            .broadcast_to([P, IT, 2, c1]), ALU.mult).then_inc(row_step, 1)
                    pool.wait_ge(row_step, 3 * g + 1)
                    settle(pool)
                    nc.gpsimd.tensor_tensor(x[:, :, 0, :], x[:, :, 0, :], x[:, :, 1, :], ALU.add).then_inc(row_step, 1)
                    pool.wait_ge(row_step, 3 * g + 2)
                    settle(pool)
                    nc.gpsimd.tensor_tensor(x[:, :, 1, 0:1], x[:, :, 0, dh:dh + 1],
                                            neg_one[:].unsqueeze(1).broadcast_to([P, IT, 1]), ALU.pow).then_inc(row_step, 1)
                    pool.wait_ge(row_step, 3 * g + 3)
                    settle(pool)
                    nc.gpsimd.tensor_tensor(hidden[:, its, bass.ds(head * dh, dh)], x[:, :, 0, 0:dh],
                                            x[:, :, 1, 0:1].broadcast_to([P, IT, dh]), ALU.mult)\
                        .then_inc(chunk_done, 1)

                def body(pair, first, last=False):
                    per_chunk = NB // NCH
                    for k in range(HC):
                        u = k // NCH
                        if not (last and u == 1):
                            for v in range((k % NCH) * per_chunk, (k % NCH + 1) * per_chunk):
                                make_parts(2 * pair + u + 1, 1 - u, v, first and u == 0)
                        if k >= 1:
                            rows_out(pair, k - 1)
                        elif not first:
                            rows_out(pair - 1, HC - 1)

                for v in range(NB):
                    make_parts(0, 0, v, True)
                body(0, True)
                with pool.Fori(1, heads // 2 - 1) as pair:
                    body(pair, False)
                body(heads // 2 - 1, False, True)
                rows_out(heads // 2 - 1, HC - 1)

            @block.scalar
            def _(act):
                def body(pair, first):
                    for k in range(HC):
                        head = 2 * pair + k // NCH
                        g = pair * HC + k
                        act.wait_ge(s1_loaded[k % 2], 16 * (pair * NCH + k // 2 + 1))
                        settle(act)
                        for b in range(NB):
                            if not first or k >= 1:
                                act.wait_ge(masks_used, NB * (g - 1) + b + 1)
                                settle(act)
                            for q in range(JB):
                                j = b * JB + q
                                if j in direct:
                                    continue
                                op = nc.scalar.activation(mask[b][:, q, :], s1_wide[k % 2][:], ACT.Relu,
                                                          bias=step_bias[:, j, bass.ds(head, 1)],
                                                          scale=STEP_SCALE)
                            op.then_inc(steps_ready, 1)
                head_pairs(act, body)

            @block.vector
            def _(dve):
                def make_masks(pair, k, b):
                    c = k % NCH
                    head = 2 * pair + k // NCH
                    g = pair * HC + k
                    dve.wait_ge(steps_ready, NB * g + b + 1)
                    cols = slice(c * CW, (c + 1) * CW)
                    alone = [q for q in range(JB) if b * JB + q in direct]
                    for q in alone:
                        j = b * JB + q
                        settle(dve)
                        nc.vector.scalar_tensor_tensor(out=mask[b][:, q, :], in0=s1_wide[k % 2][:],
                                                       scalar=keep["neg_s2"][:, j, bass.ds(head, 1)],
                                                       in1=adj_t[:, j, cols], op0=ALU.is_gt, op1=ALU.mult)
                    q = JB - len(alone)
                    nc.vector.tensor_tensor(mask[b][:, 0:q, :], mask[b][:, 0:q, :],
                                            adj_t[:, b * JB:b * JB + q, cols], ALU.min).then_inc(mask_made, 1)

                def make_other(pair, k, b):
                    c = k % NCH
                    g = pair * HC + k
                    dve.wait_ge(mask_made, NB * g + b + 1)
                    nc.vector.tensor_tensor(other[b], adj_t[:, b * JB:(b + 1) * JB, c * CW:(c + 1) * CW],
                                            mask[b], ALU.subtract).then_inc(other_made, 1)

                def evacuate(pair, k):
                    g = pair * HC + k
                    dve.wait_ge(masks_used, NB * (g + 1))
                    if not isinstance(g, int) or g >= 2:
                        dve.wait_ge(chunk_done, g - 1)
                    by_term = ps[k % 2][:, :, 0:2 * side].rearrange("p i (s n c) -> p i s n c", s=2, n=terms)
                    if terms == 3:
                        for s in range(2):
                            op = nc.vector.tensor_reduce(sums[k % 2][:, :, s, :],
                                                         by_term[:, :, s].rearrange("p i n c -> p i c n"),
                                                         AX_X, ALU.add)
                    else:
                        nc.vector.tensor_scalar(sums[k % 2], by_term[:, :, :, 1, :], 1.0 / LO_SCALE, None,
                                                ALU.mult).then_inc(lo_out, 1)
                        dve.wait_ge(lo_out, g + 1)
                        op = nc.vector.tensor_tensor(sums[k % 2], by_term[:, :, :, 0, :], sums[k % 2], ALU.add)
                    op.then_inc(sums_out, 1)

                def body(pair, first):
                    for k in range(HC):
                        for b in range(NB):
                            make_masks(pair, k, b)
                            if b in other:
                                make_other(pair, k, b)
                            if b == EVAC_AT and k >= 1:
                                evacuate(pair, k - 1)
                            if b == EVAC_AT and k == 0 and not first:
                                evacuate(pair - 1, HC - 1)

                dve.sem_inc(sums_out, 2)
                head_pairs(dve, body)
                evacuate(heads // 2 - 1, HC - 1)

            @block.tensor
            def _(pe):
                def body(pair, first):
                    for k in range(HC):
                        g = pair * HC + k
                        c, u = k % NCH, k // NCH
                        pe.wait_ge(sums_out, g + 1)
                        for b in range(NB):
                            if c == 0:
                                pe.wait_ge(parts_ready, NB * (2 * pair + u) + b + 1)
                            pe.wait_ge(mask_made, NB * g + b + 1)
                            if b in other:
                                pe.wait_ge(other_made, len(other) * g + complements.index(b) + 1)
                            for it in range(IT):
                                opens_bank = b == 0 and it * region % 512 == 0
                                for q in range(JB):
                                    j = b * JB + q
                                    out = ps[k % 2][:, it, :]
                                    width = side if b in other else 2 * side
                                    nc.tensor.matmul(out[:, 0:width], mask[b][:, q, it * P:(it + 1) * P],
                                                     parts[u][:, j, 0:width],
                                                     start=(opens_bank and q == 0), stop=(j == T - 1),
                                                     skip_group_check=True)
                                    rest_of = other[b][:, q, it * P:(it + 1) * P] if b in other else \
                                        adj_t[:, j, c * CW + it * P:c * CW + (it + 1) * P]
                                    b_terms = parts[u][:, j, side:2 * side] if all_other else minus[u][:, j, :]
                                    mm = nc.tensor.matmul(out[:, side:2 * side], rest_of, b_terms,
                                                          start=False, stop=(j == T - 1), skip_group_check=True)
                            mm.then_inc(masks_used, 1)
                with pe.Fori(0, heads // 2) as pair:
                    body(pair, False)
    return m.sems


def build_dense_attention(nc, name, settle, ident, heads, keep, adj_dram, s12_dram, spare, hidden, add_mask):
    dh = D // heads
    MASK = 65500.0 if add_mask else 9e15
    with ExitStack() as stack:
        m = Mem(nc, stack, name)
        adj_rows, s2_wide, e, et = [spare[:, n * N:(n + 1) * N] for n in range(4)]
        et = et.rearrange("p (j i) -> p j i", j=T)
        s1_col = m.sb("s1_col", [P, 1])
        row_max = m.sb("row_max", [P, 1])
        neg_max = m.sb("neg_max", [P, 1])
        row_sum = m.sb("row_sum", [P, 1])
        recip = m.sb("recip", [P, 1])
        ps_t = m.ps("ps_t", [P, T, P])
        ps_o = m.ps("ps_o", [P, 512])
        loaded = m.sem("loaded")
        mask_scaled = m.sem("mask_scaled")
        score_step = m.sem("score_step")
        shifted = m.sem("shifted")
        exps_ready = m.sem("exps_ready")
        turned = m.sem("turned")
        et_ready = m.sem("et_ready")
        summed = m.sem("summed")
        recip_ready = m.sem("recip_ready")
        tile_done = m.sem("tile_done")

        def tiles(eng, body):
            with eng.Fori(0, heads) as head:
                with eng.Fori(0, T) as it:
                    body(head, it, head * T + it)

        with nc.Block() as block:

            @block.sync
            def _(sp):
                def load(head, it, n):
                    sp.wait_ge(tile_done, n + 1)
                    sp.dma_start(adj_rows, rows(adj_dram)[it]).then_inc(loaded, 16)
                    sp.dma_start(s2_wide, s12_dram[bass.ds(head + heads, 1), :].broadcast_to([P, N])).then_inc(loaded, 16)
                    sp.dma_start(s1_col[:], s12_dram.rearrange("h (t p) -> h t p", p=P)[bass.ds(head, 1), bass.ds(it, 1), :]
                                 .rearrange("h t p -> p (h t)")).then_inc(loaded, 16)
                tiles(sp, load)

            @block.vector
            def _(dve):
                def tile(head, it, n):
                    links = [0]

                    def link(op):
                        op.then_inc(score_step, 1)
                        links[0] += 1
                        dve.wait_ge(score_step, LINKS * n + links[0])
                        settle(dve)

                    dve.wait_ge(loaded, 48 * (n + 1))
                    settle(dve)
                    link(nc.vector.tensor_scalar(e, s2_wide, s1_col[:], None, ALU.add))
                    link(nc.vector.scalar_tensor_tensor(out=e, in0=e, scalar=SLOPE, in1=e, op0=ALU.mult, op1=ALU.max))
                    if not add_mask:
                        link(nc.vector.tensor_tensor(e, e, adj_rows, ALU.mult))
                    link(nc.vector.tensor_scalar(adj_rows, adj_rows, -1.0, MASK, ALU.add, ALU.mult))
                    link(nc.vector.tensor_tensor(e, e, adj_rows, ALU.add))
                    link(nc.vector.tensor_reduce(row_max[:], e, AX_X, ALU.max))
                    nc.vector.tensor_scalar(neg_max[:], row_max[:], -1.0, None, ALU.mult).then_inc(shifted, 1)
                    dve.wait_ge(exps_ready, n + 1)
                    settle(dve)
                    link(nc.vector.tensor_reduce(row_sum[:], e, AX_X, ALU.add))
                    link(nc.vector.reciprocal(recip[:], row_sum[:]))
                    dve.wait_ge(summed, n + 1)
                    settle(dve)
                    nc.vector.tensor_scalar(hidden[:, bass.ds(it, 1), bass.ds(head * dh, dh)].rearrange("p t d -> p (t d)"),
                                            ps_o[:, 0:dh], recip[:], None, ALU.mult).then_inc(tile_done, 1)

                LINKS = 7 if add_mask else 8
                dve.sem_inc(tile_done, 1)
                tiles(dve, tile)

            @block.scalar
            def _(act):
                def tile(head, it, n):
                    act.wait_ge(shifted, n + 1)
                    settle(act)
                    nc.scalar.activation(e, e, ACT.Exp, bias=neg_max[:]).then_inc(exps_ready, 1)
                    act.wait_ge(turned, n + 1)
                    settle(act)
                    for b in range(NB):
                        js = slice(b * JB, (b + 1) * JB)
                        op = nc.scalar.copy(et[:, js, :], ps_t[:, js, :])
                    op.then_inc(et_ready, 1)
                tiles(act, tile)

            @block.tensor
            def _(pe):
                def tile(head, it, n):
                    pe.wait_ge(exps_ready, n + 1)
                    settle(pe)
                    for j in range(T):
                        mm = nc.tensor.transpose(ps_t[:, j, :], e[:, j * P:(j + 1) * P], ident[:])
                    mm.then_inc(turned, 1)
                    pe.wait_ge(et_ready, n + 1)
                    settle(pe)
                    for j in range(T):
                        mm = nc.tensor.matmul(ps_o[:, 0:dh], et[:, j, :], keep["values"][:, j, bass.ds(head, 1), 0:dh]
                                              .rearrange("p h d -> p (h d)"), start=(j == 0), stop=(j == T - 1))
                    mm.then_inc(summed, 1)
                tiles(pe, tile)
    return m.sems


class Split:

    def __init__(self, nc, m, parts, settle):
        self.nc, self.parts, self.settle = nc, parts, settle
        self.rest = [m.sb(f"split_rest{p}", [P, D]) for p in range(2)]
        self.hi_done = m.sem("split_hi_done")
        self.rest_ready = m.sem("split_rest_ready")
        self.done = m.sem("split_done")

    def pool(self, pool, h, t, par):
        pool.wait_ge(self.hi_done, t + 1)
        if later(t):
            pool.wait_ge(self.done, t - 1)
        self.settle(pool)
        self.nc.gpsimd.tensor_tensor(self.rest[par][:], h, self.parts[:, t, 0, :], ALU.subtract)\
            .then_inc(self.rest_ready, 1)

    def scalar(self, act, t, par):
        act.wait_ge(self.rest_ready, t + 1)
        self.nc.scalar.mul(self.parts[:, t, 1, :], self.rest[par][:], LO_SCALE).then_inc(self.done, 1)


def build_attention_out(nc, consts, x_src, x_dst, hidden, spare, w_dram, b_dram, h_parts, done_with):
    with ExitStack() as stack:
        m = Mem(nc, stack, "out0")
        w = spare[:, 0:KT * D].rearrange("p (k n) -> p k n", k=KT)
        bias = m.sb("bias", [P, D])
        x = [m.sb(f"x{p}", [P, D]) for p in range(2)]
        g = [m.sb(f"g{p}", [P, D]) for p in range(2)]
        gt = [m.sb(f"gt{p}", [P, KT, P]) for p in range(2)]
        y = [m.sb(f"y{p}", [P, D]) for p in range(2)]
        low = [m.sb(f"low{p}", [P, D]) for p in range(2)]
        x1 = [m.sb(f"x1{p}", [P, D]) for p in range(2)]
        h = [m.sb(f"h{p}", [P, D]) for p in range(2)]
        ps_t = [m.ps(f"ps_t{p}", [P, KT, P]) for p in range(2)]
        ps_y = [m.ps(f"ps_y{p}", [P, D]) for p in range(2)]
        ln = LayerNorm(nc, m, consts)
        split = Split(nc, m, h_parts, consts["settle"])
        w_loaded = m.sem("w_loaded")
        x_loaded = [m.sem(f"x_loaded{p}") for p in range(2)]
        x1_stored = [m.sem(f"x1_stored{p}") for p in range(2)]
        g_ready = m.sem("g_ready")
        turned = m.sem("turned")
        gt_ready = m.sem("gt_ready")
        projected = m.sem("projected")
        y_ready = m.sem("y_ready")
        low_ready = m.sem("low_ready")
        exp_ready = m.sem("exp_ready")
        x_added = m.sem("x_added")
        x1_ready = m.sem("x1_ready")
        with nc.Block() as block:

            @block.sync
            def _(sp):
                sp.dma_start(w, w_dram.rearrange("(k p) n -> p k n", p=P)).then_inc(w_loaded, 16)
                sp.dma_start(bias[:], b_dram.unsqueeze(0).broadcast_to([P, D])).then_inc(w_loaded, 16)

                def store(t, pair, par):
                    sp.wait_ge(x1_ready, t + 1)
                    sp.dma_start(rows(x_dst)[t], x1[par][:]).then_inc(x1_stored[par], 16)

                load_tiles(sp, rows(x_src), x, x_loaded, x_added, store=store, store_lag=3)
                for par in range(2):
                    sp.wait_ge(x1_stored[par], 16 * (T // 2))

            @block.gpsimd
            def _(pool):
                staged_tiles(pool, (3, lambda t, pair, par: ln.pool(pool, t, par)),
                             (4, lambda t, pair, par: split.pool(pool, h[par][:], t, par)))
                for sem in done_with:
                    pool.sem_clear(sem)

            @block.tensor
            def _(pe):
                def turn(t, pair, par):
                    pe.wait_ge(g_ready, t + 1)
                    for k in range(KT):
                        mm = nc.tensor.transpose(ps_t[par][:, k, :], g[par][:, k * P:(k + 1) * P],
                                                 consts["ident"][:])
                    mm.then_inc(turned, 1)

                def project(t, pair, par):
                    pe.wait_ge(gt_ready, t + 1)
                    if later(t):
                        pe.wait_ge(y_ready, t - 1)
                    for k in range(KT):
                        mm = nc.tensor.matmul(ps_y[par][:], gt[par][:, k, :], w[:, k, :],
                                              start=(k == 0), stop=(k == KT - 1))
                    mm.then_inc(projected, 1)

                pe.wait_ge(w_loaded, 32)
                staged_tiles(pe, (0, turn), (1, project))

            @block.scalar
            def _(act):
                def turned_out(t, pair, par):
                    act.wait_ge(turned, t + 1)
                    nc.scalar.copy(gt[par][:], ps_t[par][:]).then_inc(gt_ready, 1)

                def exp_low(t, pair, par):
                    act.wait_ge(low_ready, t + 1)
                    nc.scalar.activation(low[par][:], low[par][:], ACT.Exp).then_inc(exp_ready, 1)

                def normed(t, pair, par):
                    if later(t):
                        act.wait_ge(split.rest_ready, t - 1)
                    ln.scalar(act, h[par][:], x1[par][:], t, par)
                    consts["settle"](act)
                    ln.scalar(act, h_parts[:, t, 0, :], x1[par][:], t, par).then_inc(split.hi_done, 1)

                def pick(t, pair, par):
                    if later(t):
                        act.wait_ge(turned, t - 1)
                    nc.scalar.copy(g[par][:], hidden[:, t, :]).then_inc(g_ready, 1)

                staged_tiles(act, (0, pick), (1, turned_out), (2, exp_low), (4, normed),
                             (6, lambda t, pair, par: split.scalar(act, t, par)))

            @block.vector
            def _(dve):
                def biased(t, pair, par):
                    dve.wait_ge(projected, t + 1)
                    nc.vector.tensor_tensor(y[par][:], ps_y[par][:], bias[:], ALU.add).then_inc(y_ready, 1)

                def lower(t, pair, par):
                    dve.wait_ge(y_ready, t + 1)
                    nc.vector.tensor_scalar(low[par][:], y[par][:], 0.0, None, ALU.min).then_inc(low_ready, 1)

                def add_x(t, pair, par):
                    dve.wait_ge(x_loaded[par], 16 * (pair + 1))
                    dve.wait_ge(low_ready, t + 1)
                    nc.vector.scalar_tensor_tensor(out=y[par][:], in0=y[par][:], scalar=0.0, in1=x[par][:],
                                                   op0=ALU.max, op1=ALU.add).then_inc(x_added, 1)

                def residual(t, pair, par):
                    dve.wait_ge(exp_ready, t + 1)
                    dve.wait_ge(x_added, t + 1)
                    if later(t):
                        dve.wait_ge(x1_stored[par], 16 * pair)
                        dve.wait_ge(split.hi_done, t - 1)
                    nc.vector.scalar_tensor_tensor(out=x1[par][:], in0=low[par][:], scalar=-1.0, in1=y[par][:],
                                                   op0=ALU.add, op1=ALU.add).then_inc(x1_ready, 1)

                def stats_of(t, pair, par):
                    dve.wait_ge(x1_ready, t + 1)
                    ln.vector_stats(dve, x1[par][:], t, par)

                def moments(t, pair, par):
                    ln.vector_moments(dve, t, par)

                dve.wait_ge(w_loaded, 32)
                staged_tiles(dve, (0, biased), (1, residual), (0, lower), (1, stats_of), (0, add_x), (1, moments))


class AdjacencyProduct:

    def __init__(self, nc, m, matrix, parts):
        self.nc, self.matrix, self.parts = nc, matrix, parts
        self.hi = [m.ps(f"prod_hi{p}", [P, D]) for p in range(2)]
        self.lo = [m.ps(f"prod_lo{p}", [P, D]) for p in range(2)]
        self.lo_scaled = [m.sb(f"prod_lo_scaled{p}", [P, D]) for p in range(2)]
        self.summed = m.sem("prod_summed")
        self.lo_ready = m.sem("prod_lo_ready")
        self.joined = m.sem("prod_joined")

    def tensor(self, pe, t, par, js):
        if js[0] == 0 and later(t):
            pe.wait_ge(self.joined, t - 1)
            pe.wait_ge(self.lo_ready, t - 1)
        for j in js:
            for n, out in ((0, self.hi), (1, self.lo)):
                mm = self.nc.tensor.matmul(out[par][:], self.matrix[:, j, bass.ts(t, P)], self.parts[:, j, n, :],
                                           start=(j == 0), stop=(j == T - 1))
        if js[-1] == T - 1:
            mm.then_inc(self.summed, 1)

    def scalar(self, act, t, par, scale=1.0 / LO_SCALE):
        act.wait_ge(self.summed, t + 1)
        if later(t):
            act.wait_ge(self.joined, t - 1)
        if isinstance(scale, float):
            op = self.nc.scalar.mul(self.lo_scaled[par][:], self.lo[par][:], scale)
        else:
            op = self.nc.scalar.activation(self.lo_scaled[par][:], self.lo[par][:], ACT.Copy, scale=scale)
        op.then_inc(self.lo_ready, 1)

    def vector(self, dve, out, t, par, scale=1.0):
        dve.wait_ge(self.lo_ready, t + 1)
        return self.nc.vector.scalar_tensor_tensor(out=out, in0=self.hi[par][:], scalar=scale,
                                                   in1=self.lo_scaled[par][:], op0=ALU.mult,
                                                   op1=ALU.add).then_inc(self.joined, 1)


def build_linear_layer(nc, consts, x_src, x_dst, wt_dram, b_dram, adj_dram, adj_t, h_parts, sym, stats, lonely_wide):
    with ExitStack() as stack:
        m = Mem(nc, stack, "lin")
        w = m.sb("w", [P, KT, D])
        bias = m.sb("bias", [P, D])
        x = [m.sb(f"x{p}", [P, D]) for p in range(2)]
        agg = [m.sb(f"agg{p}", [P, D]) for p in range(2)]
        aggt = [m.sb(f"aggt{p}", [P, KT, P]) for p in range(2)]
        y = [m.sb("y", [P, D])] * 2
        x2 = [m.sb(f"x2{p}", [P, D]) for p in range(2)]
        adj_rows = m.sb("adj_rows", [P, N])
        ps_t = [m.ps(f"ps_t{p}", [P, KT, P]) for p in range(2)]
        ps_y = [m.ps(f"ps_y{p}", [P, D]) for p in range(2)]
        prod = AdjacencyProduct(nc, m, adj_t, h_parts)
        w_loaded = m.sem("w_loaded")
        x_loaded = [m.sem(f"x_loaded{p}") for p in range(2)]
        x2_stored = [m.sem(f"x2_stored{p}") for p in range(2)]
        adj_loaded = m.sem("adj_loaded")
        true_columns = m.sem("true_columns")
        sym_ready = m.sem("sym_ready")
        turned = m.sem("turned")
        aggt_ready = m.sem("aggt_ready")
        projected = m.sem("projected")
        y_ready = m.sem("y_ready")
        x2_ready = m.sem("x2_ready")
        deg_ready = m.sem("deg_ready")
        dinv_ready = m.sem("dinv_ready")
        ln = LayerNorm(nc, m, consts, stats["dinv"], (stats["ln_scale"], stats["ln_shift"]))
        with nc.Block() as block:

            @block.sync
            def _(sp):
                sp.dma_start(w[:], wt_dram.rearrange("(k p) n -> p k n", p=P)).then_inc(w_loaded, 16)
                sp.dma_start(bias[:], b_dram.unsqueeze(0).broadcast_to([P, D])).then_inc(w_loaded, 16)

                def store(t, pair, par):
                    sp.wait_ge(x2_ready, t + 1)
                    sp.dma_start(rows(x_dst)[t], x2[par][:]).then_inc(x2_stored[par], 16)

                load_tiles(sp, rows(x_src), x, x_loaded, x2_ready, store=store)
                for par in range(2):
                    sp.wait_ge(x2_stored[par], 16 * (T // 2))

            @block.gpsimd
            def _(pool):
                def fetch(t, pair, par):
                    if later(t, 0):
                        pool.wait_ge(sym_ready, t)
                    pool.dma_start(adj_rows[:], rows(adj_dram)[t]).then_inc(adj_loaded, 16)

                def inverse_root(t, pair, par):
                    pool.wait_ge(deg_ready, t + 1)
                    consts["settle"](pool)
                    nc.gpsimd.tensor_tensor(col(stats["dinv"], t), col(stats["deg"], t),
                                            consts["neg_half"][:, 0:1], ALU.pow).then_inc(dinv_ready, 1)

                def coefficients(t, pair, par):
                    pool.wait_ge(dinv_ready, t + 1)
                    ln.pool(pool, t, par)

                staged_tiles(pool, (0, fetch), (1, inverse_root), (2, coefficients))

            @block.tensor
            def _(pe):
                def turn(t, pair, par):
                    pe.wait_ge(prod.joined, t + 1)
                    for k in range(KT):
                        mm = nc.tensor.transpose(ps_t[par][:, k, :], agg[par][:, k * P:(k + 1) * P],
                                                 consts["ident"][:])
                    mm.then_inc(turned, 1)

                def project(t, pair, par):
                    pe.wait_ge(aggt_ready, t + 1)
                    if later(t):
                        pe.wait_ge(y_ready, t - 1)
                    for k in range(KT):
                        mm = nc.tensor.matmul(ps_y[par][:], aggt[par][:, k, :], w[:, k, :],
                                              start=(k == 0), stop=(k == KT - 1))
                    mm.then_inc(projected, 1)

                pe.wait_ge(w_loaded, 32)
                staged_tiles(pe, (0, lambda t, pair, par: prod.tensor(pe, t, par, range(0, T // 2))), (1, turn),
                             (0, lambda t, pair, par: prod.tensor(pe, t, par, range(T // 2, T))), (1, project))

            @block.scalar
            def _(act):
                def turned_out(t, pair, par):
                    act.wait_ge(turned, t + 1)
                    nc.scalar.copy(aggt[par][:], ps_t[par][:]).then_inc(aggt_ready, 1)

                def low(t, pair, par):
                    prod.scalar(act, t, par, col(stats["lo_has_neighbour"], t))

                staged_tiles(act, (1, turned_out), (0, low))

            @block.vector
            def _(dve):
                def join(t, pair, par):
                    if later(t):
                        dve.wait_ge(turned, t - 1)
                    prod.vector(dve, agg[par][:], t, par, col(stats["has_neighbour"], t))

                def out(t, pair, par):
                    dve.wait_ge(projected, t + 1)
                    if later(t, 0):
                        dve.wait_ge(x2_ready, t)
                    nc.vector.tensor_tensor(y[par][:], ps_y[par][:], bias[:], ALU.add).then_inc(y_ready, 1)
                    dve.wait_ge(y_ready, t + 1)
                    dve.wait_ge(x_loaded[par], 16 * (pair + 1))
                    if later(t):
                        dve.wait_ge(x2_stored[par], 16 * pair)
                    if later(t):
                        dve.wait_ge(ln.stats_done, t - 1)
                    nc.vector.scalar_tensor_tensor(out=x2[par][:], in0=y[par][:], scalar=0.0, in1=x[par][:],
                                                   op0=ALU.max, op1=ALU.add).then_inc(x2_ready, 1)

                def moments(t, pair, par):
                    dve.wait_ge(x2_ready, t + 1)
                    if later(t):
                        dve.wait_ge(ln.coefs_ready, t - 1)
                    ln.vector(dve, x2[par][:], t, par)

                def symmetric(t, pair, par):
                    nc.vector.tensor_tensor(sym[:, t, :], adj_t[:, t, :], lonely_wide[:],
                                            ALU.subtract).then_inc(true_columns, 1)
                    dve.wait_ge(true_columns, t + 1)
                    dve.wait_ge(adj_loaded, 16 * (t + 1))
                    nc.vector.scalar_tensor_tensor(out=sym[:, t, :], in0=adj_rows[:], scalar=1.0,
                                                   in1=sym[:, t, :], op0=ALU.mult, op1=ALU.add,
                                                   accum_out=col(stats["deg2"], t)).then_inc(sym_ready, 1)
                    dve.wait_ge(sym_ready, t + 1)
                    diag = sym[:, t, bass.ts(t, P)]
                    nc.vector.scalar_tensor_tensor(out=diag, in0=consts["ident"][:], scalar=2.0, in1=diag,
                                                   op0=ALU.mult, op1=ALU.add)

                def degree(t, pair, par):
                    nc.vector.tensor_scalar(col(stats["deg"], t), col(stats["deg2"], t), 0.5, 1.0, ALU.mult,
                                            ALU.add).then_inc(deg_ready, 1)

                dve.wait_ge(w_loaded, 32)
                staged_tiles(dve, (0, symmetric), (0, degree), (0, join), (1, out), (1, moments))
                dve.wait_ge(dinv_ready, T)
                nc.vector.tensor_scalar(stats["half_dinv"][:], stats["dinv"][:], 0.5, None, ALU.mult)
                nc.vector.tensor_scalar(stats["lo_half_dinv"][:], stats["dinv"][:], 0.5 / LO_SCALE, None, ALU.mult)


def build_scaled_rows(nc, consts, x_src, g_parts, stats):
    XB = 2
    with ExitStack() as stack:
        m = Mem(nc, stack, "scaled")
        x = m.sb("x", [P, T, D])
        h = [m.sb(f"h{p}", [P, D]) for p in range(2)]
        rest = [m.sb(f"rest{p}", [P, D]) for p in range(2)]
        x_loaded = [m.sem(f"x_loaded{b}") for b in range(T // XB)]
        h_ready = m.sem("h_ready")
        hi_done = [m.sem(f"hi_done{p}") for p in range(2)]
        rest_ready = [m.sem(f"rest_ready{p}") for p in range(2)]
        lo_done = m.sem("lo_done")
        with nc.Block() as block:

            def remainder(eng, vec, t):
                eng.wait_ge(hi_done[t % 2], t // 2 + 1)
                if t >= 2:
                    eng.wait_ge(lo_done, t - 1)
                vec.tensor_tensor(rest[t % 2][:], h[t % 2][:], g_parts[:, t, 0, :],
                                  ALU.subtract).then_inc(rest_ready[t % 2], 1)

            @block.sync
            def _(sp):
                for b in range(T // XB):
                    tiles = slice(b * XB, (b + 1) * XB)
                    sp.dma_start(x[:, tiles, :], rows(x_src)[tiles].rearrange("t p d -> p t d"))\
                        .then_inc(x_loaded[b], 16)

            @block.scalar
            def _(act):
                for t in range(T):
                    def normed(out):
                        return nc.scalar.activation(out, x[:, t, :], ACT.Relu, bias=stats["ln_shift"][:, t:t + 1],
                                                    scale=stats["ln_scale"][:, t:t + 1])

                    act.wait_ge(x_loaded[t // XB], 16)
                    if t >= 2:
                        act.wait_ge(rest_ready[t % 2], t // 2)
                    normed(h[t % 2][:]).then_inc(h_ready, 1)
                    if t % 2 == 0:
                        normed(g_parts[:, t, 0, :]).then_inc(hi_done[0], 1)

            @block.gpsimd
            def _(pool):
                for t in range(1, T, 2):
                    remainder(pool, nc.gpsimd, t)

            @block.vector
            def _(dve):
                def low(t):
                    dve.wait_ge(rest_ready[t % 2], t // 2 + 1)
                    nc.vector.tensor_scalar(g_parts[:, t, 1, :], rest[t % 2][:], LO_SCALE, None,
                                            ALU.mult).then_inc(lo_done, 1)

                for t in range(0, T, 2):
                    remainder(dve, nc.vector, t)
                    if t:
                        low(t - 1)
                    low(t)
                    dve.wait_ge(h_ready, t + 2)
                    nc.vector.tensor_copy(g_parts[:, t + 1, 0, :], h[1][:]).then_inc(hi_done[1], 1)
                low(T - 1)


def build_normalised_product(nc, consts, sym, g_parts, z_parts, stats):
    with ExitStack() as stack:
        m = Mem(nc, stack, "norm")
        z = m.sb("z", [P, D])
        prod = AdjacencyProduct(nc, m, sym, g_parts)
        split_rest = m.sb("rest", [P, D])
        hi_done = m.sem("hi_done")
        rest_ready = m.sem("rest_ready")
        lo_done = m.sem("lo_done")
        with nc.Block() as block:

            @block.tensor
            def _(pe):
                staged_tiles(pe, (0, lambda t, pair, par: prod.tensor(pe, t, par, range(T))))

            @block.scalar
            def _(act):
                def low(t, pair, par):
                    prod.scalar(act, t, par, col(stats["lo_half_dinv"], t))

                def lo_part(t, pair, par):
                    act.wait_ge(rest_ready, t + 1)
                    nc.scalar.mul(z_parts[:, t, 1, :], split_rest[:], LO_SCALE).then_inc(lo_done, 1)

                staged_tiles(act, (0, low), (0, lo_part))

            @block.vector
            def _(dve):
                def join(t, pair, par):
                    if later(t, 0):
                        dve.wait_ge(rest_ready, t)
                    prod.vector(dve, z[:], t, par, col(stats["half_dinv"], t))
                    dve.wait_ge(prod.joined, t + 1)
                    nc.vector.tensor_copy(z_parts[:, t, 0, :], z[:]).then_inc(hi_done, 1)
                    dve.wait_ge(hi_done, t + 1)
                    if later(t, 0):
                        dve.wait_ge(lo_done, t)
                    nc.vector.tensor_tensor(split_rest[:], z[:], z_parts[:, t, 0, :],
                                            ALU.subtract).then_inc(rest_ready, 1)

                staged_tiles(dve, (0, join))


def build_second_product(nc, x_src, x_dst, x3, adj_t, z_parts, spare, stats, weights, w_src, heads):
    w, a12, wa = weights
    with ExitStack() as stack:
        m = Mem(nc, stack, "second")
        x = [spare[:, p * D:(p + 1) * D] for p in range(2)]
        y = [m.sb("y", [P, D])] * 2
        wa_terms = spare[:, 2 * D:2 * D + KT * D].rearrange("p (k n) -> p k n", k=KT)
        w_loaded = m.sem("w_loaded")
        wa_step = m.sem("wa_step")
        wa_ready = m.sem("wa_ready")
        prod = AdjacencyProduct(nc, m, adj_t, z_parts)
        x_loaded = [m.sem(f"x_loaded{p}") for p in range(2)]
        x3_stored = [m.sem(f"x3_stored{p}") for p in range(2)]
        x3_ready = m.sem("x3_ready")
        with nc.Block() as block:

            @block.sync
            def _(sp):
                def store(t, pair, par):
                    sp.wait_ge(x3_ready, t + 1)
                    sp.dma_start(rows(x_dst)[t], x3[:, t, :]).then_inc(x3_stored[par], 16)

                load_tiles(sp, rows(x_src), x, x_loaded, x3_ready,
                           lambda: load_head_weights(sp, w, w_src[0], a12, w_src[1], w_loaded), store)
                for par in range(2):
                    sp.wait_ge(x3_stored[par], 16 * (T // 2))

            @block.tensor
            def _(pe):
                staged_tiles(pe, (0, lambda t, pair, par: prod.tensor(pe, t, par, range(T))))

            @block.scalar
            def _(act):
                staged_tiles(act, (0, lambda t, pair, par: prod.scalar(act, t, par, col(stats["lo_has_neighbour"], t))))

            @block.vector
            def _(dve):
                def residual(t, pair, par):
                    if later(t, 0):
                        dve.wait_ge(x3_ready, t)
                    prod.vector(dve, y[par][:], t, par, col(stats["has_neighbour"], t))
                    dve.wait_ge(prod.joined, t + 1)
                    dve.wait_ge(x_loaded[par], 16 * (pair + 1))
                    nc.vector.tensor_tensor(x3[:, t, :], y[par][:], x[par][:], ALU.add).then_inc(x3_ready, 1)

                dve.wait_ge(w_loaded, 32)
                head_weights(nc, dve, w, a12, wa, wa_terms, heads, wa_step, wa_ready)
                staged_tiles(dve, (0, residual))


def build_perceptron(nc, consts, x_src, out, hidden, value_sum, stats, layers):
    (w1_dram, b1_dram), (w2_dram, b2_dram), (w3_dram, b3_dram), (w4_dram, b4_dram) = layers
    with ExitStack() as stack:
        m = Mem(nc, stack, "mlp")
        M1, M2, M3 = (w1_dram.shape[1] // P, w2_dram.shape[1] // P, w3_dram.shape[1] // P)
        w1 = m.sb("w1", [P, KT, M1 * P])
        w2 = m.sb("w2", [P, M1, M2 * P])
        w3 = m.sb("w3", [P, M2, M3 * P])
        w4 = m.sb("w4", [P, M3, D])
        b1 = m.sb("b1", [P, M1])
        b2 = m.sb("b2", [P, M2])
        b3 = m.sb("b3", [P, M3])
        b4 = m.sb("b4", [P, D])
        x = [m.sb(f"x{p}", [P, D]) for p in range(2)]
        low = [m.sb(f"low{p}", [P, D]) for p in range(2)]
        high = [m.sb(f"high{p}", [P, D]) for p in range(2)]
        mean_rows = m.sb("mean_rows", [P, D])
        over_n = m.sb("over_n", [P, P])
        heads = value_sum.shape[1]
        dh = D // heads
        half = heads // 2
        over_n_set = m.sem("over_n_set")
        means_summed = m.sem("means_summed")
        means_ready = m.sem("means_ready")
        lonely_mean = m.sb("lonely_mean", [P, D])
        mixed = m.sb("mixed", [P, D])
        enc = [m.sb(f"enc{p}", [P, D]) for p in range(2)]
        enct = [m.sb(f"enct{p}", [P, KT, P]) for p in range(2)]
        o1 = [m.sb(f"o1{p}", [P, M1, P]) for p in range(2)]
        o2 = [m.sb(f"o2{p}", [P, M2, P]) for p in range(2)]
        o3 = [m.sb(f"o3{p}", [P, M3, P]) for p in range(2)]
        xb = [m.sb(f"xb{p}", [P, D]) for p in range(2)]
        y = [m.sb(f"y{p}", [P, D]) for p in range(2)]
        ps_t = [m.ps(f"ps_t{p}", [P, KT, P]) for p in range(2)]
        ps_1 = [m.ps(f"ps_1{p}", [P, 512]) for p in range(2)]
        ps_2 = m.ps("ps_2", [P, 512])
        ps_3 = m.ps("ps_3", [P, 512])
        ps_4 = [m.ps(f"ps_4{p}", [P, D]) for p in range(2)]
        w_loaded = m.sem("w_loaded")
        x_loaded = [m.sem(f"x_loaded{p}") for p in range(2)]
        stored = [m.sem(f"stored{p}") for p in range(2)]
        mean_picked = m.sem("mean_picked")
        mixed_ready = m.sem("mixed_ready")
        low_ready = m.sem("low_ready")
        high_ready = m.sem("high_ready")
        exp_ready = m.sem("exp_ready")
        enc_ready = m.sem("enc_ready")
        turned = m.sem("turned")
        enct_ready = m.sem("enct_ready")
        summed = [m.sem(f"summed{n}") for n in range(1, 5)]
        relu_ready = [m.sem(f"relu_ready{n}") for n in range(1, 4)]
        xb_ready = m.sem("xb_ready")
        y_ready = m.sem("y_ready")

        with nc.Block() as block:

            @block.sync
            def _(sp):
                for w, dram in ((w1, w1_dram), (w2, w2_dram), (w3, w3_dram), (w4, w4_dram)):
                    sp.dma_start(w[:], dram.rearrange("(k p) n -> p k n", p=P)).then_inc(w_loaded, 16)
                for b, dram in ((b1, b1_dram), (b2, b2_dram), (b3, b3_dram)):
                    sp.dma_start(b[:], dram).then_inc(w_loaded, 16)
                sp.dma_start(b4[:], b4_dram.unsqueeze(0).broadcast_to([P, D])).then_inc(w_loaded, 16)
                load_tiles(sp, rows(x_src), x, x_loaded, xb_ready)

            @block.gpsimd
            def _(pool):
                def biased(t, pair, par):
                    pool.wait_ge(x_loaded[par], 16 * (pair + 1))
                    if later(t):
                        pool.wait_ge(y_ready, t - 1)
                    nc.gpsimd.tensor_tensor(xb[par][:], x[par][:], b4[:], ALU.add).then_inc(xb_ready, 1)

                def store(t, pair, par):
                    pool.wait_ge(y_ready, t + 1)
                    pool.dma_start(rows(out)[t], y[par][:]).then_inc(stored[par], 16)

                pool.wait_ge(w_loaded, 16 * 8)
                staged_tiles(pool, (0, biased), (2, store))
                for par in range(2):
                    pool.wait_ge(stored[par], 16 * (T // 2))

            @block.tensor
            def _(pe):
                def turn(t, pair, par):
                    pe.wait_ge(enc_ready, t + 1)
                    for k in range(KT):
                        mm = nc.tensor.transpose(ps_t[par][:, k, :], enc[par][:, k * P:(k + 1) * P],
                                                 consts["ident"][:])
                    mm.then_inc(turned, 1)

                def layer(n, ps, w, src, src_ready, kts, mts, free, lag_free):
                    def emit(t, pair, par):
                        pe.wait_ge(src_ready, t + 1)
                        if later(t, lag_free - 1):
                            pe.wait_ge(free, t + 1 - lag_free)
                        o = ps[par] if isinstance(ps, list) else ps
                        for mt in range(mts):
                            for k in range(kts):
                                mm = nc.tensor.matmul(o[:, mt * P:(mt + 1) * P], w[:, k, mt * P:(mt + 1) * P],
                                                      src[par][:, k, :], start=(k == 0), stop=(k == kts - 1))
                        mm.then_inc(summed[n - 1], 1)
                    return emit

                def last(t, pair, par):
                    pe.wait_ge(relu_ready[2], t + 1)
                    if later(t):
                        pe.wait_ge(y_ready, t - 1)
                    for k in range(M3):
                        mm = nc.tensor.matmul(ps_4[par][:], o3[par][:, k, :], w4[:, k, :],
                                              start=(k == 0), stop=(k == M3 - 1))
                    mm.then_inc(summed[3], 1)

                pe.wait_ge(over_n_set, 1)
                for ps, s in ((ps_2, 0), (ps_3, half)):
                    nc.tensor.matmul(ps[:, 0:half * (dh + 1)], over_n[:],
                                     value_sum[:, s:s + half, :].rearrange("p h c -> p (h c)"),
                                     start=True, stop=True).then_inc(means_summed, 1)
                pe.wait_ge(w_loaded, 16 * 8)
                staged_tiles(pe, (0, turn), (4, last),
                             (3, layer(3, ps_3, w3, o2, relu_ready[1], M2, M3, relu_ready[2], 1)),
                             (2, layer(2, ps_2, w2, o1, relu_ready[0], M1, M2, relu_ready[1], 1)),
                             (1, layer(1, ps_1, w1, enct, enct_ready, KT, M1, relu_ready[0], 2)))

            @block.scalar
            def _(act):
                def exps(t, pair, par):
                    act.wait_ge(low_ready, t + 1)
                    nc.scalar.activation(low[par][:], low[par][:], ACT.Exp).then_inc(exp_ready, 1)

                def turned_out(t, pair, par):
                    act.wait_ge(turned, t + 1)
                    nc.scalar.copy(enct[par][:], ps_t[par][:]).then_inc(enct_ready, 1)

                def relu(n, ps, dst, b, mts):
                    def emit(t, pair, par):
                        act.wait_ge(summed[n - 1], t + 1)
                        o = ps[par] if isinstance(ps, list) else ps
                        for mt in range(mts):
                            op = nc.scalar.activation(dst[par][:, mt, :], o[:, mt * P:(mt + 1) * P], ACT.Relu,
                                                      bias=b[:, mt:mt + 1])
                        op.then_inc(relu_ready[n - 1], 1)
                    return emit

                act.wait_ge(w_loaded, 16 * 8)
                staged_tiles(act, (0, exps), (2, turned_out), (5, relu(3, ps_3, o3, b3, M3)),
                             (4, relu(2, ps_2, o2, b2, M2)), (3, relu(1, ps_1, o1, b1, M1)))

            @block.vector
            def _(dve):
                def parts_of(t, pair, par):
                    if later(t):
                        dve.wait_ge(enc_ready, t - 1)
                    if later(t, 0):
                        dve.wait_ge(low_ready, t)
                        dve.wait_ge(high_ready, t)
                    nc.vector.tensor_scalar(lonely_mean[:], mean_rows[:], col(stats["lonely"], t), None,
                                            ALU.mult).then_inc(mean_picked, 1)
                    dve.wait_ge(mean_picked, t + 1)
                    consts["settle"](dve)
                    nc.vector.scalar_tensor_tensor(out=mixed[:], in0=hidden[:, t, :],
                                                   scalar=col(stats["has_neighbour"], t), in1=lonely_mean[:],
                                                   op0=ALU.mult, op1=ALU.add).then_inc(mixed_ready, 1)
                    dve.wait_ge(mixed_ready, t + 1)
                    nc.vector.tensor_scalar(low[par][:], mixed[:], 0.0, None, ALU.min).then_inc(low_ready, 1)
                    nc.vector.tensor_scalar(high[par][:], mixed[:], 0.0, None, ALU.max).then_inc(high_ready, 1)

                def encode(t, pair, par):
                    dve.wait_ge(exp_ready, t + 1)
                    dve.wait_ge(high_ready, t + 1)
                    if later(t):
                        dve.wait_ge(turned, t - 1)
                    nc.vector.scalar_tensor_tensor(out=enc[par][:], in0=low[par][:], scalar=-1.0, in1=high[par][:],
                                                   op0=ALU.add, op1=ALU.add).then_inc(enc_ready, 1)

                def final(t, pair, par):
                    dve.wait_ge(summed[3], t + 1)
                    dve.wait_ge(xb_ready, t + 1)
                    if later(t):
                        dve.wait_ge(stored[par], 16 * pair)
                    nc.vector.tensor_tensor(y[par][:], ps_4[par][:], xb[par][:], ALU.add).then_inc(y_ready, 1)

                nc.vector.memset(over_n[:], 1.0 / N).then_inc(over_n_set, 1)
                dve.wait_ge(means_summed, 2)
                for ps, s in ((ps_2, 0), (ps_3, half)):
                    op = nc.vector.tensor_copy(
                        mean_rows[:].rearrange("p (h d) -> p h d", h=heads)[:, s:s + half, :],
                        ps[:, 0:half * (dh + 1)].rearrange("p (h c) -> p h c", h=half)[:, :, 0:dh])
                op.then_inc(means_ready, 1)
                dve.wait_ge(means_ready, 1)
                staged_tiles(dve, (0, parts_of), (1, encode), (6, final))


def build(nc, a, out):
    x1 = nc.dram_tensor("after_l0", (N, D), F32, kind="Internal").ap()
    x2 = nc.dram_tensor("after_l1", (N, D), F32, kind="Internal").ap()
    x3 = nc.dram_tensor("after_l2", (N, D), F32, kind="Internal").ap()

    def attention_memory(stack, prefix, heads):
        m = Mem(nc, stack, prefix)
        return {"values": m.sb("values", [P, T, heads, D // heads + 1]),
                "exp_s2": m.sb("exp_s2", [P, T, heads, 2]),
                "step_bias": m.sb("step_bias", [P, T, heads]),
                "row_exps": m.sb("row_exps", [P, T, 2, heads]),
                "far": m.sb("far", [1, 1], mybir.dt.int32),
                **({"neg_s2": m.sb("neg_s2", [P, T, heads])} if prefix == "keep0" else {})}

    def attention(name, heads, keep, s12, wide, terms, complements, direct):
        far = nc.values_load(keep["far"][:], min_val=0, max_val=1)
        with nc.If(far == 0):
            used = build_attention(nc, f"att{name}", consts["settle"], consts["neg_one"], heads, keep, adj_t, s12,
                                   ring, wide, hidden, terms, complements, direct)
        with nc.Else():
            used += build_dense_attention(nc, f"gen{name}", consts["settle"], consts["ident"], heads, keep,
                                          a["adj"], s12, spare, hidden, name == 0)
        return used

    with ExitStack() as stack:
        m = Mem(nc, stack, "all")
        consts = {"neg_half": m.sb("neg_half", [P, 1]), "neg_one": m.sb("neg_one", [P, 1]), "ident": m.sb("ident", [P, P]),
                  "ones_bf16": m.sb("ones_bf16", [P, P], BF16)}
        passed = m.sem("wait_passed")
        consts["settle"] = lambda eng: eng.sem_inc(passed, 1)
        stats = {n: m.sb(n, [P, T]) for n in ("deg2", "deg", "dinv", "half_dinv", "lo_half_dinv", "ln_scale",
                                              "ln_shift", "lonely", "has_neighbour", "lo_has_neighbour")}
        adj_t = m.sb("adj_t", [P, T, N], BF16)
        sym = m.sb("sym_or_hidden", [P, T, N], BF16)
        flat = sym[:].rearrange("p t n -> p (t n)")
        hidden = flat[:, 0:T * N // 2].bitcast(F32).rearrange("p (t d) -> p t d", t=T)
        ring = flat[:, T * N // 2:T * N]
        spare = ring.bitcast(F32)
        adj_loaded = m.sem("adj_t_loaded")

        def load_adj_t(pool):
            for b in range(NB):
                pool.dma_start(adj_t[:, b * JB:(b + 1) * JB, :],
                               a["adj_t"][b * JB * P:(b + 1) * JB * P, :].rearrange("(j p) n -> p j n", p=P))\
                    .then_inc(adj_loaded, 16)

        const_sems = build_constants(nc, consts)
        wide = m.sb("lonely_wide", [P, N], BF16)
        with ExitStack() as att:
            keep = attention_memory(att, "keep0", 16)
            s12 = nc.dram_tensor("s12_rows0", (32, N), F32, kind="Internal").ap()
            with ExitStack() as proj:
                p = Mem(nc, proj, "proj0w")
                weights = (p.sb("w", [P, KT, D])[:], p.sb("a12", [P, 2, D])[:], p.sb("wa", [P, KT, 32])[:])
                done_with = build_projection(nc, "proj0", consts, hidden, (a["x"], a["w0"], a["a0"]), weights, 16, 2,
                                             keep, s12, spare, load_adj_t)
            used = build_lonely_rows(nc, consts, adj_t, adj_loaded, wide, stats, const_sems + done_with)
            used += attention(0, 16, keep, s12, None, 2, [], [3, 7, 11, 15])
        weights3 = (spare[:, 4 * N - KT * D:].rearrange("p (k n) -> p k n", k=KT),
                    wide[:].bitcast(F32).rearrange("p (s n) -> p s n", s=2), m.sb("wa3", [P, KT, 16])[:])
        with ExitStack() as layers:
            h_parts = Mem(nc, layers, "gcn").sb("h_parts", [P, T, 2, D], F16)
            build_attention_out(nc, consts, a["x"], x1, hidden, spare, a["w0_out"], a["b0_out"], h_parts, used)
            build_linear_layer(nc, consts, x1, x2, a["w1_t"], a["b1"], a["adj"], adj_t, h_parts, sym, stats, wide)
            build_scaled_rows(nc, consts, x2, h_parts, stats)
            z_parts = Mem(nc, layers, "gcn2").sb("z_parts", [P, T, 2, D], F16)
            build_normalised_product(nc, consts, sym, h_parts, z_parts, stats)
            build_second_product(nc, x2, x3, hidden, adj_t, z_parts, spare, stats, weights3, (a["w3"], a["a3"]), 8)
        value_sum = m.sb("value_sum", [P, 8, D // 8 + 1])
        with ExitStack() as att:
            keep = attention_memory(att, "keep3", 8)
            s12 = nc.dram_tensor("s12_rows3", (16, N), F32, kind="Internal").ap()
            build_projection(nc, "proj3", consts, hidden, None, weights3, 8, 3, keep, s12, spare,
                             value_sum=value_sum)
            attention(3, 8, keep, s12, wide, 3, [0, 1, 2, 3], [])
        build_perceptron(nc, consts, x3, out, hidden, value_sum, stats,
                         [(a[f"mlp_w{n}_t"], a[f"mlp_b{n}"]) for n in range(1, 5)])


def kernel(**inputs):
    import numpy as np
    import concourse.bacc as bacc
    from concourse.bass_utils import run_bass_kernel_spmd

    i = {k: np.asarray(v) for k, v in inputs.items()}
    laid = {
        "x": i["x"], "adj": i["adj"], "adj_t": i["adj"].T,
        "w0": i["L0_gnn_W_seq"],
        "a0": np.stack([np.tile(i["L0_gnn_a1"], 16), np.tile(i["L0_gnn_a2"], 16)]),
        "w0_out": i["L0_gnn_W_out"], "b0_out": i["L0_gnn_b_out"],
        "w1_t": i["L1_gnn_W"].T, "b1": i["L1_gnn_b"],
        "w3": i["L3_gnn_W"].transpose(1, 0, 2).reshape(D, D),
        "a3": np.stack([i["L3_gnn_a1"].reshape(D), i["L3_gnn_a2"].reshape(D)]),
    }
    for n in range(1, 5):
        laid[f"mlp_w{n}_t"] = i[f"L3_gnn_W{n}"].T
        b = i[f"L3_gnn_b{n}"]
        laid[f"mlp_b{n}"] = b if n == 4 else b.reshape(-1, P).T
    nc = bacc.Bacc("TRN2", target_bir_lowering=False, num_devices=1)
    arrays = {f"in_{k}": np.ascontiguousarray(v) for k, v in laid.items()}
    aps = {k: nc.dram_tensor(f"in_{k}", arrays[f"in_{k}"].shape, F32, kind="ExternalInput").ap() for k in laid}
    out = nc.dram_tensor("out_0_dram", (N, D), F32, kind="ExternalOutput").ap()
    build(nc, aps, out)
    return run_bass_kernel_spmd(nc, [arrays], core_ids=[0]).results[0]["out_0_dram"]
```
